# Optimizing a Trainium2 kernel written in Bass

```python
import numpy as np
import jax
import jax.numpy as jnp

def _softmax(x, axis=-1):
    return jax.nn.softmax(x, axis=axis)

def _gelu(x):
    return jax.nn.gelu(x, approximate=True)

def _silu(x):
    return jax.nn.silu(x)

def _sigmoid(x):
    return jax.nn.sigmoid(x)

def _layernorm(x, axis=-1, eps=1e-05):
    m = jnp.mean(x, axis=axis, keepdims=True)
    v = jnp.var(x, axis=axis, keepdims=True)
    return (x - m) / jnp.sqrt(v + eps)

def _scatter_add(tgt, idx, src, axis=0):
    return tgt.at[idx].add(src)

def _segment_sum(src, seg, n):
    return jax.ops.segment_sum(src, seg, n)
kernel_name = 'mk_audio_tower_d1_tok_audfeat4096_r4_8d35d1'

def setup_inputs(seed: int=0):
    np.random.seed(seed)
    _w = jnp.asarray

    def _rec_inputs():
        import jax
        import jax.numpy as jnp
        _rk = jax.random.key(seed)
        x = 7.22013e-05 + 1.00017 * jax.random.normal(jax.random.fold_in(_rk, 1), (16, 64, 2048), jnp.float32)
        return x
    x = _rec_inputs()

    def _L0_tok_setup():
        import jax, jax.numpy as jnp
        import numpy as np
        EPS = 1e-05

        def conv1d(x, w, stride=1, pad=0, groups=1):
            return jax.lax.conv_general_dilated(x, w, window_strides=(stride,), padding=[(pad, pad)], dimension_numbers=('NCH', 'OIH', 'NCH'), feature_group_count=groups)

        def groupnorm1(x, gamma, beta):
            m = jnp.mean(x, axis=(1, 2), keepdims=True)
            v = jnp.mean((x - m) ** 2, axis=(1, 2), keepdims=True)
            xn = (x - m) * jax.lax.rsqrt(v + EPS)
            return xn * gamma[None, :, None] + beta[None, :, None]
        key = jax.random.key(seed)
        ks = jax.random.split(key, 8)
        B, C_IN, T, H = (16, 64, 2048, 128)
        x = jax.random.normal(ks[0], (B, C_IN, T), dtype=jnp.float32)
        conv_in_w = jax.random.normal(ks[1], (H, C_IN, 7), dtype=jnp.float32) * 0.05
        dw_w = jax.random.normal(ks[2], (H, 1, 5), dtype=jnp.float32) * 0.1
        dw_b = jax.random.normal(ks[3], (H,), dtype=jnp.float32) * 0.01
        pw_w = jax.random.normal(ks[4], (H, H, 1), dtype=jnp.float32) * 0.04
        gn1_w = jnp.ones((H,), jnp.float32)
        gn1_b = jnp.zeros((H,), jnp.float32)
        gn2_w = jnp.ones((H,), jnp.float32)
        gn2_b = jnp.zeros((H,), jnp.float32)
        return {'x': x, 'conv_in_w': conv_in_w, 'dw_w': dw_w, 'dw_b': dw_b, 'pw_w': pw_w, 'gn1_w': gn1_w, 'gn1_b': gn1_b, 'gn2_w': gn2_w, 'gn2_b': gn2_b}
    _L0_tok_all = _L0_tok_setup()
    _L0_tok_in = {k: v for k, v in _L0_tok_all.items() if k in ('conv_in_w', 'dw_w', 'dw_b', 'pw_w', 'gn1_w', 'gn1_b', 'gn2_w', 'gn2_b')}
    del _L0_tok_all

    def _L0_attn_setup():
        import jax, jax.numpy as jnp
        import numpy as np
        EMBED = 1024
        HEADS = 16
        HEAD_DIM = EMBED // HEADS
        ROT = 64
        B, S = (1, 512)
        MASK_VAL = -1000000000.0

        def _rotate_every_two(x):
            r = jnp.stack((x[..., 1::2], x[..., ::2]), axis=-1)
            return r.reshape(x.shape)

        def _fixed_pos_embedding(seq_len, rot_dim):
            inv_freq = 1.0 / 10000.0 ** (jnp.arange(0, rot_dim, 2, dtype=jnp.float32) / rot_dim)
            t = jnp.arange(seq_len, dtype=jnp.float32)
            sinusoid = jnp.einsum('i,j->ij', t, inv_freq)
            return (jnp.sin(sinusoid), jnp.cos(sinusoid))

        def _apply_rotary(x, sin, cos):
            sin = jnp.repeat(sin[None, :, None, :], 2, axis=3)
            cos = jnp.repeat(cos[None, :, None, :], 2, axis=3)
            return x * cos + _rotate_every_two(x) * sin
        key = jax.random.key(seed)
        ks = jax.random.split(key, 5)
        sc = 0.02
        return {'hidden_states': jax.random.normal(ks[0], (B, S, EMBED), jnp.float32), 'Wq': jax.random.normal(ks[1], (EMBED, EMBED), jnp.float32) * sc, 'Wk': jax.random.normal(ks[2], (EMBED, EMBED), jnp.float32) * sc, 'Wv': jax.random.normal(ks[3], (EMBED, EMBED), jnp.float32) * sc, 'Wo': jax.random.normal(ks[4], (EMBED, EMBED), jnp.float32) * sc}
    _L0_attn_all = _L0_attn_setup()
    _L0_attn_in = {k: v for k, v in _L0_attn_all.items() if k in ('Wq', 'Wk', 'Wv', 'Wo')}
    del _L0_attn_all

    def _L0_ffn_setup():
        import jax, jax.numpy as jnp
        import numpy as np
        IN_F = 1024
        OUT_F = 1024
        RANK = 8
        NUM_EXPERTS = 64
        TOP_K = 16
        ROUTER_DIM = 16
        ALPHA = 32
        SCALING = ALPHA / TOP_K
        BOTTLENECK = NUM_EXPERTS * RANK
        key = jax.random.key(seed)
        ks = jax.random.split(key, 5)
        x = jax.random.normal(ks[0], (4, 1024, IN_F), dtype=jnp.float32)
        bound_a = float(np.sqrt(6.0 / IN_F))
        A_w = jax.random.uniform(ks[1], (BOTTLENECK, IN_F), jnp.float32, -bound_a, bound_a)
        B_w = jax.random.normal(ks[2], (OUT_F, BOTTLENECK), dtype=jnp.float32) * 0.02
        Wq_w = jax.random.normal(ks[3], (ROUTER_DIM, IN_F), dtype=jnp.float32) * 0.02
        keys = jax.random.normal(ks[4], (NUM_EXPERTS, ROUTER_DIM), dtype=jnp.float32) * 0.01
        return {'x': x, 'A_w': A_w, 'B_w': B_w, 'Wq_w': Wq_w, 'keys': keys}
    _L0_ffn_all = _L0_ffn_setup()
    _L0_ffn_in = {k: v for k, v in _L0_ffn_all.items() if k in ('A_w', 'B_w', 'Wq_w', 'keys')}
    del _L0_ffn_all
    return {'x': x, 'L0_tok_conv_in_w': _L0_tok_in['conv_in_w'], 'L0_tok_dw_w': _L0_tok_in['dw_w'], 'L0_tok_dw_b': _L0_tok_in['dw_b'], 'L0_tok_pw_w': _L0_tok_in['pw_w'], 'L0_tok_gn1_w': _L0_tok_in['gn1_w'], 'L0_tok_gn1_b': _L0_tok_in['gn1_b'], 'L0_tok_gn2_w': _L0_tok_in['gn2_w'], 'L0_tok_gn2_b': _L0_tok_in['gn2_b'], 'L0_attn_Wq': _L0_attn_in['Wq'], 'L0_attn_Wk': _L0_attn_in['Wk'], 'L0_attn_Wv': _L0_attn_in['Wv'], 'L0_attn_Wo': _L0_attn_in['Wo'], 'L0_ffn_A_w': _L0_ffn_in['A_w'], 'L0_ffn_B_w': _L0_ffn_in['B_w'], 'L0_ffn_Wq_w': _L0_ffn_in['Wq_w'], 'L0_ffn_keys': _L0_ffn_in['keys']}

def reference(x, L0_tok_conv_in_w, L0_tok_dw_w, L0_tok_dw_b, L0_tok_pw_w, L0_tok_gn1_w, L0_tok_gn1_b, L0_tok_gn2_w, L0_tok_gn2_b, L0_attn_Wq, L0_attn_Wk, L0_attn_Wv, L0_attn_Wo, L0_ffn_A_w, L0_ffn_B_w, L0_ffn_Wq_w, L0_ffn_keys):
    import jax
    import jax.numpy as jnp

    def _L0_tok_ref(x, conv_in_w, dw_w, dw_b, pw_w, gn1_w, gn1_b, gn2_w, gn2_b):
        import jax, jax.numpy as jnp
        import numpy as np
        EPS = 1e-05

        def conv1d(x, w, stride=1, pad=0, groups=1):
            return jax.lax.conv_general_dilated(x, w, window_strides=(stride,), padding=[(pad, pad)], dimension_numbers=('NCH', 'OIH', 'NCH'), feature_group_count=groups)

        def groupnorm1(x, gamma, beta):
            m = jnp.mean(x, axis=(1, 2), keepdims=True)
            v = jnp.mean((x - m) ** 2, axis=(1, 2), keepdims=True)
            xn = (x - m) * jax.lax.rsqrt(v + EPS)
            return xn * gamma[None, :, None] + beta[None, :, None]
        H = conv_in_w.shape[0]
        h = conv1d(x, conv_in_w, stride=1, pad=3)
        h = jax.nn.gelu(groupnorm1(h, gn1_w, gn1_b), approximate=False)
        h = conv1d(h, dw_w, stride=2, pad=2, groups=H) + dw_b[None, :, None]
        h = conv1d(h, pw_w)
        h = jax.nn.gelu(groupnorm1(h, gn2_w, gn2_b), approximate=False)
        return h

    def _L0_attn_ref(hidden_states, Wq, Wk, Wv, Wo):
        import jax, jax.numpy as jnp
        import numpy as np
        EMBED = 1024
        HEADS = 16
        HEAD_DIM = EMBED // HEADS
        ROT = 64
        B, S = (1, 512)
        MASK_VAL = -1000000000.0

        def _rotate_every_two(x):
            r = jnp.stack((x[..., 1::2], x[..., ::2]), axis=-1)
            return r.reshape(x.shape)

        def _fixed_pos_embedding(seq_len, rot_dim):
            inv_freq = 1.0 / 10000.0 ** (jnp.arange(0, rot_dim, 2, dtype=jnp.float32) / rot_dim)
            t = jnp.arange(seq_len, dtype=jnp.float32)
            sinusoid = jnp.einsum('i,j->ij', t, inv_freq)
            return (jnp.sin(sinusoid), jnp.cos(sinusoid))

        def _apply_rotary(x, sin, cos):
            sin = jnp.repeat(sin[None, :, None, :], 2, axis=3)
            cos = jnp.repeat(cos[None, :, None, :], 2, axis=3)
            return x * cos + _rotate_every_two(x) * sin
        b, s, e = hidden_states.shape
        q = (hidden_states @ Wq).reshape(b, s, HEADS, HEAD_DIM)
        k = (hidden_states @ Wk).reshape(b, s, HEADS, HEAD_DIM)
        v = (hidden_states @ Wv).reshape(b, s, HEADS, HEAD_DIM)
        sin, cos = _fixed_pos_embedding(s, ROT)
        q = jnp.concatenate([_apply_rotary(q[..., :ROT], sin, cos), q[..., ROT:]], axis=-1)
        k = jnp.concatenate([_apply_rotary(k[..., :ROT], sin, cos), k[..., ROT:]], axis=-1)
        q = q.transpose(0, 2, 1, 3)
        k = k.transpose(0, 2, 1, 3)
        v = v.transpose(0, 2, 1, 3)
        logits = jnp.einsum('bhqd,bhkd->bhqk', q, k)
        causal = jnp.tril(jnp.ones((s, s), dtype=bool))[None, None]
        logits = jnp.where(causal, logits, MASK_VAL)
        logits = logits / jnp.sqrt(jnp.float32(HEAD_DIM))
        attn = jax.nn.softmax(logits, axis=-1)
        out = jnp.einsum('bhqk,bhkd->bhqd', attn, v)
        out = out.transpose(0, 2, 1, 3).reshape(b, s, e)
        return out @ Wo

    def _L0_ffn_ref(x, A_w, B_w, Wq_w, keys):
        import jax, jax.numpy as jnp
        import numpy as np
        IN_F = 1024
        OUT_F = 1024
        RANK = 8
        NUM_EXPERTS = 64
        TOP_K = 16
        ROUTER_DIM = 16
        ALPHA = 32
        SCALING = ALPHA / TOP_K
        BOTTLENECK = NUM_EXPERTS * RANK
        q = jnp.einsum('bsd,rd->bsr', x, Wq_w)
        scores = jnp.einsum('bsr,er->bse', q, keys)
        top_vals, top_idx = jax.lax.top_k(scores, TOP_K)
        top_w = jax.nn.softmax(top_vals, axis=-1)
        gate = jnp.sum(jax.nn.one_hot(top_idx, NUM_EXPERTS, dtype=top_w.dtype) * top_w[..., None], axis=-2)
        z = jnp.einsum('bsd,nd->bsn', x, A_w)
        z = z.reshape(*z.shape[:-1], NUM_EXPERTS, RANK)
        z_gated = (z * gate[..., None]).reshape(*z.shape[:-2], BOTTLENECK)
        out = jnp.einsum('bsn,on->bso', z_gated, B_w) * SCALING
        return out
    h = _L0_tok_ref(x, L0_tok_conv_in_w, L0_tok_dw_w, L0_tok_dw_b, L0_tok_pw_w, L0_tok_gn1_w, L0_tok_gn1_b, L0_tok_gn2_w, L0_tok_gn2_b)
    h = h + _L0_attn_ref(_layernorm(h, axis=-1), L0_attn_Wq, L0_attn_Wk, L0_attn_Wv, L0_attn_Wo)
    h = h + _L0_ffn_ref(_layernorm(h, axis=-1), L0_ffn_A_w, L0_ffn_B_w, L0_ffn_Wq_w, L0_ffn_keys)
    return h

_drawn_inputs = setup_inputs


def setup_inputs(seed=0):
    import zlib

    import numpy as np

    out = dict(_drawn_inputs(seed))
    spreads = {'L0_tok_gn1_w': (1.0, 0.2),
     'L0_tok_gn1_b': (0.0, 0.1),
     'L0_tok_gn2_w': (1.0, 0.2),
     'L0_tok_gn2_b': (0.0, 0.1)}
    factors = {}
    for name, (base, spread) in spreads.items():
        noise = np.random.default_rng([zlib.crc32(name.encode()), seed]).standard_normal(out[name].shape)
        drawn = base * np.exp(spread * noise) if base else spread * noise
        out[name] = jnp.asarray(drawn.astype(out[name].dtype))
    for name, factor in factors.items():
        out[name] = (out[name] * factor).astype(out[name].dtype)
    return out
```

```python
from contextlib import ExitStack

import concourse.bass as bass
from concourse import mybir

F32 = mybir.dt.float32
F32R = mybir.dt.float32r
F16 = mybir.dt.float16
BF16 = mybir.dt.bfloat16
I32 = mybir.dt.int32
ALU = mybir.AluOpType
ACT = mybir.ActivationFunctionType
AX_X = mybir.AxisListType.X

P = 128
B, CIN, T = 16, 64, 2048
H, TO = 128, 1024
TAPS, DW = 7, 5
PAD = 3
XW = T + 2 * PAD + 2
GW = T + 4
BLK = 512
NBLK = T // BLK
EPS = 1e-5
E = TO
KC = E // P
HEADS, HD = 16, 64
PAIRS = HEADS // 2
BOT = 512
NE, RANK, RD, TOPK = 64, 8, 16, 16
SCALING = 2.0
PIECE = 2048
NPIECE = 20
TENSOR_OF = [(0, 4), (4, 4), (8, 4), (12, 4), (16, 2), (18, 2)]
Q_, K_, V_, O_, A_, B_ = range(6)
MASKED = -3e38
GB = 2
GT = GB * P
NG = B // GB


def after(eng, sem, n):
    if not isinstance(n, int) or n > 0:
        eng.wait_ge(sem, n)


class Chain:

    def __init__(self, eng, sem):
        self.eng, self.sem, self.n = eng, sem, 0

    def begin(self):
        self.eng.sem_clear(self.sem)
        self.n = 0

    def link(self, ins):
        self.n += 1
        ins.then_inc(self.sem, 1)
        self.eng.wait_ge(self.sem, self.n)


class Step:

    def __init__(self, b, parity, i=0, per=0, items=()):
        self.b, self.parity, self.i, self.per, self.items = b, parity, i, per, items
        self.next_x = b + 2

    def has(self, lag):
        return not isinstance(self.b, int) or 0 <= self.b - lag < B

    def round(self, n):
        return n // 2 + self.i * (self.per // 2)


NORM, PAIRED, PLAIN, KEPT = "norm", "paired", "plain", "kept"


def steps_of_phase_a(eng):
    for b in range(3):
        yield Step(b, b % 2, items=[(NORM, 4 * b + m, 4 * b + m, None) for m in range(4)])
    with eng.Fori(0, 2) as i:
        for p in range(2):
            n = 12 + 2 * p
            yield Step(i * 2 + (3 + p), 1 - p, i, 4, [(NORM, n + m, i * 4 + (n + m), None) for m in range(2)])
    yield None
    with eng.Fori(0, 2) as i:
        for p in range(2):
            n = NPIECE + 2 * p
            yield Step(i * 2 + (7 + p), 1 - p, i, 4, [(PAIRED, n + m, i * 4 + (2 * p + m), i) for m in range(2)])
    with eng.Fori(0, 2) as i:
        for p in range(2):
            n = NPIECE + 8 + 3 * p
            s = Step(i * 2 + (11 + p), 1 - p, i, 6, [
                (PLAIN, n, i * 2 + (8 + p), V_),
                (KEPT, n + 1, i * 4 + (12 + 2 * p), i * (1 + p) + O_),
                (KEPT, n + 2, i * 4 + (13 + 2 * p), i * (1 + p) + O_)])
            if p == 1:
                s.next_x = i + (B - 2)
            yield s
    for b in range(15, 19):
        yield Step(b, b % 2)


def phase_a(nc, st, sb, x, conv_w, par, pw_w, w_all, wr, keys_t, const, h0, split_dram,
            wqk_hi, wqk_lo, wv_hi, wv_lo, cst, ident, ones, mask32, mask_bf, ident_bf,
            scl, inv, unscale, half_neg, g_hi, g_lo):
    def buf(name, shape, dt):
        return sb(name, shape, dt, st)

    def psum(name, shape):
        return st.enter_context(nc.psum_tensor(name, shape, F32))

    def sem(name):
        return st.enter_context(nc.semaphore(name))

    xs = buf("xs", [P, XW], F32)
    pair = [buf(f"pair{i}", [P, XW], F32R) for i in range(2)]
    split = [buf(f"split{i}", [P, XW], F32R) for i in range(2)]
    raw = buf("raw", [P, T], F32)
    act1 = buf("act1", [P, GW], F32)
    dwo = buf("dwo", [P, TO], F32)
    dw_hi = buf("dw_hi", [P, TO], F32R)
    dw_lo = buf("dw_lo", [P, TO], F32R)
    tok = buf("tok", [P, TO], F32)
    stage = [buf(f"stage{i}", [P, PIECE], F32) for i in range(2)]
    plus_minus = buf("plus_minus", [P, PIECE], F32)
    squares = plus_minus[:, :]
    out_hi = plus_minus[:, 0:PIECE // 2].bitcast(F16)
    out_lo = plus_minus[:, PIECE // 2:PIECE].bitcast(F16)
    cw_dup = raw[:, 0:TAPS * H]
    cw_pair = raw[:, TAPS * H:(TAPS + 4) * H]
    pw32 = raw[:, (TAPS + 4) * H:(TAPS + 5) * H]
    wr_sb = act1[0:RD, 0:E]
    keys_sb = act1[0:RD, E:E + NE]
    cwh_dup = buf("cwh_dup", [P, TAPS * H], F32R)
    cwl_pair = buf("cwl_pair", [P, 4 * H], F32R)
    pw_hi = buf("pw_hi", [P, H], F32R)
    pw_lo = buf("pw_lo", [P, H], F32R)
    prm = buf("prm", [P, DW + 5], F32)
    tap = [prm[:, k:k + 1] for k in range(DW)]
    dw_bias, gn_w, gn_b = prm[:, DW:DW + 1], (prm[:, 6:7], prm[:, 8:9]), (prm[:, 7:8], prm[:, 9:10])
    sq = buf("sq", [P, NPIECE], F32)
    sqt = buf("sqt", [P, 8], F32)
    tmp_i = buf("tmp_i", [P, 8], I32)
    exp_i = buf("exp_i", [P, 8], I32)
    bn1 = buf("bn1", [P, NBLK, 6], F32)
    bn2 = buf("bn2", [P, 2, 6], F32)
    mv = [buf(f"mv{i}", [P, 2], F32) for i in range(2)]
    moments = [buf(f"moments{i}", [P, 2], F32) for i in range(2)]
    neg_mean = [buf(f"neg_mean{i}", [P, 1], F32) for i in range(2)]
    var = [buf(f"var{i}", [P, 1], F32) for i in range(2)]
    rstd = [buf(f"rstd{i}", [P, 1], F32) for i in range(2)]
    gscale = [buf(f"gscale{i}", [P, 1], F32) for i in range(2)]
    gbias = [buf(f"gbias{i}", [P, 1], F32) for i in range(2)]
    g32 = buf("g32", [P, KC * NE], F32)

    conv_ps = [psum(f"conv_ps{i}", [P, BLK]) for i in range(NBLK)]
    pw_ps = psum("pw_ps", [P, TO])
    stat_ps = psum("stat_ps", [P, 16])
    g_ps = psum("g_ps", [P, KC * NE])

    consts_in = sem("a_consts_in")
    pads_made = sem("a_pads_made")
    pool_done = sem("a_pool_done")
    ready = sem("a_ready")
    g_made = sem("a_g_made")
    g_copied = sem("a_g_copied")
    x_in = sem("a_x_in")
    pair_made = sem("a_pair_made")
    high_made = sem("a_high_made")
    low_made = sem("a_low_made")
    conv_done = sem("a_conv_done")
    evacuated = sem("a_evacuated")
    stat1 = sem("a_stat1")
    stat1_ps = sem("a_stat1_ps")
    var1 = sem("a_var1")
    rstd1 = sem("a_rstd1")
    affine1 = sem("a_affine1")
    gelu1 = sem("a_gelu1")
    tap0_made = sem("a_tap0_made")
    dw_split = sem("a_dw_split")
    pw_done = sem("a_pw_done")
    stat2 = sem("a_stat2")
    stat2_ps = sem("a_stat2_ps")
    var2 = sem("a_var2")
    rstd2 = sem("a_rstd2")
    affine2 = sem("a_affine2")
    gelu2 = sem("a_gelu2")
    stored = sem("a_stored")
    w_in = [sem(f"a_w_in{i}") for i in range(2)]
    w_used = [sem(f"a_w_used{i}") for i in range(2)]
    sums_made = sem("a_sums_made")
    hi_made = sem("a_hi_made")
    lo_made = sem("a_lo_made")
    kept = sem("a_kept")
    out_free = sem("a_out_free")
    squared = sem("a_squared")
    sums_split = sem("a_sums_split")
    sums_total = sem("a_sums_total")
    scaled = sem("a_scaled")
    chain_v = sem("a_chain_v")
    passed = sem("a_passed")

    N_CONSTS = 7 + TAPS

    def split_count(s, n):
        return (n - NPIECE) + s.i * s.per

    def kept_count(s, n):
        m = n - NPIECE - 8
        return (m // 3) * 2 + m % 3 - 1 + s.i * 4

    with nc.Block("phase_a") as block:

        @block.sync
        def _(sp):
            sp.dma_start(cst[:, :], const).then_inc(consts_in, 16)
            sp.dma_start(prm[:, :], par).then_inc(consts_in, 16)
            sp.dma_start(pw32, pw_w).then_inc(consts_in, 16)
            for half in range(2):
                sp.dma_start(cw_dup[half * CIN:(half + 1) * CIN, :], conv_w).then_inc(consts_in, 16)
            for k in range(TAPS):
                half, m = k % 2, k // 2
                sp.dma_start(cw_pair[half * CIN:(half + 1) * CIN, m * H:(m + 1) * H],
                             conv_w[:, k * H:(k + 1) * H]).then_inc(consts_in, 16)
            sp.dma_start(wr_sb, wr).then_inc(consts_in, 16)
            sp.dma_start(keys_sb, keys_t).then_inc(consts_in, 16)

            def load_x(b):
                sp.dma_start(xs[0:CIN, PAD:PAD + T], x[b]).then_inc(x_in, 16)
                sp.dma_start(xs[CIN:P, PAD - 1:PAD - 1 + T], x[b]).then_inc(x_in, 16)

            def copy_high(b, parity):
                sp.wait_ge(pair_made, b + 1)
                sp.dma_start(split[parity][0:CIN, :].bitcast(F32),
                             pair[parity][0:CIN, :].bitcast(F32)).then_inc(high_made, 16)

            sp.wait_ge(pads_made, 1)
            load_x(0)
            copy_high(0, 0)
            sp.wait_ge(low_made, 1)
            load_x(1)
            for s in steps_of_phase_a(sp):
                if s is None:
                    continue
                b = s.b
                if s.has(-1):
                    copy_high(b + 1, 1 - s.parity)
                for kind, n, piece, tensor in s.items:
                    after(sp, w_used[n % 2], s.round(n))
                    sp.dma_start(stage[n % 2][:, :], w_all[piece]).then_inc(w_in[n % 2], 16)
                if s.has(-2):
                    sp.wait_ge(low_made, b + 2)
                    load_x(s.next_x)
                if s.has(3):
                    sp.wait_ge(gelu2, b - 2)
                    sp.dma_start(h0[b - 3], tok[:, :]).then_inc(stored, 16)
            sp.wait_ge(x_in, 32 * (B + 1))
            sp.wait_ge(stored, 16 * B)

        @block.gpsimd
        def _(pool):
            pool.memset(half_neg[:, :], -0.5).then_inc(pool_done, 1)
            pool.wait_ge(pool_done, 1)
            for i in range(2):
                pool.memset(split[i][CIN:P, 0:1].bitcast(F32), 0.0).then_inc(pool_done, 1)
                pool.wait_ge(pool_done, 2 + i)
            pool.memset(xs[:, :], 0.0).then_inc(pads_made, 1)
            pool.wait_ge(pads_made, 1)

            def low(b, parity):
                pool.wait_ge(pair_made, b + 1)
                pool.tensor_tensor(out=split[parity][CIN:P, 1:XW], in0=xs[CIN:P, 0:XW - 1],
                                   in1=pair[parity][CIN:P, 0:XW - 1].bitcast(F32),
                                   op=ALU.subtract).then_inc(low_made, 1)
                pool.wait_ge(low_made, b + 1)

            low(0, 0)
            for s in steps_of_phase_a(pool):
                if s is None:
                    pool.wait_ge(scaled, 1)
                    pool.sem_inc(out_free, 1)
                    continue
                b = s.b
                if s.has(1):
                    pool.wait_ge(var1, b)
                    pool.tensor_tensor(out=rstd[0][:, :], in0=var[0][:, :], in1=half_neg[:, 0:1],
                                       op=ALU.pow).then_inc(rstd1, 1)
                    pool.wait_ge(rstd1, b)
                if s.has(-1):
                    low(b + 1, 1 - s.parity)
                for kind, n, piece, tensor in s.items:
                    if kind == PAIRED:
                        src = stage[n % 2][:, :].rearrange("p (a h c two) -> p a h c two", a=2, h=HEADS, two=2)
                        dst = plus_minus[:, :].rearrange("p (a h s c) -> p a h s c", a=2, h=HEADS, s=2)
                        pool.wait_ge(w_in[n % 2], (s.round(n) + 1) * 16)
                        pool.wait_ge(lo_made, split_count(s, n) + 1)
                        for half, op in enumerate((ALU.add, ALU.subtract)):
                            for a in range(2):
                                last = pool.tensor_tensor(out=dst[:, a, :, half, :], in0=src[:, a, :, :, 0],
                                                          in1=src[:, a, :, :, 1], op=op)
                                if half == 1 and a == 1:
                                    last.then_inc(sums_made, 1)
                        pool.wait_ge(sums_made, split_count(s, n) + 1)
                        pool.sem_inc(w_used[n % 2], 1)
                    if kind == KEPT:
                        row = piece - 12
                        pool.wait_ge(lo_made, split_count(s, n) + 2)
                        pool.dma_start(split_dram[row, 0], out_hi).then_inc(kept, 16)
                        pool.dma_start(split_dram[row, 1], out_lo).then_inc(kept, 16)
                        pool.wait_ge(kept, kept_count(s, n) * 32 + 32)
                        pool.sem_inc(out_free, 1)
                if s.has(2):
                    pool.wait_ge(var2, b - 1)
                    pool.tensor_tensor(out=rstd[1][:, :], in0=var[1][:, :], in1=half_neg[:, 0:1],
                                       op=ALU.pow).then_inc(rstd2, 1)
                    pool.wait_ge(rstd2, b - 1)

        @block.scalar
        def _(act):
            def make_pair(b, parity):
                act.wait_ge(x_in, (b + 1) * 32)
                after(act, conv_done, (b - 1) * NBLK)
                act.activation(pair[parity][:, :], xs[:, :], ACT.Copy).then_inc(pair_made, 1)

            act.wait_ge(g_copied, 1)
            act.activation(squares[:, 0:KC * NE], g32[:, :], ACT.Square,
                           accum_out=sqt[:, 6:7]).then_inc(squared, 1)
            make_pair(0, 0)
            for s in steps_of_phase_a(act):
                if s is None:
                    act.wait_ge(scaled, 1)
                    continue
                b = s.b
                if s.has(-1):
                    make_pair(b + 1, 1 - s.parity)
                if s.has(3):
                    act.wait_ge(affine2, b - 2)
                    after(act, stored, (b - 3) * 16)
                    act.activation(tok[:, :], pw_ps[:, :], ACT.Gelu, bias=gbias[1][:, :],
                                   scale=gscale[1][:, :]).then_inc(gelu2, 1)
                if s.has(1):
                    act.wait_ge(affine1, b)
                    after(act, dw_split, b - 1)
                    act.activation(act1[:, 2:2 + T], raw[:, :], ACT.Gelu, bias=gbias[0][:, :],
                                   scale=gscale[0][:, :]).then_inc(gelu1, 1)
                    act.wait_ge(gelu1, b)
                    act.activation(dwo[:, :], act1[:, 0:2 * TO:2], ACT.Identity, bias=dw_bias,
                                   scale=tap[0]).then_inc(tap0_made, 1)
                if s.has(0):
                    for blk in range(NBLK):
                        act.wait_ge(conv_done, b * NBLK + (blk + 1))
                        act.activation(raw[:, blk * BLK:(blk + 1) * BLK], conv_ps[blk][:, :],
                                       ACT.Copy).then_inc(evacuated, 1)
                for kind, n, piece, tensor in s.items:
                    w = stage[n % 2][:, :]
                    done = split_count(s, n)
                    if kind == NORM:
                        act.wait_ge(w_in[n % 2], (s.round(n) + 1) * 16)
                        if n == 0:
                            act.wait_ge(squared, 1)
                        else:
                            act.wait_ge(w_used[(n - 1) % 2], s.round(n - 1) + 1)
                            act.sem_inc(passed, 1)
                        act.activation(squares, w, ACT.Square,
                                       accum_out=sq[:, bass.ds(piece, 1)]).then_inc(w_used[n % 2], 1)
                        continue
                    scale = scl[:, bass.ds(tensor, 1)]
                    if kind == PAIRED:
                        act.wait_ge(sums_made, done + 1)
                        act.sem_inc(passed, 1)
                        act.activation(wqk_hi[:, bass.ds(piece * PIECE, PIECE)], plus_minus[:, :],
                                       ACT.Copy, scale=scale).then_inc(hi_made, 1)
                    if kind == PLAIN:
                        act.wait_ge(w_in[n % 2], (s.round(n) + 1) * 16)
                        act.sem_inc(passed, 1)
                        act.activation(wv_hi[:, bass.ds((piece - 8) * PIECE, PIECE)], w,
                                       ACT.Copy, scale=scale).then_inc(hi_made, 1)
                    if kind == KEPT:
                        act.wait_ge(w_in[n % 2], (s.round(n) + 1) * 16)
                        act.wait_ge(lo_made, done + 1)
                        act.wait_ge(out_free, kept_count(s, n) + 1)
                        act.sem_inc(passed, 1)
                        act.activation(out_hi, w, ACT.Copy, scale=scale).then_inc(hi_made, 1)

        @block.tensor
        def _(pe):
            pe.wait_ge(consts_in, 16 * N_CONSTS)
            for k in range(KC):
                last = pe.matmul(g_ps[:, k * NE:(k + 1) * NE], wr_sb[:, k * P:(k + 1) * P], keys_sb,
                                 start=True, stop=True)
            last.then_inc(g_made, 1)
            pe.wait_ge(ready, 1)
            for s in steps_of_phase_a(pe):
                if s is None:
                    pe.wait_ge(sums_split, 1)
                    pe.matmul(g_ps[:, 0:7], ones, sqt[:, 0:7], start=True, stop=True).then_inc(sums_total, 1)
                    continue
                b = s.b

                def convolve(blk):
                    after(pe, evacuated, (b - 1) * NBLK + (blk + 1))
                    t0 = blk * BLK
                    hi_lo, hi_hi = split[s.parity], pair[s.parity]
                    for k in range(TAPS):
                        pe.matmul(conv_ps[blk][:, :], cwh_dup[:, k * H:(k + 1) * H],
                                  hi_lo[:, t0 + k:t0 + k + BLK], start=(k == 0), stop=False)
                    for m in range(4):
                        last = pe.matmul(conv_ps[blk][:, :], cwl_pair[:, m * H:(m + 1) * H],
                                         hi_hi[:, t0 + 2 * m:t0 + 2 * m + BLK], start=False, stop=(m == 3))
                    last.then_inc(conv_done, 1)

                if s.has(0):
                    pe.wait_ge(high_made, (b + 1) * 16)
                    pe.wait_ge(low_made, b + 1)
                    convolve(0)
                if s.has(1):
                    pe.wait_ge(stat1, b)
                    pe.matmul(stat_ps[:, 0:2], ones, moments[0][:, :], start=True,
                              stop=True).then_inc(stat1_ps, 1)
                if s.has(2):
                    pe.wait_ge(dw_split, b - 1)
                    after(pe, gelu2, b - 2)
                    for half in range(2):
                        c = slice(half * BLK, (half + 1) * BLK)
                        pe.matmul(pw_ps[:, c], pw_hi[:, :], dw_hi[:, c], start=True, stop=False)
                        pe.matmul(pw_ps[:, c], pw_lo[:, :], dw_hi[:, c], start=False, stop=False)
                        last = pe.matmul(pw_ps[:, c], pw_hi[:, :], dw_lo[:, c], start=False, stop=True)
                    last.then_inc(pw_done, 1)
                if s.has(0):
                    convolve(1)
                    convolve(2)
                if s.has(2):
                    pe.wait_ge(stat2, b - 1)
                    pe.matmul(g_ps[:, 0:2], ones, moments[1][:, :], start=True,
                              stop=True).then_inc(stat2_ps, 1)
                if s.has(0):
                    convolve(3)

        @block.vector
        def _(dve):
            chain = Chain(dve, chain_v)
            chain.begin()

            def rounded(hi, lo, src):
                chain.link(dve.tensor_copy(hi, src))
                return dve.tensor_tensor(out=lo, in0=src, in1=hi.bitcast(F32), op=ALU.subtract)

            dve.memset(act1[:, GW - 2:GW], 0.0)
            chain.link(dve.memset(cw_pair[CIN:P, 3 * H:4 * H], 0.0))
            dve.wait_ge(consts_in, 16 * N_CONSTS)
            dve.tensor_copy(mask_bf[:, :], mask32)
            dve.tensor_copy(ident_bf[:, :], ident)
            dve.tensor_copy(cwh_dup[:, :], cw_dup)
            dve.tensor_copy(dw_hi[:, 0:4 * H], cw_pair)
            rounded(pw_hi[:, :], pw_lo[:, :], pw32)
            dve.tensor_tensor(out=cwl_pair[:, :], in0=cw_pair, in1=dw_hi[:, 0:4 * H].bitcast(F32),
                              op=ALU.subtract).then_inc(ready, 1)
            dve.wait_ge(g_made, 1)
            dve.tensor_copy(g32[:, :], g_ps[:, :]).then_inc(g_copied, 1)
            dve.wait_ge(g_copied, 1)
            dve.memset(act1[:, 0:2], 0.0)

            def average(which, bn):
                m = moments[which]
                chain.link(dve.bn_aggr(mv[which][:, :], bn.rearrange("p a s -> p (a s)")))
                dve.tensor_copy(m[:, 0:1], mv[which][:, 0:1])
                return dve.scalar_tensor_tensor(out=m[:, 1:2], in0=mv[which][:, 0:1], scalar=mv[which][:, 0:1],
                                                in1=mv[which][:, 1:2], op0=ALU.mult, op1=ALU.add)

            def variance(which):
                ps = (stat_ps, g_ps)[which]
                mean, msq = ps[:, 0:1], ps[:, 1:2]
                chain.link(dve.tensor_scalar(out=neg_mean[which][:, :], in0=mean, scalar1=-1.0, scalar2=None,
                                             op0=ALU.mult))
                chain.link(dve.tensor_tensor(out=var[which][:, :], in0=mean, in1=neg_mean[which][:, :],
                                             op=ALU.mult))
                return dve.tensor_scalar(out=var[which][:, :], in0=var[which][:, :], scalar1=msq, scalar2=EPS,
                                         op0=ALU.add, op1=ALU.add)

            def affine(which):
                chain.link(dve.tensor_tensor(out=gscale[which][:, :], in0=rstd[which][:, :], in1=gn_w[which],
                                             op=ALU.mult))
                return dve.scalar_tensor_tensor(out=gbias[which][:, :], in0=neg_mean[which][:, :],
                                                scalar=gscale[which][:, :], in1=gn_b[which],
                                                op0=ALU.mult, op1=ALU.add)

            for s in steps_of_phase_a(dve):
                if s is None:
                    for t in range(2):
                        dve.wait_ge(w_used[t], NPIECE // 2)
                    dve.wait_ge(squared, 1)
                    dve.tensor_reduce(out=sqt[:, 0:4], in_=sq[:, 0:16].rearrange("p (t n) -> p t n", n=4),
                                      axis=AX_X, op=ALU.add)
                    dve.tensor_reduce(out=sqt[:, 4:6], in_=sq[:, 16:20].rearrange("p (t n) -> p t n", n=2),
                                      axis=AX_X, op=ALU.add).then_inc(sums_split, 1)
                    dve.wait_ge(sums_total, 1)
                    steps = iter(range(2, 40))

                    def link(ins):
                        ins.then_inc(sums_split, 1)
                        dve.wait_ge(sums_split, next(steps))

                    link(dve.tensor_scalar(out=sqt[:, 0:7], in0=g_ps[:, 0:7], scalar1=float(P), scalar2=1e-18,
                                           op0=ALU.mult, op1=ALU.max))
                    link(dve.tensor_scalar(out=tmp_i[:, 0:7], in0=sqt[:, 0:7].bitcast(I32), scalar1=24,
                                           scalar2=None, op0=ALU.logical_shift_right))
                    link(dve.tensor_scalar(out=exp_i[:, 0:7], in0=tmp_i[:, 0:7], scalar1=-1.0, scalar2=199.0,
                                           op0=ALU.mult, op1=ALU.add))
                    link(dve.tensor_scalar(out=scl[:, 0:7].bitcast(I32), in0=exp_i[:, 0:7], scalar1=23,
                                           scalar2=None, op0=ALU.logical_shift_left))
                    link(dve.tensor_scalar(out=exp_i[:, 0:7], in0=tmp_i[:, 0:7], scalar1=1.0, scalar2=55.0,
                                           op0=ALU.mult, op1=ALU.add))
                    link(dve.tensor_scalar(out=inv[:, 0:7].bitcast(I32), in0=exp_i[:, 0:7], scalar1=23,
                                           scalar2=None, op0=ALU.logical_shift_left))
                    for c, (t, u, f) in enumerate(((Q_, K_, 0.5 / HD ** 0.5), (Q_, K_, -0.5 / HD ** 0.5),
                                                   (V_, O_, 1.0), (A_, B_, SCALING))):
                        dve.tensor_scalar(out=unscale[:, c:c + 1], in0=inv[:, t:t + 1], scalar1=inv[:, u:u + 1],
                                          scalar2=f, op0=ALU.mult, op1=ALU.mult)
                    link(dve.tensor_scalar(out=g_hi[:, :], in0=g32[:, :], scalar1=scl[:, 6:7], scalar2=None,
                                           op0=ALU.mult))
                    dve.scalar_tensor_tensor(out=g_lo[:, :], in0=g32[:, :], scalar=scl[:, 6:7], in1=g_hi[:, :],
                                             op0=ALU.mult, op1=ALU.subtract).then_inc(scaled, 1)
                    dve.sem_inc(lo_made, 1)
                    continue
                b = s.b
                chain.begin()

                if s.has(1):
                    dve.wait_ge(stat1_ps, b)
                    variance(0).then_inc(var1, 1)
                    dve.wait_ge(rstd1, b)
                    affine(0).then_inc(affine1, 1)
                if s.has(2):
                    dve.wait_ge(pw_done, b - 1)
                    dve.bn_stats(bn2[:, 0, :], pw_ps[:, 0:BLK])
                    chain.link(dve.bn_stats(bn2[:, 1, :], pw_ps[:, BLK:TO]))
                    average(1, bn2[:, :, :]).then_inc(stat2, 1)
                if s.has(1):
                    dve.wait_ge(tap0_made, b)
                    for k in range(1, DW):
                        chain.link(dve.scalar_tensor_tensor(out=dwo[:, :], in0=act1[:, k:k + 2 * TO - 1:2],
                                                            scalar=tap[k], in1=dwo[:, :],
                                                            op0=ALU.mult, op1=ALU.add))
                    after(dve, pw_done, b - 1)
                    rounded(dw_hi[:, :], dw_lo[:, :], dwo[:, :]).then_inc(dw_split, 1)
                if s.has(0):
                    for blk in range(NBLK):
                        dve.wait_ge(evacuated, b * NBLK + (blk + 1))
                        last = dve.bn_stats(bn1[:, blk, :], raw[:, blk * BLK:(blk + 1) * BLK])
                    chain.link(last)
                    average(0, bn1[:, :, :]).then_inc(stat1, 1)
                if s.has(2):
                    dve.wait_ge(stat2_ps, b - 1)
                    variance(1).then_inc(var2, 1)
                for kind, n, piece, tensor in s.items:
                    if kind == NORM:
                        continue
                    w = stage[n % 2][:, :]
                    done = split_count(s, n)
                    if kind == PAIRED:
                        src, hi = plus_minus[:, :], wqk_hi[:, bass.ds(piece * PIECE, PIECE)]
                        lo = wqk_lo[:, bass.ds(piece * PIECE, PIECE)]
                    if kind == PLAIN:
                        src, hi = w, wv_hi[:, bass.ds((piece - 8) * PIECE, PIECE)]
                        lo = wv_lo[:, bass.ds((piece - 8) * PIECE, PIECE)]
                    if kind == KEPT:
                        src, hi, lo = w, out_hi, out_lo
                    dve.wait_ge(hi_made, done + 1)
                    dve.scalar_tensor_tensor(out=lo, in0=src, scalar=scl[:, bass.ds(tensor, 1)], in1=hi,
                                             op0=ALU.mult, op1=ALU.subtract).then_inc(lo_made, 1)
                    if kind != PAIRED:
                        dve.wait_ge(lo_made, done + 2)
                        dve.sem_inc(w_used[n % 2], 1)
                if s.has(2):
                    dve.wait_ge(rstd2, b - 1)
                    affine(1).then_inc(affine2, 1)


def phase_b(nc, st, sb, h0, h1, split_dram, wqk_hi, wqk_lo, wv_hi, wv_lo, ident, rot,
            mask_bf, ident_bf, u_exp, u_neg, u_vo, half_neg):
    def buf(name, shape, dt):
        return sb(name, shape, dt, st)

    def psum(name, shape):
        return st.enter_context(nc.psum_tensor(name, shape, F32))

    def sem(name):
        return st.enter_context(nc.semaphore(name))

    NH = GB * 2
    wo_hi = buf("wo_hi", [P, 4 * PIECE], F16)
    wo_lo = buf("wo_lo", [P, 4 * PIECE], F16)
    h_ln = buf("h_ln", [P, GB, E], F32)
    h_res = buf("h_res", [P, GB, E], F32)
    xn = buf("xn", [P, GB, E], F32)
    xt_hi = buf("xt_hi", [P, KC, GT], F16)
    xt_lo = buf("xt_lo", [P, KC, GT], F16)
    v_hi = buf("v_hi", [P, GB, E], F16)
    v_lo = buf("v_lo", [P, GB, E], F16)
    qk32 = buf("qk32", [P, 2 * GT], F32)
    qk_hi = [buf(f"qk_hi{i}", [P, 2 * GT], F16) for i in range(2)]
    qk_lo = [buf(f"qk_lo{i}", [P, 2 * GT], F16) for i in range(2)]
    prob = buf("prob", [P, NH, P], F32)
    pn = buf("pn", [P, NH, P], F32)
    pt_hi = [buf(f"pt_hi{i}", [P, NH, P], F16) for i in range(2)]
    pt_lo = [buf(f"pt_lo{i}", [P, NH, P], F16) for i in range(2)]
    o_hi = buf("o_hi", [P, PAIRS, GT], F16)
    o_lo = buf("o_lo", [P, PAIRS, GT], F16)
    mx = buf("mx", [P, NH], F32)
    nb = buf("nb", [P, NH], F32)
    rsum = buf("rsum", [P, NH], F32)
    rinv = buf("rinv", [P, NH], F32)
    bn = buf("bnb", [P, GB, 2, 6], F32)
    mvb = buf("mvb", [P, GB, 2], F32)
    rstd = buf("rstdb", [P, GB], F32)

    qk_ps = [psum(f"qk_ps{i}", [P, 2 * GT]) for i in range(2)]
    wide_ps = [psum(f"wide_ps{i}", [P, BLK]) for i in range(2)]
    s_ps = psum("s_ps", [P, 2, BLK])
    t_ps = psum("t_ps", [P, BLK])
    o_ps = psum("o_ps", [P, BLK])

    wo_in = sem("b_wo_in")
    ln_in = sem("b_ln_in")
    res_in = sem("b_res_in")
    var_made = sem("b_var_made")
    rstd_made = sem("b_rstd_made")
    normed = sem("b_normed")
    xt_ps = sem("b_xt_ps")
    xt_high = sem("b_xt_high")
    xt_low = sem("b_xt_low")
    v_ps = sem("b_v_ps")
    v_high = sem("b_v_high")
    v_low = sem("b_v_low")
    wo_ps = sem("b_wo_ps")
    added = sem("b_added")
    qk_made = sem("b_qk_made")
    rotated = sem("b_rotated")
    qk_high = sem("b_qk_high")
    qk_low = sem("b_qk_low")
    scores = sem("b_scores")
    bias_made = sem("b_bias_made")
    exp_made = sem("b_exp_made")
    inverted = sem("b_inverted")
    divided = sem("b_divided")
    pt_ps = sem("b_pt_ps")
    pt_high = sem("b_pt_high")
    pt_low = sem("b_pt_low")
    o_made = sem("b_o_made")
    o_high = sem("b_o_high")
    o_low = sem("b_o_low")
    stored = sem("b_stored")
    chain_v = sem("b_chain_v")

    def groups(eng):
        yield 0, True
        with eng.Fori(1, NG - 1) as g:
            yield g, True
        yield NG - 1, False

    WIDE = GB * 2

    with nc.Block("phase_b") as block:

        @block.sync
        def _(sp):
            def load(dst, g, signal):
                sp.dma_start(dst[:, :, :], h0[bass.ds(g * GB, GB)].rearrange("b p e -> p b e")).then_inc(signal, 16)

            load(h_ln, 0, ln_in)
            for n in range(4):
                for part, dst in enumerate((wo_hi, wo_lo)):
                    sp.dma_start(dst[:, n * PIECE:(n + 1) * PIECE], split_dram[n, part]).then_inc(wo_in, 16)
            for g, more in groups(sp):
                after(sp, stored, g * 16 * GB)
                load(h_res, g, res_in)
                if more:
                    sp.wait_ge(normed, (g + 1) * GB)
                    load(h_ln, g + 1, ln_in)
                for b in range(GB):
                    sp.wait_ge(added, g * WIDE + (b + 1) * 2)
                    sp.dma_start(h1[g * GB + b], h_res[:, b, :]).then_inc(stored, 16)
            sp.wait_ge(stored, 16 * B)

        @block.gpsimd
        def _(pool):
            def root(g):
                pool.wait_ge(var_made, g + 1)
                pool.tensor_tensor(out=rstd[:, :], in0=mvb[:, :, 1], in1=half_neg[:, 0:GB],
                                   op=ALU.pow).then_inc(rstd_made, 1)
                pool.wait_ge(rstd_made, g + 1)

            root(0)
            for g, more in groups(pool):
                for j in range(PAIRS):
                    n = g * PAIRS + j
                    pool.wait_ge(inverted, n + 1)
                    after(pool, pt_ps, n)
                    pool.tensor_tensor(out=pn[:, :, :], in0=prob[:, :, :],
                                       in1=rinv[:, :].unsqueeze(2).to_broadcast([P, NH, P]),
                                       op=ALU.mult).then_inc(divided, 1)
                    pool.wait_ge(divided, n + 1)
                    if j == 2 and more:
                        root(g + 1)

        @block.scalar
        def _(act):
            def high(dst, src):
                return act.activation(dst, src, ACT.Copy)

            def xt_parts(g):
                for f in range(WIDE):
                    act.wait_ge(xt_ps, g * WIDE + (f + 1))
                    b, half = f // 2, f % 2
                    high(xt_hi[:, half * 4:half * 4 + 4, b * P:(b + 1) * P],
                         wide_ps[f % 2][:, :].rearrange("p (k t) -> p k t", k=4)).then_inc(xt_high, 1)

            def v_parts(g):
                for f in range(WIDE):
                    act.wait_ge(v_ps, g * WIDE + (f + 1))
                    b, half = f // 2, f % 2
                    high(v_hi[:, b, half * BLK:(half + 1) * BLK], wide_ps[f % 2][:, :]).then_inc(v_high, 1)

            def qk_part(g, j):
                act.wait_ge(rotated, g * PAIRS + (j + 1))
                after(act, scores, g * PAIRS + (j - 1))
                high(qk_hi[j % 2][:, :], qk32[:, :]).then_inc(qk_high, 1)

            def exps(g, j):
                act.wait_ge(bias_made, g * PAIRS + (j + 1))
                after(act, divided, g * PAIRS + j)
                for hh in range(2):
                    for b in range(GB):
                        c = hh * GB + b
                        act.activation(prob[:, c, :], s_ps[:, hh, b * P:(b + 1) * P], ACT.Exp,
                                       bias=nb[:, c:c + 1], scale=u_exp,
                                       accum_out=rsum[:, c:c + 1]).then_inc(exp_made, 1)

            def pt_part(g, j):
                act.wait_ge(pt_ps, g * PAIRS + (j + 1))
                after(act, o_made, g * PAIRS + (j - 1))
                high(pt_hi[j % 2][:, :, :].rearrange("p a t -> p (a t)"), t_ps[:, :]).then_inc(pt_high, 1)

            def o_part(g, j):
                act.wait_ge(o_made, g * PAIRS + (j + 1))
                high(o_hi[:, j, :], o_ps[:, 0:GT]).then_inc(o_high, 1)

            xt_parts(0)
            v_parts(0)
            for g, more in groups(act):
                qk_part(g, 0)
                for j in range(PAIRS):
                    if j + 1 < PAIRS:
                        qk_part(g, j + 1)
                    exps(g, j)
                    if j >= 1:
                        pt_part(g, j - 1)
                    if j >= 2:
                        o_part(g, j - 2)
                pt_part(g, PAIRS - 1)
                o_part(g, PAIRS - 2)
                if more:
                    xt_parts(g + 1)
                o_part(g, PAIRS - 1)
                if more:
                    v_parts(g + 1)

        @block.tensor
        def _(pe):
            def products(out, pairs, start=True, stop=True):
                steps = [(l[0], r[0]) for l, r in pairs] + [(l[0], r[1]) for l, r in pairs] \
                    + [(l[1], r[0]) for l, r in pairs]
                n = len(pairs)
                steps = [steps[c + part * n] for c in range(n) for part in range(3)]
                for i, (l, r) in enumerate(steps):
                    last = pe.matmul(out, l, r, start=start and i == 0, stop=stop and i == len(steps) - 1)
                return last

            def parts(hi, lo, *index):
                return hi[index], lo[index]

            ALL = slice(None)

            def transpose_xn(g):
                for f in range(WIDE):
                    b, half = f // 2, f % 2
                    pe.wait_ge(normed, g * GB + (b + 1))
                    if f < 2:
                        after(pe, added, (g - 1) * WIDE)
                    else:
                        pe.wait_ge(xt_low, g * WIDE + (f - 1))
                    for k in range(4):
                        c = half * 4 + k
                        last = pe.transpose(wide_ps[f % 2][:, k * P:(k + 1) * P], xn[:, b, c * P:(c + 1) * P], ident)
                    last.then_inc(xt_ps, 1)

            def project_v(g):
                for f in range(WIDE):
                    b, half = f // 2, f % 2
                    pe.wait_ge(xt_low, (g + 1) * WIDE)
                    if f >= 2:
                        pe.wait_ge(v_low, g * WIDE + (f - 1))
                    products(wide_ps[f % 2][:, :], [
                        (parts(xt_hi, xt_lo, ALL, k, slice(b * P, (b + 1) * P)),
                         parts(wv_hi, wv_lo, ALL, slice(k * E + half * BLK, k * E + (half + 1) * BLK)))
                        for k in range(KC)]).then_inc(v_ps, 1)

            def project_qk(g, j):
                after(pe, rotated, g * PAIRS + (j - 1))
                for which in range(2):
                    last = products(qk_ps[j % 2][:, which * GT:(which + 1) * GT], [
                        (parts(wqk_hi, wqk_lo, ALL, slice((which * KC + k) * E + j * P, (which * KC + k) * E + (j + 1) * P)),
                         parts(xt_hi, xt_lo, ALL, k, ALL))
                        for k in range(KC)])
                last.then_inc(qk_made, 1)

            def score(g, j):
                pe.wait_ge(qk_low, g * PAIRS + (j + 1))
                after(pe, exp_made, (g * PAIRS + j) * NH)
                for hh in range(2):
                    pe.matmul(s_ps[:, hh, 0:GT], ident_bf[:, :],
                              mask_bf[:, :].unsqueeze(1).to_broadcast([P, GB, P]), start=True, stop=False)
                    rows = slice(hh * HD, (hh + 1) * HD)
                    for b in range(GB):
                        q = parts(qk_hi[j % 2], qk_lo[j % 2], rows, slice(b * P, (b + 1) * P))
                        k = parts(qk_hi[j % 2], qk_lo[j % 2], rows, slice(GT + b * P, GT + (b + 1) * P))
                        last = products(s_ps[:, hh, b * P:(b + 1) * P], [(q, k)], start=False,
                                        stop=(b == GB - 1))
                last.then_inc(scores, 1)

            def transpose_p(g, j):
                pe.wait_ge(divided, g * PAIRS + (j + 1))
                after(pe, pt_low, g * PAIRS + j)
                for c in range(NH):
                    last = pe.transpose(t_ps[:, c * P:(c + 1) * P], pn[:, c, :], ident)
                last.then_inc(pt_ps, 1)

            def weigh_v(g, j):
                pe.wait_ge(pt_low, g * PAIRS + (j + 1))
                if j == 0:
                    pe.wait_ge(v_low, (g + 1) * WIDE)
                after(pe, o_low, g * PAIRS + j)
                for hh in range(2):
                    for b in range(GB):
                        head = (2 * j + hh) * HD
                        last = products(o_ps[hh * HD:(hh + 1) * HD, b * P:(b + 1) * P], [
                            (parts(v_hi, v_lo, ALL, b, slice(head, head + HD)),
                             parts(pt_hi[j % 2], pt_lo[j % 2], ALL, hh * GB + b, ALL))])
                last.then_inc(o_made, 1)

            def project_out(g, more):
                pe.wait_ge(o_low, (g + 1) * PAIRS)
                for f in range(WIDE):
                    b, half = f // 2, f % 2
                    if f >= 2:
                        pe.wait_ge(added, g * WIDE + (f - 1))
                    elif more:
                        pe.wait_ge(v_low, (g + 1) * WIDE + (f + 3))
                    products(wide_ps[f % 2][:, :], [
                        (parts(o_hi, o_lo, ALL, j, slice(b * P, (b + 1) * P)),
                         parts(wo_hi, wo_lo, ALL, slice(j * E + half * BLK, j * E + (half + 1) * BLK)))
                        for j in range(PAIRS)]).then_inc(wo_ps, 1)

            transpose_xn(0)
            project_v(0)
            for g, more in groups(pe):
                project_qk(g, 0)
                for j in range(PAIRS):
                    if j + 1 < PAIRS:
                        project_qk(g, j + 1)
                    score(g, j)
                    if j >= 1:
                        transpose_p(g, j - 1)
                    if j >= 2:
                        weigh_v(g, j - 2)
                transpose_p(g, PAIRS - 1)
                weigh_v(g, PAIRS - 2)
                if more:
                    transpose_xn(g + 1)
                weigh_v(g, PAIRS - 1)
                if more:
                    project_v(g + 1)
                pe.wait_ge(wo_in, 16 * 8)
                project_out(g, more)

        @block.vector
        def _(dve):
            chain = Chain(dve, chain_v)

            def statistics(g):
                dve.wait_ge(ln_in, (g + 1) * 16)
                for b in range(GB):
                    for half in range(2):
                        last = dve.bn_stats(bn[:, b, half, :], h_ln[:, b, half * BLK:(half + 1) * BLK])
                chain.link(last)
                for b in range(GB):
                    last = dve.bn_aggr(mvb[:, b, :], bn[:, b, :, :].rearrange("p a s -> p (a s)"))
                chain.link(last)
                dve.tensor_scalar(out=mvb[:, :, 1], in0=mvb[:, :, 1], scalar1=EPS, scalar2=None,
                                  op0=ALU.add).then_inc(var_made, 1)

            def norm(g):
                dve.wait_ge(rstd_made, g + 1)
                after(dve, xt_ps, g * WIDE)
                for b in range(GB):
                    dve.tensor_scalar(out=xn[:, b, :], in0=h_ln[:, b, :], scalar1=mvb[:, b, 0:1],
                                      scalar2=rstd[:, b:b + 1], op0=ALU.subtract,
                                      op1=ALU.mult).then_inc(normed, 1)

            def low(dst, src, hi):
                return dve.tensor_tensor(out=dst, in0=src, in1=hi, op=ALU.subtract)

            def xt_parts(g):
                for f in range(WIDE):
                    dve.wait_ge(xt_high, g * WIDE + (f + 1))
                    b, half = f // 2, f % 2
                    at = (slice(None), slice(half * 4, half * 4 + 4), slice(b * P, (b + 1) * P))
                    low(xt_lo[at], wide_ps[f % 2][:, :].rearrange("p (k t) -> p k t", k=4),
                        xt_hi[at]).then_inc(xt_low, 1)

            def v_parts(g):
                for f in range(WIDE):
                    dve.wait_ge(v_high, g * WIDE + (f + 1))
                    b, half = f // 2, f % 2
                    at = (slice(None), b, slice(half * BLK, (half + 1) * BLK))
                    low(v_lo[at], wide_ps[f % 2][:, :], v_hi[at]).then_inc(v_low, 1)

            def rotate(g, j):
                dve.wait_ge(qk_made, g * PAIRS + (j + 1))
                after(dve, qk_low, g * PAIRS + j)
                dve.tensor_tensor(out=qk32[:, :].rearrange("p (a t) -> p a t", t=P),
                                  in0=qk_ps[j % 2][:, :].rearrange("p (a t) -> p a t", t=P),
                                  in1=rot.unsqueeze(1).to_broadcast([P, 2 * GB, P]),
                                  op=ALU.mult).then_inc(rotated, 1)
                dve.wait_ge(qk_high, g * PAIRS + (j + 1))
                low(qk_lo[j % 2][:, :], qk32[:, :], qk_hi[j % 2][:, :]).then_inc(qk_low, 1)

            def maxima(g, j):
                dve.wait_ge(scores, g * PAIRS + (j + 1))
                chain.link(dve.tensor_reduce(out=mx[:, :].rearrange("p (h b) -> p h b", h=2),
                                             in_=s_ps[:, :, 0:GT].rearrange("p h (b t) -> p h b t", b=GB),
                                             axis=AX_X, op=ALU.max))
                dve.tensor_scalar(out=nb[:, :], in0=mx[:, :], scalar1=u_neg, scalar2=None,
                                  op0=ALU.mult).then_inc(bias_made, 1)

            def invert(g, j):
                dve.wait_ge(exp_made, (g * PAIRS + (j + 1)) * NH)
                after(dve, divided, g * PAIRS + j)
                dve.reciprocal(rinv[:, :], rsum[:, :]).then_inc(inverted, 1)

            def pt_part(g, j):
                dve.wait_ge(pt_high, g * PAIRS + (j + 1))
                low(pt_lo[j % 2][:, :, :].rearrange("p a t -> p (a t)"), t_ps[:, :],
                    pt_hi[j % 2][:, :, :].rearrange("p a t -> p (a t)")).then_inc(pt_low, 1)

            def o_part(g, j):
                dve.wait_ge(o_high, g * PAIRS + (j + 1))
                low(o_lo[:, j, :], o_ps[:, 0:GT], o_hi[:, j, :]).then_inc(o_low, 1)

            def residual(g):
                dve.wait_ge(res_in, (g + 1) * 16)
                for f in range(WIDE):
                    dve.wait_ge(wo_ps, g * WIDE + (f + 1))
                    b, half = f // 2, f % 2
                    at = h_res[:, b, half * BLK:(half + 1) * BLK]
                    dve.scalar_tensor_tensor(out=at, in0=wide_ps[f % 2][:, :], scalar=u_vo, in1=at,
                                             op0=ALU.mult, op1=ALU.add).then_inc(added, 1)

            chain.begin()
            statistics(0)
            norm(0)
            xt_parts(0)
            v_parts(0)
            for g, more in groups(dve):
                chain.begin()
                rotate(g, 0)
                for j in range(PAIRS):
                    if j + 1 < PAIRS:
                        rotate(g, j + 1)
                    maxima(g, j)
                    if j == 1 and more:
                        statistics(g + 1)
                    if j >= 1:
                        pt_part(g, j - 1)
                    if j >= 2:
                        o_part(g, j - 2)
                    invert(g, j)
                    if j == 4 and more:
                        norm(g + 1)
                pt_part(g, PAIRS - 1)
                o_part(g, PAIRS - 2)
                if more:
                    xt_parts(g + 1)
                o_part(g, PAIRS - 1)
                if more:
                    v_parts(g + 1)
                residual(g)


def phase_c(nc, st, sb, h1, out, split_dram, ident, u_ab, half_neg, g_hi, g_lo, g_inv):
    def buf(name, shape, dt):
        return sb(name, shape, dt, st)

    def psum(name, shape):
        return st.enter_context(nc.psum_tensor(name, shape, F32))

    def sem(name):
        return st.enter_context(nc.semaphore(name))

    ZC = BOT // P
    h = buf("h_all", [P, B, E], F32)
    a_hi = buf("a_hi", [P, 2 * PIECE], F16)
    a_lo = buf("a_lo", [P, 2 * PIECE], F16)
    b_hi = buf("b_hi", [P, 2 * PIECE], F16)
    b_lo = buf("b_lo", [P, 2 * PIECE], F16)
    xn = buf("xnc", [P, E], F32)
    xt_hi = buf("xtc_hi", [P, KC, P], F16)
    xt_lo = buf("xtc_lo", [P, KC, P], F16)
    sc = buf("sc", [P, NE], F32)
    left8 = buf("left8", [P, NE], F32)
    left16 = buf("left16", [P, NE], F32)
    top = buf("top", [P, 2, 8], F32)
    neg_top = buf("neg_top", [P, 1], F32)
    ex = buf("ex", [P, NE], F32)
    gate = buf("gate", [P, NE], F32)
    gsum = buf("gsum", [P, 1], F32)
    ginv = buf("ginv", [P, 1], F32)
    zg = buf("zg", [P, BOT], F32)
    zt_hi = buf("zt_hi", [P, ZC, P], F16)
    zt_lo = buf("zt_lo", [P, ZC, P], F16)
    res = [buf(f"res{i}", [P, E], F32) for i in range(1)][0]
    bn = buf("bnc", [P, 2, 6], F32)
    mvc = buf("mvc", [P, 2], F32)
    rstd = buf("rstdc", [P, 1], F32)

    xt_bank = [psum(f"xt_bank{i}", [P, BLK]) for i in range(2)]
    out_bank = [psum(f"out_bank{i}", [P, BLK]) for i in range(2)]
    z_bank = psum("z_bank", [P, BOT])
    zt_bank = psum("zt_bank", [P, BOT])
    sc_bank = psum("sc_bank", [P, NE])

    ab_in = sem("c_ab_in")
    h_in = sem("c_h_in")
    var_made = sem("c_var_made")
    rstd_made = sem("c_rstd_made")
    normed = sem("c_normed")
    xt_ps = sem("c_xt_ps")
    xt_high = sem("c_xt_high")
    xt_low = sem("c_xt_low")
    scored = sem("c_scored")
    z_made = sem("c_z_made")
    top_made = sem("c_top_made")
    exp_made = sem("c_exp_made")
    gated = sem("c_gated")
    zt_ps = sem("c_zt_ps")
    zt_high = sem("c_zt_high")
    zt_low = sem("c_zt_low")
    out_ps = sem("c_out_ps")
    added = sem("c_added")
    stored = sem("c_stored")
    chain_v = sem("c_chain_v")

    def steps(eng):
        def has(b):
            return lambda lag: not isinstance(b, int) or 0 <= b - lag < B

        for b in (0, 1):
            yield b, has(b)
        with eng.Fori(2, B - 2) as b:
            yield b, has(b)
        for b in (B - 2, B - 1, B):
            yield b, has(b)

    def products(pe, bank, pairs):
        for c, ((l_hi, l_lo), (r_hi, r_lo)) in enumerate(pairs):
            pe.matmul(bank, l_hi, r_hi, start=(c == 0), stop=False)
            pe.matmul(bank, l_hi, r_lo, start=False, stop=False)
            last = pe.matmul(bank, l_lo, r_hi, start=False, stop=(c == len(pairs) - 1))
        return last

    with nc.Block("phase_c") as block:

        @block.sync
        def _(sp):
            sp.dma_start(h[:, 0, :], h1[0]).then_inc(h_in, 16)
            for n in range(2):
                for row, parts in ((4, (a_hi, a_lo)), (6, (b_hi, b_lo))):
                    for part, dst in enumerate(parts):
                        sp.dma_start(dst[:, n * PIECE:(n + 1) * PIECE],
                                     split_dram[row + n, part]).then_inc(ab_in, 16)
            with sp.Fori(1, B) as b:
                sp.wait_ge(h_in, b * 16)
                sp.dma_start(h[:, b, :], h1[b]).then_inc(h_in, 16)
            for b, has in steps(sp):
                if has(1):
                    sp.wait_ge(added, b * 2)
                    sp.dma_start(out[b - 1], res[:, :]).then_inc(stored, 16)
            sp.wait_ge(stored, 16 * B)

        @block.gpsimd
        def _(pool):
            with pool.Fori(0, B) as b:
                pool.wait_ge(var_made, b + 1)
                pool.tensor_tensor(out=rstd[:, :], in0=mvc[:, 1:2], in1=half_neg[:, 0:1],
                                   op=ALU.pow).then_inc(rstd_made, 1)

        @block.scalar
        def _(act):
            def xt_parts(b):
                for f in range(2):
                    act.wait_ge(xt_ps, b * 2 + (f + 1))
                    act.activation(xt_hi[:, f * 4:f * 4 + 4, :],
                                   xt_bank[f][:, :].rearrange("p (k t) -> p k t", k=4),
                                   ACT.Copy).then_inc(xt_high, 1)

            xt_parts(0)
            for b, has in steps(act):
                if has(0):
                    act.wait_ge(top_made, b + 1)
                    act.activation(ex[:, :], sc[:, :], ACT.Exp, bias=neg_top[:, :]).then_inc(exp_made, 1)
                if has(-1):
                    xt_parts(b + 1)
                if has(0):
                    act.wait_ge(zt_ps, b + 1)
                    act.activation(zt_hi[:, :, :].rearrange("p k t -> p (k t)"), zt_bank[:, :],
                                   ACT.Copy).then_inc(zt_high, 1)

        @block.tensor
        def _(pe):
            def transpose_xn(b):
                pe.wait_ge(normed, b + 1)
                for f in range(2):
                    after(pe, xt_low, (b - 1) * 2 + (f + 1))
                    for k in range(4):
                        c = f * 4 + k
                        last = pe.transpose(xt_bank[f][:, k * P:(k + 1) * P], xn[:, c * P:(c + 1) * P], ident)
                    last.then_inc(xt_ps, 1)

            transpose_xn(0)
            pe.wait_ge(ab_in, 16 * 8)
            for b, has in steps(pe):
                x_parts = [(xt_hi[:, k, :], xt_lo[:, k, :]) for k in range(KC)]
                if has(0):
                    pe.wait_ge(xt_low, (b + 1) * 2)
                    after(pe, top_made, b)
                    products(pe, sc_bank[:, :], [
                        (x_parts[k], (g_hi[:, k * NE:(k + 1) * NE], g_lo[:, k * NE:(k + 1) * NE]))
                        for k in range(KC)]).then_inc(scored, 1)
                    after(pe, gated, b)
                    products(pe, z_bank[:, :], [
                        (x_parts[k], (a_hi[:, k * BOT:(k + 1) * BOT], a_lo[:, k * BOT:(k + 1) * BOT]))
                        for k in range(KC)]).then_inc(z_made, 1)
                if has(-1):
                    transpose_xn(b + 1)
                if has(1):
                    pe.wait_ge(zt_low, b)
                    for half in range(2):
                        after(pe, added, (b - 2) * 2 + (half + 1))
                        products(pe, out_bank[half][:, :], [
                            ((zt_hi[:, k, :], zt_lo[:, k, :]),
                             tuple(w[:, k * E + half * BLK:k * E + (half + 1) * BLK] for w in (b_hi, b_lo)))
                            for k in range(ZC)]).then_inc(out_ps, 1)
                if has(0):
                    pe.wait_ge(gated, b + 1)
                    for k in range(ZC):
                        last = pe.transpose(zt_bank[:, k * P:(k + 1) * P], zg[:, k * P:(k + 1) * P], ident)
                    last.then_inc(zt_ps, 1)

        @block.vector
        def _(dve):
            chain = Chain(dve, chain_v)

            def norm(b):
                dve.wait_ge(h_in, (b + 1) * 16)
                at = [h[:, bass.ds(b, 1), half * BLK:(half + 1) * BLK].rearrange("p a e -> p (a e)")
                      for half in range(2)]
                dve.bn_stats(bn[:, 0, :], at[0])
                chain.link(dve.bn_stats(bn[:, 1, :], at[1]))
                chain.link(dve.bn_aggr(mvc[:, :], bn[:, :, :].rearrange("p a s -> p (a s)")))
                chain.link(dve.tensor_scalar(out=mvc[:, 1:2], in0=mvc[:, 1:2], scalar1=EPS, scalar2=None,
                                             op0=ALU.add))
                dve.sem_inc(var_made, 1)
                dve.wait_ge(rstd_made, b + 1)
                after(dve, xt_ps, b * 2)
                dve.tensor_scalar(out=xn[:, :], in0=h[:, bass.ds(b, 1), :].rearrange("p a e -> p (a e)"),
                                  scalar1=mvc[:, 0:1], scalar2=rstd[:, :], op0=ALU.subtract,
                                  op1=ALU.mult).then_inc(normed, 1)

            def xt_parts(b):
                for f in range(2):
                    dve.wait_ge(xt_high, b * 2 + (f + 1))
                    dve.tensor_tensor(out=xt_lo[:, f * 4:f * 4 + 4, :],
                                      in0=xt_bank[f][:, :].rearrange("p (k t) -> p k t", k=4),
                                      in1=xt_hi[:, f * 4:f * 4 + 4, :], op=ALU.subtract).then_inc(xt_low, 1)

            chain.begin()
            norm(0)
            xt_parts(0)
            chain.begin()
            norm(1)
            for b, has in steps(dve):
                chain.begin()
                if has(0):
                    dve.wait_ge(scored, b + 1)
                    chain.link(dve.tensor_scalar(out=sc[:, :], in0=sc_bank[:, :], scalar1=g_inv, scalar2=None,
                                                 op0=ALU.mult))
                    chain.link(dve.max(out=top[:, 0, :], in_=sc[:, :]))
                    dve.tensor_scalar(out=neg_top[:, :], in0=top[:, 0, 0:1], scalar1=-1.0, scalar2=None,
                                      op0=ALU.mult).then_inc(top_made, 1)
                    chain.link(dve.match_replace(out=left8[:, :], in_to_replace=top[:, 0, :],
                                                 in_values=sc[:, :], imm_value=MASKED))
                    chain.link(dve.max(out=top[:, 1, :], in_=left8[:, :]))
                    chain.link(dve.match_replace(out=left16[:, :], in_to_replace=top[:, 1, :],
                                                 in_values=left8[:, :], imm_value=MASKED))
                    dve.wait_ge(exp_made, b + 1)
                    chain.link(dve.scalar_tensor_tensor(out=ex[:, :], in0=left16[:, :], scalar=MASKED / 2,
                                                        in1=ex[:, :], op0=ALU.is_le, op1=ALU.mult,
                                                        accum_out=gsum[:, :]))
                    chain.link(dve.reciprocal(ginv[:, :], gsum[:, :]))
                    chain.link(dve.tensor_scalar(out=gate[:, :], in0=ex[:, :], scalar1=ginv[:, :], scalar2=None,
                                                 op0=ALU.mult))
                    dve.wait_ge(z_made, b + 1)
                    after(dve, zt_ps, b)
                    dve.tensor_tensor(out=zg[:, :].rearrange("p (n r) -> p n r", r=RANK),
                                      in0=z_bank[:, :].rearrange("p (n r) -> p n r", r=RANK),
                                      in1=gate[:, :].unsqueeze(2).to_broadcast([P, NE, RANK]),
                                      op=ALU.mult).then_inc(gated, 1)
                if has(-1):
                    xt_parts(b + 1)
                if has(-2):
                    norm(b + 2)
                if has(1):
                    for half in range(2):
                        c = slice(half * BLK, (half + 1) * BLK)
                        dve.wait_ge(out_ps, (b - 1) * 2 + (half + 1))
                        after(dve, stored, (b - 1) * 16)
                        dve.scalar_tensor_tensor(
                            out=res[:, c], in0=out_bank[half][:, :], scalar=u_ab,
                            in1=h[:, bass.ds(b - 1, 1), c].rearrange("p a e -> p (a e)"),
                            op0=ALU.mult, op1=ALU.add).then_inc(added, 1)
                if has(0):
                    dve.wait_ge(zt_high, b + 1)
                    dve.tensor_tensor(out=zt_lo[:, :, :].rearrange("p k t -> p (k t)"), in0=zt_bank[:, :],
                                      in1=zt_hi[:, :, :].rearrange("p k t -> p (k t)"),
                                      op=ALU.subtract).then_inc(zt_low, 1)
def audio_tower_kernel(nc, x, conv_w, par, pw_w, w_all, wr, keys_t, const, out):
    h0 = nc.dram_tensor("h0", (B, P, E), F32, kind="Internal").ap()
    h1 = nc.dram_tensor("h1", (B, P, E), F32, kind="Internal").ap()
    split_dram = nc.dram_tensor("split_dram", (8, 2, P, PIECE), F16, kind="Internal").ap()
    with ExitStack() as whole:
        def sb(name, shape, dt, stack=whole):
            return stack.enter_context(nc.sbuf_tensor(name, shape, dt))

        cst = sb("cst", [P, 4 * P], F32)
        ident, rot, ones, mask32 = (cst[:, i * P:(i + 1) * P] for i in range(4))
        mask_bf = sb("mask_bf", [P, P], BF16)
        ident_bf = sb("ident_bf", [P, P], BF16)
        scl = sb("scl", [P, 8], F32)
        inv = sb("inv", [P, 8], F32)
        unscale = sb("unscale", [P, 4], F32)
        half_neg = sb("half_neg", [P, 8], F32)
        g_hi = sb("g_hi", [P, KC * NE], F16)
        g_lo = sb("g_lo", [P, KC * NE], F16)
        g_inv = inv[:, 6:7]
        u_exp, u_neg, u_vo, u_ab = (unscale[:, i:i + 1] for i in range(4))

        with ExitStack() as dense:
            wqk_hi = sb("wqk_hi", [P, 8 * PIECE], F16, dense)
            wqk_lo = sb("wqk_lo", [P, 8 * PIECE], F16, dense)
            wv_hi = sb("wv_hi", [P, 4 * PIECE], F16, dense)
            wv_lo = sb("wv_lo", [P, 4 * PIECE], F16, dense)
            with ExitStack() as s:
                phase_a(nc, s, sb, x, conv_w, par, pw_w, w_all, wr, keys_t, const, h0, split_dram,
                        wqk_hi, wqk_lo, wv_hi, wv_lo, cst, ident, ones, mask32, mask_bf, ident_bf,
                        scl, inv, unscale, half_neg, g_hi, g_lo)
            with ExitStack() as s:
                phase_b(nc, s, sb, h0, h1, split_dram, wqk_hi, wqk_lo, wv_hi, wv_lo, ident, rot,
                        mask_bf, ident_bf, u_exp, u_neg, u_vo, half_neg)
        with ExitStack() as s:
            phase_c(nc, s, sb, h1, out, split_dram, ident, u_ab, half_neg, g_hi, g_lo, g_inv)


def constants():
    import numpy as np

    j = np.arange(P) % HD
    inv_freq = (1.0 / 10000.0 ** (np.arange(0, HD, 2, dtype=np.float32) / np.float32(HD))).astype(np.float32)
    t = np.arange(P, dtype=np.float32)
    ang = (inv_freq[j % (HD // 2)][:, None] * t[None, :]).astype(np.float32).astype(np.float64)
    rot = np.cos(ang) + np.where(j < HD // 2, 1.0, -1.0)[:, None] * np.sin(ang)
    mask = np.where(np.arange(P)[None, :] > np.arange(P)[:, None], MASKED, 0.0)
    return np.concatenate([np.eye(P), rot, np.full((P, P), 1.0 / P), mask], 1).astype(np.float32)


def laid_out(inputs):
    import numpy as np

    i = {k: np.asarray(v) for k, v in inputs.items()}
    pieces = [i["L0_attn_" + w].reshape(KC, P, E) for w in ("Wq", "Wk", "Wv", "Wo")]
    pieces = [w.reshape(4, 2, P, E).transpose(0, 2, 1, 3).reshape(4, P, PIECE) for w in pieces]
    a = i["L0_ffn_A_w"].T.reshape(2, 4, P, BOT).transpose(0, 2, 1, 3).reshape(2, P, PIECE)
    b = i["L0_ffn_B_w"].T.reshape(2, 2, P, E).transpose(0, 2, 1, 3).reshape(2, P, PIECE)
    cols = [i["L0_tok_" + k][:, None] for k in ("dw_b", "gn1_w", "gn1_b", "gn2_w", "gn2_b")]
    arrays = {
        "x": i["x"],
        "conv_w": i["L0_tok_conv_in_w"].transpose(1, 2, 0).reshape(CIN, TAPS * H),
        "par": np.concatenate([i["L0_tok_dw_w"].reshape(H, DW)] + cols, 1),
        "pw_w": i["L0_tok_pw_w"].reshape(H, H).T,
        "w_all": np.concatenate(pieces + [a, b], 0),
        "wr": i["L0_ffn_Wq_w"],
        "keys_t": i["L0_ffn_keys"].T,
        "const": constants(),
    }
    return {k: np.ascontiguousarray(v) for k, v in arrays.items()}


def kernel(**inputs):
    import concourse.bacc as bacc
    from concourse.bass_utils import run_bass_kernel_spmd

    nc = bacc.Bacc("TRN2", target_bir_lowering=False, num_devices=1)
    arrays = laid_out(inputs)
    args = {n: nc.dram_tensor(n, a.shape, F32, kind="ExternalInput").ap() for n, a in arrays.items()}
    out = nc.dram_tensor("out", (B, P, E), F32, kind="ExternalOutput").ap()
    audio_tower_kernel(nc, out=out, **args)
    r = run_bass_kernel_spmd(nc, [arrays], core_ids=[0])
    return r.results[0]["out"]
```

```python
from contextlib import ExitStack

import concourse.bass as bass
from concourse import mybir

F32 = mybir.dt.float32
F32R = mybir.dt.float32r
F16 = mybir.dt.float16
BF16 = mybir.dt.bfloat16
I32 = mybir.dt.int32
ALU = mybir.AluOpType
ACT = mybir.ActivationFunctionType
AX_X = mybir.AxisListType.X

P = 128
B, CIN, T = 16, 64, 2048
H, TO = 128, 1024
TAPS, DW = 7, 5
PAD = 3
XW = T + 2 * PAD + 2
GW = T + 4
BLK = 512
NBLK = T // BLK
EPS = 1e-5
E = TO
KC = E // P
HEADS, HD = 16, 64
PAIRS = HEADS // 2
BOT = 512
NE, RANK, RD, TOPK = 64, 8, 16, 16
SCALING = 2.0
PIECE = 2048
NPIECE = 20
TENSOR_OF = [(0, 4), (4, 4), (8, 4), (12, 4), (16, 2), (18, 2)]
Q_, K_, V_, O_, A_, B_ = range(6)
MASKED = -3e38
GB = 2
GT = GB * P
NG = B // GB


def after(eng, sem, n):
    if not isinstance(n, int) or n > 0:
        eng.wait_ge(sem, n)


class Chain:

    def __init__(self, eng, sem):
        self.eng, self.sem, self.n = eng, sem, 0

    def begin(self):
        self.eng.sem_clear(self.sem)
        self.n = 0

    def link(self, ins):
        self.n += 1
        ins.then_inc(self.sem, 1)
        self.eng.wait_ge(self.sem, self.n)


class Step:

    def __init__(self, b, parity, i=0, per=0, items=()):
        self.b, self.parity, self.i, self.per, self.items = b, parity, i, per, items

    def has(self, lag):
        return not isinstance(self.b, int) or 0 <= self.b - lag < B

    def round(self, n):
        return n // 2 + self.i * (self.per // 2)


NORM, PAIRED, PLAIN, KEPT = "norm", "paired", "plain", "kept"


def steps_of_phase_a(eng):
    n = 0
    for b, count in enumerate((4, 4, 3, 3, 3, 3)):
        yield Step(b, b % 2, items=[(NORM, m, m, None) for m in range(n, n + count)])
        n += count
    yield None
    with eng.Fori(0, 2) as i:
        for p in range(4):
            n = NPIECE + 2 * p
            kept, tensor = (12 + p, O_) if p < 2 else (16 + p - 2, i + A_)
            yield Step(i * 4 + (6 + p), p % 2, i, 8, [(PAIRED, n, i * 4 + p, i),
                                                      (KEPT, n + 1, i * 2 + kept, tensor)])
    for b in range(14, 20):
        piece = b - 14 + 8
        yield Step(b, b % 2, items=[(PLAIN, NPIECE + 8 + piece, piece, V_)] if b < 18 else [])


def phase_a(nc, st, sb, x, conv_w, par, pw_w, w_all, wr, keys_t, const, h0, split_dram,
            wqk_hi, wqk_lo, wv_hi, wv_lo, cst, ident, ones, mask32, mask_bf, ident_bf,
            scl, inv, unscale, half_neg, g_hi, g_lo):
    def buf(name, shape, dt):
        return sb(name, shape, dt, st)

    def psum(name, shape):
        return st.enter_context(nc.psum_tensor(name, shape, F32))

    def sem(name):
        return st.enter_context(nc.semaphore(name))

    xs = buf("xs", [P, XW], F32)
    pair = [buf(f"pair{i}", [P, XW], F32R) for i in range(2)]
    split = [buf(f"split{i}", [P, XW], F32R) for i in range(2)]
    mid = [buf(f"mid{i}", [P, GW], F32) for i in range(2)]
    dwo = buf("dwo", [P, TO], F32)
    dw_hi = buf("dw_hi", [P, TO], F32R)
    dw_lo = buf("dw_lo", [P, TO], F32R)
    tok = buf("tok", [P, TO], F32)
    stage = [buf(f"stage{i}", [P, PIECE], F32) for i in range(2)]
    plus_minus = buf("plus_minus", [P, PIECE], F32)
    squares = plus_minus
    out = [wv_lo[:, 2 * i * PIECE:2 * (i + 1) * PIECE].rearrange("p (t c) -> p t c", t=2) for i in range(2)]
    cw_dup = mid[0][:, 0:TAPS * H]
    cw_pair = mid[0][:, TAPS * H:(TAPS + 4) * H]
    pw32 = mid[0][:, (TAPS + 4) * H:(TAPS + 5) * H]
    wr_sb = mid[1][0:RD, 0:E]
    keys_sb = mid[1][0:RD, E:E + NE]
    cwh_dup = buf("cwh_dup", [P, TAPS * H], F32R)
    cwl_pair = buf("cwl_pair", [P, 4 * H], F32R)
    pw_hi = buf("pw_hi", [P, H], F32R)
    pw_lo = buf("pw_lo", [P, H], F32R)
    prm = buf("prm", [P, DW + 5], F32)
    tap = [prm[:, k:k + 1] for k in range(DW)]
    dw_bias, gn_w, gn_b = prm[:, DW:DW + 1], (prm[:, 6:7], prm[:, 8:9]), (prm[:, 7:8], prm[:, 9:10])
    sq = buf("sq", [P, NPIECE], F32)
    sqt = buf("sqt", [P, 8], F32)
    tmp_i = buf("tmp_i", [P, 8], I32)
    exp_i = buf("exp_i", [P, 8], I32)
    bn1 = buf("bn1", [P, NBLK, 6], F32)
    bn2 = buf("bn2", [P, 2, 6], F32)
    mv = [buf(f"mv{i}", [P, 2], F32) for i in range(2)]
    moments = [buf(f"moments{i}", [P, 2], F32) for i in range(2)]
    neg_mean = [buf(f"neg_mean{i}", [P, 1], F32) for i in range(2)]
    var = [buf(f"var{i}", [P, 1], F32) for i in range(2)]
    rstd = [buf(f"rstd{i}", [P, 1], F32) for i in range(2)]
    gscale = [buf(f"gscale{i}", [P, 1], F32) for i in range(2)]
    gbias = [buf(f"gbias{i}", [P, 1], F32) for i in range(2)]
    g32 = buf("g32", [P, KC * NE], F32)

    conv_ps = [psum(f"conv_ps{i}", [P, BLK]) for i in range(NBLK)]
    pw_ps = psum("pw_ps", [P, TO])
    stat_ps = psum("stat_ps", [P, 16])
    g_ps = psum("g_ps", [P, KC * NE])

    consts_in = sem("a_consts_in")
    pads_made = sem("a_pads_made")
    pool_done = sem("a_pool_done")
    ready = sem("a_ready")
    g_made = sem("a_g_made")
    g_copied = sem("a_g_copied")
    x_in = sem("a_x_in")
    pair_made = sem("a_pair_made")
    high_made = sem("a_high_made")
    low_made = sem("a_low_made")
    conv_done = sem("a_conv_done")
    evacuated = sem("a_evacuated")
    stat1 = sem("a_stat1")
    stat1_ps = sem("a_stat1_ps")
    var1 = sem("a_var1")
    rstd1 = sem("a_rstd1")
    affine1 = sem("a_affine1")
    gelu1 = sem("a_gelu1")
    tap0_made = sem("a_tap0_made")
    dw_high = sem("a_dw_high")
    dw_split = sem("a_dw_split")
    pw_done = sem("a_pw_done")
    stat2 = sem("a_stat2")
    stat2_ps = sem("a_stat2_ps")
    var2 = sem("a_var2")
    rstd2 = sem("a_rstd2")
    affine2 = sem("a_affine2")
    gelu2 = sem("a_gelu2")
    stored = sem("a_stored")
    w_in = [sem(f"a_w_in{i}") for i in range(2)]
    w_used = [sem(f"a_w_used{i}") for i in range(2)]
    sums_made = sem("a_sums_made")
    paired_hi = sem("a_paired_hi")
    paired_lo = sem("a_paired_lo")
    kept_hi = sem("a_kept_hi")
    kept_lo = sem("a_kept_lo")
    plain_hi = sem("a_plain_hi")
    plain_lo = sem("a_plain_lo")
    kept = sem("a_kept")
    squared = sem("a_squared")
    sums_split = sem("a_sums_split")
    sums_total = sem("a_sums_total")
    scaled = sem("a_scaled")
    chain_v = sem("a_chain_v")
    passed = sem("a_passed")

    N_CONSTS = 7 + TAPS

    def place_parity(n):
        return (n // 2) % 2

    def place(s, n):
        return (n - NPIECE) // 2 + s.i * (s.per // 2)

    def load_x(eng, b):
        eng.dma_start(xs[0:CIN, PAD:PAD + T], x[b]).then_inc(x_in, 16)
        eng.dma_start(xs[CIN:P, PAD - 1:PAD - 1 + T], x[b]).then_inc(x_in, 16)

    with nc.Block("phase_a") as block:

        @block.sync
        def _(sp):
            sp.dma_start(cst[:, :], const).then_inc(consts_in, 16)
            sp.dma_start(prm[:, :], par).then_inc(consts_in, 16)
            sp.dma_start(pw32, pw_w).then_inc(consts_in, 16)
            for half in range(2):
                sp.dma_start(cw_dup[half * CIN:(half + 1) * CIN, :], conv_w).then_inc(consts_in, 16)
            for k in range(TAPS):
                half, m = k % 2, k // 2
                sp.dma_start(cw_pair[half * CIN:(half + 1) * CIN, m * H:(m + 1) * H],
                             conv_w[:, k * H:(k + 1) * H]).then_inc(consts_in, 16)
            sp.dma_start(wr_sb, wr).then_inc(consts_in, 16)
            sp.dma_start(keys_sb, keys_t).then_inc(consts_in, 16)

            def copy_high(b, parity):
                after(sp, high_made, b * 16)
                sp.sem_inc(passed, 1)
                sp.wait_ge(pair_made, b + 1)
                sp.dma_start(split[parity][0:CIN, :].bitcast(F32),
                             pair[parity][0:CIN, :].bitcast(F32)).then_inc(high_made, 16)

            sp.wait_ge(pads_made, 1)
            load_x(sp, 0)
            copy_high(0, 0)
            for s in steps_of_phase_a(sp):
                if s is None:
                    continue
                b = s.b
                for kind, n, piece, tensor in s.items:
                    after(sp, w_used[n % 2], s.round(n))
                    sp.dma_start(stage[n % 2][:, :], w_all[piece]).then_inc(w_in[n % 2], 16)
                if s.has(-1):
                    copy_high(b + 1, 1 - s.parity)
                if s.has(4):
                    sp.wait_ge(gelu2, b - 3)
                    sp.dma_start(h0[b - 4], tok[:, :]).then_inc(stored, 16)
            sp.wait_ge(stored, 16 * B)

        @block.gpsimd
        def _(pool):
            pool.memset(half_neg[:, :], -0.5).then_inc(pool_done, 1)
            pool.wait_ge(pool_done, 1)
            for i in range(2):
                pool.memset(split[i][CIN:P, 0:1].bitcast(F32), 0.0).then_inc(pool_done, 1)
                pool.wait_ge(pool_done, 2 + i)
            pool.memset(xs[:, :], 0.0).then_inc(pads_made, 1)
            pool.wait_ge(pads_made, 1)

            def low(b, parity):
                pool.wait_ge(pair_made, b + 1)
                pool.tensor_tensor(out=split[parity][CIN:P, 1:XW], in0=xs[CIN:P, 0:XW - 1],
                                   in1=pair[parity][CIN:P, 0:XW - 1].bitcast(F32),
                                   op=ALU.subtract).then_inc(low_made, 1)
                pool.wait_ge(low_made, b + 1)

            low(0, 0)
            for s in steps_of_phase_a(pool):
                if s is None:
                    pool.wait_ge(scaled, 1)
                    continue
                b = s.b

                def sums(half):
                    for kind, n, piece, tensor in s.items:
                        if kind != PAIRED:
                            continue
                        src = stage[n % 2][:, :].rearrange("p (a h c two) -> p a h c two", a=2, h=HEADS, two=2)
                        dst = plus_minus[:, :].rearrange("p (a h s c) -> p a h s c", a=2, h=HEADS, s=2)
                        if half == 0:
                            pool.wait_ge(w_in[n % 2], (s.round(n) + 1) * 16)
                            pool.wait_ge(paired_lo, place(s, n) + 1)
                        for a in range(2):
                            last = pool.tensor_tensor(out=dst[:, a, :, half, :], in0=src[:, a, :, :, 0],
                                                      in1=src[:, a, :, :, 1], op=(ALU.add, ALU.subtract)[half])
                        last.then_inc(sums_made, 1)
                        pool.wait_ge(sums_made, 2 * place(s, n) + 1 + half)
                        if half == 1:
                            pool.sem_inc(w_used[n % 2], 1)

                if s.has(4):
                    pool.wait_ge(var2, b - 3)
                    pool.tensor_tensor(out=rstd[1][:, :], in0=var[1][:, :], in1=half_neg[:, 0:1],
                                       op=ALU.pow).then_inc(rstd2, 1)
                    pool.wait_ge(rstd2, b - 3)
                sums(0)
                if s.has(1):
                    pool.wait_ge(var1, b)
                    pool.tensor_tensor(out=rstd[0][:, :], in0=var[0][:, :], in1=half_neg[:, 0:1],
                                       op=ALU.pow).then_inc(rstd1, 1)
                    pool.wait_ge(rstd1, b)
                sums(1)
                if s.has(-1):
                    low(b + 1, 1 - s.parity)
                if s.has(2):
                    pool.wait_ge(dw_high, b - 1)
                    pool.tensor_tensor(out=dw_lo[:, :], in0=dwo[:, :], in1=dw_hi[:, :].bitcast(F32),
                                       op=ALU.subtract).then_inc(dw_split, 1)
                    pool.wait_ge(dw_split, b - 1)

        @block.scalar
        def _(act):
            def make_pair(b, parity):
                act.wait_ge(x_in, (b + 1) * 32)
                after(act, conv_done, (b - 1) * NBLK)
                act.activation(pair[parity][:, :], xs[:, :], ACT.Copy).then_inc(pair_made, 1)

            act.sem_inc(kept, 32)
            act.wait_ge(g_copied, 1)
            act.activation(squares[:, 0:KC * NE], g32[:, :], ACT.Square,
                           accum_out=sqt[:, 6:7]).then_inc(squared, 1)
            make_pair(0, 0)
            act.wait_ge(low_made, 1)
            load_x(act, 1)
            for s in steps_of_phase_a(act):
                if s is None:
                    act.wait_ge(scaled, 1)
                    continue
                b = s.b

                def copy_out(blk):
                    act.wait_ge(conv_done, b * NBLK + (blk + 1))
                    if blk == 0:
                        after(act, dw_high, b - 1)
                    c = 2 + blk * BLK
                    act.activation(mid[s.parity][:, c:c + BLK], conv_ps[blk][:, :],
                                   ACT.Copy).then_inc(evacuated, 1)

                def item(kind, n, piece, tensor):
                    w = stage[n % 2][:, :]
                    if kind == NORM:
                        act.wait_ge(w_in[n % 2], (s.round(n) + 1) * 16)
                        if n == 0:
                            act.wait_ge(squared, 1)
                        else:
                            act.wait_ge(w_used[(n - 1) % 2], s.round(n - 1) + 1)
                            act.sem_inc(passed, 1)
                        act.activation(squares[:, :], w, ACT.Square,
                                       accum_out=sq[:, bass.ds(piece, 1)]).then_inc(w_used[n % 2], 1)
                        return
                    scale = scl[:, bass.ds(tensor, 1)]
                    if kind == PAIRED:
                        act.wait_ge(sums_made, 2 * place(s, n) + 2)
                        act.sem_inc(passed, 1)
                        act.activation(wqk_hi[:, bass.ds(piece * PIECE, PIECE)], plus_minus[:, :],
                                       ACT.Copy, scale=scale).then_inc(paired_hi, 1)
                    if kind == PLAIN:
                        act.wait_ge(w_in[n % 2], (s.round(n) + 1) * 16)
                        act.activation(wv_hi[:, (piece - 8) * PIECE:(piece - 7) * PIECE], w,
                                       ACT.Copy, scale=scale).then_inc(plain_hi, 1)
                    if kind == KEPT:
                        act.wait_ge(w_in[n % 2], (s.round(n) + 1) * 16)
                        act.wait_ge(kept, place(s, n) * 16 + 16)
                        act.sem_inc(passed, 1)
                        act.activation(out[place_parity(n)][:, 0, :], w, ACT.Copy,
                                       scale=scale).then_inc(kept_hi, 1)

                if s.has(2):
                    act.wait_ge(gelu1, b - 1)
                    after(act, dw_split, b - 2)
                    act.activation(dwo[:, :], mid[s.parity][:, 0:2 * TO:2], ACT.Identity, bias=dw_bias,
                                   scale=tap[0]).then_inc(tap0_made, 1)
                if s.has(-1):
                    make_pair(b + 1, 1 - s.parity)
                if s.has(4):
                    act.wait_ge(affine2, b - 3)
                    after(act, stored, (b - 4) * 16)
                    act.activation(tok[:, :], pw_ps[:, :], ACT.Gelu, bias=gbias[1][:, :],
                                   scale=gscale[1][:, :]).then_inc(gelu2, 1)
                paired = s.items and s.items[0][0] == PAIRED
                first, rest = (s.items[1:], s.items[:1]) if paired else (s.items[:1], s.items[1:])
                for it in first:
                    item(*it)
                if s.has(0):
                    copy_out(0)
                    copy_out(1)
                if paired:
                    item(*rest[0])
                if s.has(1):
                    act.wait_ge(affine1, b)
                    m = mid[1 - s.parity][:, 2:2 + T]
                    act.activation(m, m, ACT.Gelu, bias=gbias[0][:, :],
                                   scale=gscale[0][:, :]).then_inc(gelu1, 1)
                if s.has(-2):
                    act.wait_ge(low_made, b + 2)
                    load_x(act, b + 2)
                if s.has(0):
                    copy_out(2)
                    copy_out(3)
                for kind, n, piece, tensor in s.items:
                    if kind == KEPT:
                        act.wait_ge(kept_lo, place(s, n) + 1)
                        act.dma_start(split_dram[piece - 12].rearrange("t p c -> p t c"),
                                     out[place_parity(n)]).then_inc(kept, 16)
                if not paired:
                    for it in rest:
                        item(*it)

        @block.tensor
        def _(pe):
            pe.wait_ge(consts_in, 16 * N_CONSTS)
            for k in range(KC):
                last = pe.matmul(g_ps[:, k * NE:(k + 1) * NE], wr_sb[:, k * P:(k + 1) * P], keys_sb,
                                 start=True, stop=True)
            last.then_inc(g_made, 1)
            pe.wait_ge(ready, 1)
            for s in steps_of_phase_a(pe):
                if s is None:
                    pe.wait_ge(sums_split, 1)
                    pe.matmul(stat_ps[:, 8:15], ones, sqt[:, 0:7], start=True, stop=True).then_inc(sums_total, 1)
                    pe.wait_ge(sums_split, 2)
                    continue
                b = s.b

                def convolve(blk):
                    after(pe, evacuated, (b - 1) * NBLK + (blk + 1))
                    t0 = blk * BLK
                    hi_lo, hi_hi = split[s.parity], pair[s.parity]
                    for k in range(TAPS):
                        pe.matmul(conv_ps[blk][:, :], cwh_dup[:, k * H:(k + 1) * H],
                                  hi_lo[:, t0 + k:t0 + k + BLK], start=(k == 0), stop=False)
                    for m in range(4):
                        last = pe.matmul(conv_ps[blk][:, :], cwl_pair[:, m * H:(m + 1) * H],
                                         hi_hi[:, t0 + 2 * m:t0 + 2 * m + BLK], start=False, stop=(m == 3))
                    last.then_inc(conv_done, 1)

                if s.has(0):
                    pe.wait_ge(high_made, (b + 1) * 16)
                    pe.wait_ge(low_made, b + 1)
                    convolve(0)
                if s.has(1):
                    pe.wait_ge(stat1, b)
                    pe.matmul(stat_ps[:, 0:2], ones, moments[0][:, :], start=True,
                              stop=True).then_inc(stat1_ps, 1)
                if s.has(0):
                    convolve(1)
                    convolve(2)
                if s.has(3):
                    pe.wait_ge(dw_split, b - 2)
                    after(pe, gelu2, b - 3)
                    for half in range(2):
                        c = slice(half * BLK, (half + 1) * BLK)
                        pe.matmul(pw_ps[:, c], pw_hi[:, :], dw_hi[:, c], start=True, stop=False)
                        pe.matmul(pw_ps[:, c], pw_lo[:, :], dw_hi[:, c], start=False, stop=False)
                        last = pe.matmul(pw_ps[:, c], pw_hi[:, :], dw_lo[:, c], start=False, stop=True)
                    last.then_inc(pw_done, 1)
                if s.has(0):
                    convolve(3)
                if s.has(3):
                    pe.wait_ge(stat2, b - 2)
                    pe.matmul(g_ps[:, 0:2], ones, moments[1][:, :], start=True,
                              stop=True).then_inc(stat2_ps, 1)

        @block.vector
        def _(dve):
            chain = Chain(dve, chain_v)
            chain.begin()

            def rounded(hi, lo, src):
                chain.link(dve.tensor_copy(hi, src))
                return dve.tensor_tensor(out=lo, in0=src, in1=hi.bitcast(F32), op=ALU.subtract)

            for m in mid:
                dve.memset(m[:, GW - 2:GW], 0.0)
            chain.link(dve.memset(cw_pair[CIN:P, 3 * H:4 * H], 0.0))
            dve.wait_ge(consts_in, 16 * N_CONSTS)
            dve.tensor_copy(mask_bf[:, :], mask32)
            dve.tensor_copy(ident_bf[:, :], ident)
            dve.tensor_copy(cwh_dup[:, :], cw_dup)
            dve.tensor_copy(dw_hi[:, 0:4 * H], cw_pair)
            rounded(pw_hi[:, :], pw_lo[:, :], pw32)
            dve.tensor_tensor(out=cwl_pair[:, :], in0=cw_pair, in1=dw_hi[:, 0:4 * H].bitcast(F32),
                              op=ALU.subtract).then_inc(ready, 1)
            dve.wait_ge(g_made, 1)
            dve.tensor_copy(g32[:, :], g_ps[:, :]).then_inc(g_copied, 1)
            dve.wait_ge(g_copied, 1)
            for m in mid:
                dve.memset(m[:, 0:2], 0.0)

            def average(which, bn):
                m = moments[which]
                chain.link(dve.bn_aggr(mv[which][:, :], bn.rearrange("p a s -> p (a s)")))
                dve.tensor_copy(m[:, 0:1], mv[which][:, 0:1])
                return dve.scalar_tensor_tensor(out=m[:, 1:2], in0=mv[which][:, 0:1], scalar=mv[which][:, 0:1],
                                                in1=mv[which][:, 1:2], op0=ALU.mult, op1=ALU.add)

            def variance(which):
                ps = (stat_ps, g_ps)[which]
                mean, msq = ps[:, 0:1], ps[:, 1:2]
                chain.link(dve.tensor_scalar(out=neg_mean[which][:, :], in0=mean, scalar1=-1.0, scalar2=None,
                                             op0=ALU.mult))
                chain.link(dve.tensor_tensor(out=var[which][:, :], in0=mean, in1=neg_mean[which][:, :],
                                             op=ALU.mult))
                return dve.tensor_scalar(out=var[which][:, :], in0=var[which][:, :], scalar1=msq, scalar2=EPS,
                                         op0=ALU.add, op1=ALU.add)

            def affine(which):
                chain.link(dve.tensor_tensor(out=gscale[which][:, :], in0=rstd[which][:, :], in1=gn_w[which],
                                             op=ALU.mult))
                return dve.scalar_tensor_tensor(out=gbias[which][:, :], in0=neg_mean[which][:, :],
                                                scalar=gscale[which][:, :], in1=gn_b[which],
                                                op0=ALU.mult, op1=ALU.add)

            for s in steps_of_phase_a(dve):
                if s is None:
                    for t in range(2):
                        dve.wait_ge(w_used[t], NPIECE // 2)
                    dve.wait_ge(squared, 1)
                    dve.tensor_reduce(out=sqt[:, 0:4], in_=sq[:, 0:16].rearrange("p (t n) -> p t n", n=4),
                                      axis=AX_X, op=ALU.add)
                    dve.tensor_reduce(out=sqt[:, 4:6], in_=sq[:, 16:20].rearrange("p (t n) -> p t n", n=2),
                                      axis=AX_X, op=ALU.add).then_inc(sums_split, 1)
                    dve.wait_ge(sums_total, 1)
                    steps = iter(range(2, 40))

                    def link(ins):
                        ins.then_inc(sums_split, 1)
                        dve.wait_ge(sums_split, next(steps))

                    link(dve.tensor_scalar(out=sqt[:, 0:7], in0=stat_ps[:, 8:15], scalar1=float(P), scalar2=1e-18,
                                           op0=ALU.mult, op1=ALU.max))
                    link(dve.tensor_scalar(out=tmp_i[:, 0:7], in0=sqt[:, 0:7].bitcast(I32), scalar1=24,
                                           scalar2=None, op0=ALU.logical_shift_right))
                    link(dve.tensor_scalar(out=exp_i[:, 0:7], in0=tmp_i[:, 0:7], scalar1=-1.0, scalar2=199.0,
                                           op0=ALU.mult, op1=ALU.add))
                    link(dve.tensor_scalar(out=scl[:, 0:7].bitcast(I32), in0=exp_i[:, 0:7], scalar1=23,
                                           scalar2=None, op0=ALU.logical_shift_left))
                    link(dve.tensor_scalar(out=exp_i[:, 0:7], in0=tmp_i[:, 0:7], scalar1=1.0, scalar2=55.0,
                                           op0=ALU.mult, op1=ALU.add))
                    link(dve.tensor_scalar(out=inv[:, 0:7].bitcast(I32), in0=exp_i[:, 0:7], scalar1=23,
                                           scalar2=None, op0=ALU.logical_shift_left))
                    for c, (t, u, f) in enumerate(((Q_, K_, 0.5 / HD ** 0.5), (Q_, K_, -0.5 / HD ** 0.5),
                                                   (V_, O_, 1.0), (A_, B_, SCALING))):
                        dve.tensor_scalar(out=unscale[:, c:c + 1], in0=inv[:, t:t + 1], scalar1=inv[:, u:u + 1],
                                          scalar2=f, op0=ALU.mult, op1=ALU.mult)
                    link(dve.tensor_scalar(out=g_hi[:, :], in0=g32[:, :], scalar1=scl[:, 6:7], scalar2=None,
                                           op0=ALU.mult))
                    dve.scalar_tensor_tensor(out=g_lo[:, :], in0=g32[:, :], scalar=scl[:, 6:7], in1=g_hi[:, :],
                                             op0=ALU.mult, op1=ALU.subtract).then_inc(scaled, 1)
                    dve.sem_inc(paired_lo, 1)
                    continue
                b = s.b
                chain.begin()


                def taps(*ks):
                    for k in ks:
                        last = dve.scalar_tensor_tensor(out=dwo[:, :], in0=mid[s.parity][:, k:k + 2 * TO - 1:2],
                                                        scalar=tap[k], in1=dwo[:, :], op0=ALU.mult, op1=ALU.add)
                        chain.link(last)

                def stats(blk):
                    dve.wait_ge(evacuated, b * NBLK + (blk + 1))
                    c = 2 + blk * BLK
                    return dve.bn_stats(bn1[:, blk, :], mid[s.parity][:, c:c + BLK])

                def low_part(kind, n, piece, tensor):
                    if kind == NORM:
                        return
                    w = stage[n % 2][:, :]
                    if kind == PAIRED:
                        dve.wait_ge(paired_hi, place(s, n) + 1)
                        src, hi = plus_minus[:, :], wqk_hi[:, bass.ds(piece * PIECE, PIECE)]
                        lo, made = wqk_lo[:, bass.ds(piece * PIECE, PIECE)], paired_lo
                    if kind == KEPT:
                        dve.wait_ge(kept_hi, place(s, n) + 1)
                        src, hi, lo, made = w, out[place_parity(n)][:, 0, :], out[place_parity(n)][:, 1, :], kept_lo
                    if kind == PLAIN:
                        dve.wait_ge(plain_hi, piece - 7)
                        dve.wait_ge(kept, 32 + 16 * 8)
                        c = slice((piece - 8) * PIECE, (piece - 7) * PIECE)
                        src, hi, lo, made = w, wv_hi[:, c], wv_lo[:, c], plain_lo
                    dve.scalar_tensor_tensor(out=lo, in0=src, scalar=scl[:, bass.ds(tensor, 1)], in1=hi,
                                             op0=ALU.mult, op1=ALU.subtract).then_inc(made, 1)
                    if kind == KEPT:
                        dve.wait_ge(kept_lo, place(s, n) + 1)
                    if kind == PLAIN:
                        dve.wait_ge(plain_lo, piece - 7)
                    if kind != PAIRED:
                        dve.sem_inc(w_used[n % 2], 1)

                if s.has(4):
                    dve.wait_ge(stat2_ps, b - 3)
                    variance(1).then_inc(var2, 1)
                if s.has(2):
                    dve.wait_ge(tap0_made, b - 1)
                    taps(1, 2)
                if s.has(1):
                    dve.wait_ge(stat1_ps, b)
                    variance(0).then_inc(var1, 1)
                if s.has(4):
                    dve.wait_ge(rstd2, b - 3)
                    affine(1).then_inc(affine2, 1)
                if s.has(2):
                    taps(3)
                if s.has(1):
                    dve.wait_ge(rstd1, b)
                    affine(0).then_inc(affine1, 1)
                if s.has(2):
                    taps(4)
                    after(dve, pw_done, b - 2)
                    dve.tensor_copy(dw_hi[:, :], dwo[:, :]).then_inc(dw_high, 1)
                for it in s.items:
                    if it[0] == KEPT:
                        low_part(*it)
                if s.has(3):
                    dve.wait_ge(pw_done, b - 2)
                    dve.bn_stats(bn2[:, 0, :], pw_ps[:, 0:BLK])
                    chain.link(dve.bn_stats(bn2[:, 1, :], pw_ps[:, BLK:TO]))
                    average(1, bn2[:, :, :]).then_inc(stat2, 1)
                if s.has(0):
                    for blk in range(2):
                        stats(blk)
                for it in s.items:
                    if it[0] != KEPT:
                        low_part(*it)
                if s.has(0):
                    for blk in range(2, NBLK):
                        last = stats(blk)
                    chain.link(last)
                    average(0, bn1[:, :, :]).then_inc(stat1, 1)


def phase_b(nc, st, sb, h0, h1, split_dram, wqk_hi, wqk_lo, wv_hi, wv_lo, ident, rot,
            mask_bf, ident_bf, u_exp, u_neg, u_vo, half_neg):
    def buf(name, shape, dt):
        return sb(name, shape, dt, st)

    def psum(name, shape):
        return st.enter_context(nc.psum_tensor(name, shape, F32))

    def sem(name):
        return st.enter_context(nc.semaphore(name))

    NH = GB * 2
    wo_hi = buf("wo_hi", [P, 4 * PIECE], F16)
    wo_lo = buf("wo_lo", [P, 4 * PIECE], F16)
    h_ln = buf("h_ln", [P, GB, E], F32)
    h_res = buf("h_res", [P, GB, E], F32)
    xn = buf("xn", [P, GB, E], F32)
    xt_hi = buf("xt_hi", [P, KC, GT], F16)
    xt_lo = buf("xt_lo", [P, KC, GT], F16)
    v_hi = buf("v_hi", [P, GB, E], F16)
    v_lo = buf("v_lo", [P, GB, E], F16)
    qk32 = buf("qk32", [P, 2 * GT], F32)
    qk_hi = [buf(f"qk_hi{i}", [P, 2 * GT], F16) for i in range(2)]
    qk_lo = [buf(f"qk_lo{i}", [P, 2 * GT], F16) for i in range(2)]
    prob = buf("prob", [P, NH, P], F32)
    pn = buf("pn", [P, NH, P], F32)
    pt_hi = [buf(f"pt_hi{i}", [P, NH, P], F16) for i in range(2)]
    pt_lo = [buf(f"pt_lo{i}", [P, NH, P], F16) for i in range(2)]
    o_hi = buf("o_hi", [P, PAIRS, GT], F16)
    o_lo = buf("o_lo", [P, PAIRS, GT], F16)
    mx = buf("mx", [P, NH], F32)
    nb = buf("nb", [P, NH], F32)
    rsum = buf("rsum", [P, NH], F32)
    rinv = buf("rinv", [P, NH], F32)
    bn = buf("bnb", [P, GB, 2, 6], F32)
    mvb = buf("mvb", [P, GB, 2], F32)
    rstd = buf("rstdb", [P, GB], F32)

    qk_ps = [psum(f"qk_ps{i}", [P, 2 * GT]) for i in range(2)]
    out_ps = [psum(f"out_ps{i}", [P, BLK]) for i in range(2)]
    s_ps = psum("s_ps", [P, 2, BLK])
    t_ps = psum("t_ps", [P, BLK])
    o_ps = psum("o_ps", [P, BLK])

    wo_in = sem("b_wo_in")
    ln_in = sem("b_ln_in")
    res_in = sem("b_res_in")
    var_made = sem("b_var_made")
    rstd_made = sem("b_rstd_made")
    normed = sem("b_normed")
    xt_ps = sem("b_xt_ps")
    xt_high = sem("b_xt_high")
    xt_low = sem("b_xt_low")
    v_ps = sem("b_v_ps")
    v_high = sem("b_v_high")
    v_low = sem("b_v_low")
    wo_ps = sem("b_wo_ps")
    added = sem("b_added")
    qk_made = sem("b_qk_made")
    rotated = sem("b_rotated")
    qk_high = sem("b_qk_high")
    qk_low = sem("b_qk_low")
    scores = sem("b_scores")
    bias_made = sem("b_bias_made")
    exp_made = sem("b_exp_made")
    inverted = sem("b_inverted")
    divided = sem("b_divided")
    pt_ps = sem("b_pt_ps")
    pt_high = sem("b_pt_high")
    pt_low = sem("b_pt_low")
    o_made = sem("b_o_made")
    o_high = sem("b_o_high")
    o_low = sem("b_o_low")
    stored = sem("b_stored")
    chain_v = sem("b_chain_v")

    def groups(eng):
        yield 0, True
        with eng.Fori(1, NG - 1) as g:
            yield g, True
        yield NG - 1, False

    WIDE = GB * 2

    with nc.Block("phase_b") as block:

        @block.sync
        def _(sp):
            def load(dst, g, signal):
                sp.dma_start(dst[:, :, :], h0[bass.ds(g * GB, GB)].rearrange("b p e -> p b e")).then_inc(signal, 16)

            load(h_ln, 0, ln_in)
            for n in range(4):
                for part, dst in enumerate((wo_hi, wo_lo)):
                    sp.dma_start(dst[:, n * PIECE:(n + 1) * PIECE], split_dram[n, part]).then_inc(wo_in, 16)
            for g, more in groups(sp):
                after(sp, stored, g * 16 * GB)
                load(h_res, g, res_in)
                if more:
                    sp.wait_ge(normed, (g + 1) * GB)
                    load(h_ln, g + 1, ln_in)
                for b in range(GB):
                    sp.wait_ge(added, g * WIDE + (b + 1) * 2)
                    sp.dma_start(h1[g * GB + b], h_res[:, b, :]).then_inc(stored, 16)
            sp.wait_ge(stored, 16 * B)

        @block.gpsimd
        def _(pool):
            def root(g):
                pool.wait_ge(var_made, g + 1)
                pool.tensor_tensor(out=rstd[:, :], in0=mvb[:, :, 1], in1=half_neg[:, 0:GB],
                                   op=ALU.pow).then_inc(rstd_made, 1)
                pool.wait_ge(rstd_made, g + 1)

            root(0)
            for g, more in groups(pool):
                for j in range(PAIRS):
                    n = g * PAIRS + j
                    pool.wait_ge(inverted, n + 1)
                    after(pool, pt_ps, n)
                    pool.tensor_tensor(out=pn[:, :, :], in0=prob[:, :, :],
                                       in1=rinv[:, :].unsqueeze(2).to_broadcast([P, NH, P]),
                                       op=ALU.mult).then_inc(divided, 1)
                    pool.wait_ge(divided, n + 1)
                    if j == 2 and more:
                        root(g + 1)

        @block.scalar
        def _(act):
            def high(dst, src):
                return act.activation(dst, src, ACT.Copy)

            def xt_part(g, f):
                act.wait_ge(xt_ps, g * WIDE + (f + 1))
                b, half = f // 2, f % 2
                high(xt_hi[:, half * 4:half * 4 + 4, b * P:(b + 1) * P],
                     qk_ps[f % 2][:, :].rearrange("p (k t) -> p k t", k=4)).then_inc(xt_high, 1)

            def v_parts(g):
                for f in range(WIDE):
                    act.wait_ge(v_ps, g * WIDE + (f + 1))
                    b, half = f // 2, f % 2
                    high(v_hi[:, b, half * BLK:(half + 1) * BLK], qk_ps[f % 2][:, :]).then_inc(v_high, 1)

            def qk_part(g, j):
                act.wait_ge(rotated, g * PAIRS + (j + 1))
                after(act, scores, g * PAIRS + (j - 1))
                high(qk_hi[j % 2][:, :], qk32[:, :]).then_inc(qk_high, 1)

            def exps(g, j):
                act.wait_ge(bias_made, g * PAIRS + (j + 1))
                after(act, divided, g * PAIRS + j)
                for hh in range(2):
                    for b in range(GB):
                        c = hh * GB + b
                        act.activation(prob[:, c, :], s_ps[:, hh, b * P:(b + 1) * P], ACT.Exp,
                                       bias=nb[:, c:c + 1], scale=u_exp,
                                       accum_out=rsum[:, c:c + 1]).then_inc(exp_made, 1)

            def pt_part(g, j):
                act.wait_ge(pt_ps, g * PAIRS + (j + 1))
                after(act, o_made, g * PAIRS + (j - 1))
                high(pt_hi[j % 2][:, :, :].rearrange("p a t -> p (a t)"), t_ps[:, :]).then_inc(pt_high, 1)

            def o_part(g, j):
                act.wait_ge(o_made, g * PAIRS + (j + 1))
                high(o_hi[:, j, :], o_ps[:, 0:GT]).then_inc(o_high, 1)

            for f in range(WIDE):
                xt_part(0, f)
            v_parts(0)
            for g, more in groups(act):
                qk_part(g, 0)
                for j in range(PAIRS):
                    if j + 1 < PAIRS:
                        qk_part(g, j + 1)
                    elif more:
                        xt_part(g + 1, 0)
                    exps(g, j)
                    if j >= 1:
                        pt_part(g, j - 1)
                    if j >= 2:
                        o_part(g, j - 2)
                pt_part(g, PAIRS - 1)
                o_part(g, PAIRS - 2)
                if more:
                    xt_part(g + 1, 1)
                o_part(g, PAIRS - 1)
                if more:
                    xt_part(g + 1, 2)
                    xt_part(g + 1, 3)
                    v_parts(g + 1)

        @block.tensor
        def _(pe):
            def products(out, pairs, start=True, stop=True):
                steps = [(l[0], r[0]) for l, r in pairs] + [(l[0], r[1]) for l, r in pairs] \
                    + [(l[1], r[0]) for l, r in pairs]
                n = len(pairs)
                steps = [steps[c + part * n] for c in range(n) for part in range(3)]
                for i, (l, r) in enumerate(steps):
                    last = pe.matmul(out, l, r, start=start and i == 0, stop=stop and i == len(steps) - 1)
                return last

            def parts(hi, lo, *index):
                return hi[index], lo[index]

            ALL = slice(None)

            def transpose_xn(g, f):
                b, half = f // 2, f % 2
                pe.wait_ge(normed, g * GB + (b + 1))
                if f < 2:
                    after(pe, rotated, g * PAIRS - (1 - f))
                else:
                    pe.wait_ge(xt_low, g * WIDE + (f - 1))
                for k in range(4):
                    c = half * 4 + k
                    last = pe.transpose(qk_ps[f % 2][:, k * P:(k + 1) * P], xn[:, b, c * P:(c + 1) * P], ident)
                last.then_inc(xt_ps, 1)

            def project_v(g):
                pe.wait_ge(xt_low, (g + 1) * WIDE)
                for f in range(WIDE):
                    b, half = f // 2, f % 2
                    if f >= 2:
                        pe.wait_ge(v_low, g * WIDE + (f - 1))
                    products(qk_ps[f % 2][:, :], [
                        (parts(xt_hi, xt_lo, ALL, k, slice(b * P, (b + 1) * P)),
                         parts(wv_hi, wv_lo, ALL, slice(k * E + half * BLK, k * E + (half + 1) * BLK)))
                        for k in range(KC)]).then_inc(v_ps, 1)

            def project_qk(g, j):
                if j < 2:
                    pe.wait_ge(v_low, (g + 1) * WIDE - (1 - j))
                else:
                    pe.wait_ge(rotated, g * PAIRS + (j - 1))
                for which in range(2):
                    last = products(qk_ps[j % 2][:, which * GT:(which + 1) * GT], [
                        (parts(wqk_hi, wqk_lo, ALL, slice((which * KC + k) * E + j * P, (which * KC + k) * E + (j + 1) * P)),
                         parts(xt_hi, xt_lo, ALL, k, ALL))
                        for k in range(KC)])
                last.then_inc(qk_made, 1)

            def score(g, j):
                pe.wait_ge(qk_low, g * PAIRS + (j + 1))
                after(pe, exp_made, (g * PAIRS + j) * NH)
                for hh in range(2):
                    pe.matmul(s_ps[:, hh, 0:GT], ident_bf[:, :],
                              mask_bf[:, :].unsqueeze(1).to_broadcast([P, GB, P]), start=True, stop=False)
                    rows = slice(hh * HD, (hh + 1) * HD)
                    for b in range(GB):
                        q = parts(qk_hi[j % 2], qk_lo[j % 2], rows, slice(b * P, (b + 1) * P))
                        k = parts(qk_hi[j % 2], qk_lo[j % 2], rows, slice(GT + b * P, GT + (b + 1) * P))
                        last = products(s_ps[:, hh, b * P:(b + 1) * P], [(q, k)], start=False,
                                        stop=(b == GB - 1))
                last.then_inc(scores, 1)

            def transpose_p(g, j):
                pe.wait_ge(divided, g * PAIRS + (j + 1))
                after(pe, pt_low, g * PAIRS + j)
                for c in range(NH):
                    last = pe.transpose(t_ps[:, c * P:(c + 1) * P], pn[:, c, :], ident)
                last.then_inc(pt_ps, 1)

            def weigh_v(g, j):
                pe.wait_ge(pt_low, g * PAIRS + (j + 1))
                if j == 0:
                    pe.wait_ge(v_low, (g + 1) * WIDE)
                after(pe, o_low, g * PAIRS + j)
                for hh in range(2):
                    for b in range(GB):
                        head = (2 * j + hh) * HD
                        last = products(o_ps[hh * HD:(hh + 1) * HD, b * P:(b + 1) * P], [
                            (parts(v_hi, v_lo, ALL, b, slice(head, head + HD)),
                             parts(pt_hi[j % 2], pt_lo[j % 2], ALL, hh * GB + b, ALL))])
                last.then_inc(o_made, 1)

            def project_out(g, f, first, last):
                b, half = f // 2, f % 2
                if first == 0:
                    after(pe, added, g * WIDE + (f - 1))
                pe.wait_ge(o_low, g * PAIRS + last)
                done = products(out_ps[f % 2][:, :], [
                    (parts(o_hi, o_lo, ALL, j, slice(b * P, (b + 1) * P)),
                     parts(wo_hi, wo_lo, ALL, slice(j * E + half * BLK, j * E + (half + 1) * BLK)))
                    for j in range(first, last)], start=first == 0, stop=last == PAIRS)
                if last == PAIRS:
                    done.then_inc(wo_ps, 1)

            for f in range(WIDE):
                transpose_xn(0, f)
            project_v(0)
            pe.wait_ge(wo_in, 16 * 8)
            for g, more in groups(pe):
                project_qk(g, 0)
                for j in range(PAIRS):
                    if j + 1 < PAIRS:
                        project_qk(g, j + 1)
                    else:
                        if more:
                            transpose_xn(g + 1, 0)
                        project_out(g, 0, 0, 4)
                    score(g, j)
                    if j >= 1:
                        transpose_p(g, j - 1)
                    if j >= 2:
                        weigh_v(g, j - 2)
                project_out(g, 1, 0, 4)
                transpose_p(g, PAIRS - 1)
                weigh_v(g, PAIRS - 2)
                project_out(g, 0, 4, 6)
                project_out(g, 1, 4, 6)
                if more:
                    transpose_xn(g + 1, 1)
                weigh_v(g, PAIRS - 1)
                project_out(g, 0, 6, 7)
                project_out(g, 1, 6, 7)
                if more:
                    transpose_xn(g + 1, 2)
                    transpose_xn(g + 1, 3)
                project_out(g, 0, 7, 8)
                project_out(g, 1, 7, 8)
                project_out(g, 2, 0, PAIRS)
                project_out(g, 3, 0, PAIRS)
                if more:
                    project_v(g + 1)

        @block.vector
        def _(dve):
            chain = Chain(dve, chain_v)

            def statistics(g):
                dve.wait_ge(ln_in, (g + 1) * 16)
                for b in range(GB):
                    for half in range(2):
                        last = dve.bn_stats(bn[:, b, half, :], h_ln[:, b, half * BLK:(half + 1) * BLK])
                chain.link(last)
                for b in range(GB):
                    last = dve.bn_aggr(mvb[:, b, :], bn[:, b, :, :].rearrange("p a s -> p (a s)"))
                chain.link(last)
                dve.tensor_scalar(out=mvb[:, :, 1], in0=mvb[:, :, 1], scalar1=EPS, scalar2=None,
                                  op0=ALU.add).then_inc(var_made, 1)

            def norm(g):
                dve.wait_ge(rstd_made, g + 1)
                after(dve, xt_ps, g * WIDE)
                for b in range(GB):
                    dve.tensor_scalar(out=xn[:, b, :], in0=h_ln[:, b, :], scalar1=mvb[:, b, 0:1],
                                      scalar2=rstd[:, b:b + 1], op0=ALU.subtract,
                                      op1=ALU.mult).then_inc(normed, 1)

            def low(dst, src, hi):
                return dve.tensor_tensor(out=dst, in0=src, in1=hi, op=ALU.subtract)

            def xt_part(g, f):
                dve.wait_ge(xt_high, g * WIDE + (f + 1))
                b, half = f // 2, f % 2
                at = (slice(None), slice(half * 4, half * 4 + 4), slice(b * P, (b + 1) * P))
                low(xt_lo[at], qk_ps[f % 2][:, :].rearrange("p (k t) -> p k t", k=4),
                    xt_hi[at]).then_inc(xt_low, 1)

            def v_parts(g):
                for f in range(WIDE):
                    dve.wait_ge(v_high, g * WIDE + (f + 1))
                    b, half = f // 2, f % 2
                    at = (slice(None), b, slice(half * BLK, (half + 1) * BLK))
                    low(v_lo[at], qk_ps[f % 2][:, :], v_hi[at]).then_inc(v_low, 1)

            def rotate(g, j):
                dve.wait_ge(qk_made, g * PAIRS + (j + 1))
                after(dve, qk_low, g * PAIRS + j)
                dve.tensor_tensor(out=qk32[:, :].rearrange("p (a t) -> p a t", t=P),
                                  in0=qk_ps[j % 2][:, :].rearrange("p (a t) -> p a t", t=P),
                                  in1=rot.unsqueeze(1).to_broadcast([P, 2 * GB, P]),
                                  op=ALU.mult).then_inc(rotated, 1)
                dve.wait_ge(qk_high, g * PAIRS + (j + 1))
                low(qk_lo[j % 2][:, :], qk32[:, :], qk_hi[j % 2][:, :]).then_inc(qk_low, 1)

            def maxima(g, j):
                dve.wait_ge(scores, g * PAIRS + (j + 1))
                chain.link(dve.tensor_reduce(out=mx[:, :].rearrange("p (h b) -> p h b", h=2),
                                             in_=s_ps[:, :, 0:GT].rearrange("p h (b t) -> p h b t", b=GB),
                                             axis=AX_X, op=ALU.max))
                dve.tensor_scalar(out=nb[:, :], in0=mx[:, :], scalar1=u_neg, scalar2=None,
                                  op0=ALU.mult).then_inc(bias_made, 1)

            def invert(g, j):
                dve.wait_ge(exp_made, (g * PAIRS + (j + 1)) * NH)
                after(dve, divided, g * PAIRS + j)
                dve.reciprocal(rinv[:, :], rsum[:, :]).then_inc(inverted, 1)

            def pt_part(g, j):
                dve.wait_ge(pt_high, g * PAIRS + (j + 1))
                low(pt_lo[j % 2][:, :, :].rearrange("p a t -> p (a t)"), t_ps[:, :],
                    pt_hi[j % 2][:, :, :].rearrange("p a t -> p (a t)")).then_inc(pt_low, 1)

            def o_part(g, j):
                dve.wait_ge(o_high, g * PAIRS + (j + 1))
                low(o_lo[:, j, :], o_ps[:, 0:GT], o_hi[:, j, :]).then_inc(o_low, 1)

            def residual(g):
                dve.wait_ge(res_in, (g + 1) * 16)
                for f in range(WIDE):
                    dve.wait_ge(wo_ps, g * WIDE + (f + 1))
                    b, half = f // 2, f % 2
                    at = h_res[:, b, half * BLK:(half + 1) * BLK]
                    dve.scalar_tensor_tensor(out=at, in0=out_ps[f % 2][:, :], scalar=u_vo, in1=at,
                                             op0=ALU.mult, op1=ALU.add).then_inc(added, 1)

            chain.begin()
            statistics(0)
            norm(0)
            for f in range(WIDE):
                xt_part(0, f)
            v_parts(0)
            for g, more in groups(dve):
                chain.begin()
                rotate(g, 0)
                for j in range(PAIRS):
                    if j + 1 < PAIRS:
                        rotate(g, j + 1)
                    elif more:
                        xt_part(g + 1, 0)
                    maxima(g, j)
                    if j == 1 and more:
                        statistics(g + 1)
                    if j >= 1:
                        pt_part(g, j - 1)
                    if j >= 2:
                        o_part(g, j - 2)
                    invert(g, j)
                    if j == 4 and more:
                        norm(g + 1)
                pt_part(g, PAIRS - 1)
                o_part(g, PAIRS - 2)
                if more:
                    xt_part(g + 1, 1)
                o_part(g, PAIRS - 1)
                if more:
                    xt_part(g + 1, 2)
                    xt_part(g + 1, 3)
                residual(g)
                if more:
                    v_parts(g + 1)


def phase_c(nc, st, sb, h1, out, split_dram, ident, u_ab, half_neg, g_hi, g_lo, g_inv):
    def buf(name, shape, dt):
        return sb(name, shape, dt, st)

    def psum(name, shape):
        return st.enter_context(nc.psum_tensor(name, shape, F32))

    def sem(name):
        return st.enter_context(nc.semaphore(name))

    ZC = BOT // P
    h = buf("h_all", [P, B, E], F32)
    a_hi = buf("a_hi", [P, 2 * PIECE], F16)
    a_lo = buf("a_lo", [P, 2 * PIECE], F16)
    b_hi = buf("b_hi", [P, 2 * PIECE], F16)
    b_lo = buf("b_lo", [P, 2 * PIECE], F16)
    xn = buf("xnc", [P, E], F32)
    xt_hi = buf("xtc_hi", [P, KC, P], F16)
    xt_lo = buf("xtc_lo", [P, KC, P], F16)
    sc = buf("sc", [P, NE], F32)
    left8 = buf("left8", [P, NE], F32)
    left16 = buf("left16", [P, NE], F32)
    top = buf("top", [P, 2, 8], F32)
    neg_top = buf("neg_top", [P, 1], F32)
    ex = buf("ex", [P, NE], F32)
    gate = buf("gate", [P, NE], F32)
    gsum = buf("gsum", [P, 1], F32)
    ginv = buf("ginv", [P, 1], F32)
    zg = buf("zg", [P, BOT], F32)
    zt_hi = buf("zt_hi", [P, ZC, P], F16)
    zt_lo = buf("zt_lo", [P, ZC, P], F16)
    res = [buf(f"res{i}", [P, E], F32) for i in range(1)][0]
    bn = buf("bnc", [P, 2, 6], F32)
    mvc = buf("mvc", [P, 2], F32)
    rstd = buf("rstdc", [P, 1], F32)

    xt_bank = [psum(f"xt_bank{i}", [P, BLK]) for i in range(2)]
    out_bank = [psum(f"out_bank{i}", [P, BLK]) for i in range(2)]
    z_bank = psum("z_bank", [P, BOT])
    zt_bank = psum("zt_bank", [P, BOT])
    sc_bank = psum("sc_bank", [P, NE])

    ab_in = sem("c_ab_in")
    h_in = sem("c_h_in")
    var_made = sem("c_var_made")
    rstd_made = sem("c_rstd_made")
    normed = sem("c_normed")
    xt_ps = sem("c_xt_ps")
    xt_high = sem("c_xt_high")
    xt_low = sem("c_xt_low")
    scored = sem("c_scored")
    z_made = sem("c_z_made")
    top_made = sem("c_top_made")
    exp_made = sem("c_exp_made")
    gated = sem("c_gated")
    zt_ps = sem("c_zt_ps")
    zt_high = sem("c_zt_high")
    zt_low = sem("c_zt_low")
    out_ps = sem("c_out_ps")
    added = sem("c_added")
    stored = sem("c_stored")
    chain_v = sem("c_chain_v")

    def steps(eng):
        def has(b):
            return lambda lag: not isinstance(b, int) or 0 <= b - lag < B

        for b in (0, 1):
            yield b, has(b)
        with eng.Fori(2, B - 2) as b:
            yield b, has(b)
        for b in (B - 2, B - 1, B):
            yield b, has(b)

    def products(pe, bank, pairs):
        for c, ((l_hi, l_lo), (r_hi, r_lo)) in enumerate(pairs):
            pe.matmul(bank, l_hi, r_hi, start=(c == 0), stop=False)
            pe.matmul(bank, l_hi, r_lo, start=False, stop=False)
            last = pe.matmul(bank, l_lo, r_hi, start=False, stop=(c == len(pairs) - 1))
        return last

    with nc.Block("phase_c") as block:

        @block.sync
        def _(sp):
            sp.dma_start(h[:, 0, :], h1[0]).then_inc(h_in, 16)
            for n in range(2):
                for row, parts in ((4, (a_hi, a_lo)), (6, (b_hi, b_lo))):
                    for part, dst in enumerate(parts):
                        sp.dma_start(dst[:, n * PIECE:(n + 1) * PIECE],
                                     split_dram[row + n, part]).then_inc(ab_in, 16)
            with sp.Fori(1, B) as b:
                sp.wait_ge(h_in, b * 16)
                sp.dma_start(h[:, b, :], h1[b]).then_inc(h_in, 16)
            for b, has in steps(sp):
                if has(1):
                    sp.wait_ge(added, b * 2)
                    sp.dma_start(out[b - 1], res[:, :]).then_inc(stored, 16)
            sp.wait_ge(stored, 16 * B)

        @block.gpsimd
        def _(pool):
            with pool.Fori(0, B) as b:
                pool.wait_ge(var_made, b + 1)
                pool.tensor_tensor(out=rstd[:, :], in0=mvc[:, 1:2], in1=half_neg[:, 0:1],
                                   op=ALU.pow).then_inc(rstd_made, 1)

        @block.scalar
        def _(act):
            def xt_parts(b):
                for f in range(2):
                    act.wait_ge(xt_ps, b * 2 + (f + 1))
                    act.activation(xt_hi[:, f * 4:f * 4 + 4, :],
                                   xt_bank[f][:, :].rearrange("p (k t) -> p k t", k=4),
                                   ACT.Copy).then_inc(xt_high, 1)

            xt_parts(0)
            for b, has in steps(act):
                if has(0):
                    act.wait_ge(top_made, b + 1)
                    act.activation(ex[:, :], sc[:, :], ACT.Exp, bias=neg_top[:, :]).then_inc(exp_made, 1)
                if has(-1):
                    xt_parts(b + 1)
                if has(0):
                    act.wait_ge(zt_ps, b + 1)
                    act.activation(zt_hi[:, :, :].rearrange("p k t -> p (k t)"), zt_bank[:, :],
                                   ACT.Copy).then_inc(zt_high, 1)

        @block.tensor
        def _(pe):
            def transpose_xn(b):
                pe.wait_ge(normed, b + 1)
                for f in range(2):
                    after(pe, xt_low, (b - 1) * 2 + (f + 1))
                    for k in range(4):
                        c = f * 4 + k
                        last = pe.transpose(xt_bank[f][:, k * P:(k + 1) * P], xn[:, c * P:(c + 1) * P], ident)
                    last.then_inc(xt_ps, 1)

            transpose_xn(0)
            pe.wait_ge(ab_in, 16 * 8)
            for b, has in steps(pe):
                x_parts = [(xt_hi[:, k, :], xt_lo[:, k, :]) for k in range(KC)]
                if has(0):
                    pe.wait_ge(xt_low, (b + 1) * 2)
                    after(pe, top_made, b)
                    products(pe, sc_bank[:, :], [
                        (x_parts[k], (g_hi[:, k * NE:(k + 1) * NE], g_lo[:, k * NE:(k + 1) * NE]))
                        for k in range(KC)]).then_inc(scored, 1)
                    after(pe, gated, b)
                    products(pe, z_bank[:, :], [
                        (x_parts[k], (a_hi[:, k * BOT:(k + 1) * BOT], a_lo[:, k * BOT:(k + 1) * BOT]))
                        for k in range(KC)]).then_inc(z_made, 1)
                if has(-1):
                    transpose_xn(b + 1)
                if has(1):
                    pe.wait_ge(zt_low, b)
                    for half in range(2):
                        after(pe, added, (b - 2) * 2 + (half + 1))
                        products(pe, out_bank[half][:, :], [
                            ((zt_hi[:, k, :], zt_lo[:, k, :]),
                             tuple(w[:, k * E + half * BLK:k * E + (half + 1) * BLK] for w in (b_hi, b_lo)))
                            for k in range(ZC)]).then_inc(out_ps, 1)
                if has(0):
                    pe.wait_ge(gated, b + 1)
                    for k in range(ZC):
                        last = pe.transpose(zt_bank[:, k * P:(k + 1) * P], zg[:, k * P:(k + 1) * P], ident)
                    last.then_inc(zt_ps, 1)

        @block.vector
        def _(dve):
            chain = Chain(dve, chain_v)

            def norm(b):
                dve.wait_ge(h_in, (b + 1) * 16)
                at = [h[:, bass.ds(b, 1), half * BLK:(half + 1) * BLK].rearrange("p a e -> p (a e)")
                      for half in range(2)]
                dve.bn_stats(bn[:, 0, :], at[0])
                chain.link(dve.bn_stats(bn[:, 1, :], at[1]))
                chain.link(dve.bn_aggr(mvc[:, :], bn[:, :, :].rearrange("p a s -> p (a s)")))
                chain.link(dve.tensor_scalar(out=mvc[:, 1:2], in0=mvc[:, 1:2], scalar1=EPS, scalar2=None,
                                             op0=ALU.add))
                dve.sem_inc(var_made, 1)
                dve.wait_ge(rstd_made, b + 1)
                after(dve, xt_ps, b * 2)
                dve.tensor_scalar(out=xn[:, :], in0=h[:, bass.ds(b, 1), :].rearrange("p a e -> p (a e)"),
                                  scalar1=mvc[:, 0:1], scalar2=rstd[:, :], op0=ALU.subtract,
                                  op1=ALU.mult).then_inc(normed, 1)

            def xt_parts(b):
                for f in range(2):
                    dve.wait_ge(xt_high, b * 2 + (f + 1))
                    dve.tensor_tensor(out=xt_lo[:, f * 4:f * 4 + 4, :],
                                      in0=xt_bank[f][:, :].rearrange("p (k t) -> p k t", k=4),
                                      in1=xt_hi[:, f * 4:f * 4 + 4, :], op=ALU.subtract).then_inc(xt_low, 1)

            chain.begin()
            norm(0)
            xt_parts(0)
            chain.begin()
            norm(1)
            for b, has in steps(dve):
                chain.begin()
                if has(0):
                    dve.wait_ge(scored, b + 1)
                    chain.link(dve.tensor_scalar(out=sc[:, :], in0=sc_bank[:, :], scalar1=g_inv, scalar2=None,
                                                 op0=ALU.mult))
                    chain.link(dve.max(out=top[:, 0, :], in_=sc[:, :]))
                    dve.tensor_scalar(out=neg_top[:, :], in0=top[:, 0, 0:1], scalar1=-1.0, scalar2=None,
                                      op0=ALU.mult).then_inc(top_made, 1)
                    chain.link(dve.match_replace(out=left8[:, :], in_to_replace=top[:, 0, :],
                                                 in_values=sc[:, :], imm_value=MASKED))
                    chain.link(dve.max(out=top[:, 1, :], in_=left8[:, :]))
                    chain.link(dve.match_replace(out=left16[:, :], in_to_replace=top[:, 1, :],
                                                 in_values=left8[:, :], imm_value=MASKED))
                    dve.wait_ge(exp_made, b + 1)
                    chain.link(dve.scalar_tensor_tensor(out=ex[:, :], in0=left16[:, :], scalar=MASKED / 2,
                                                        in1=ex[:, :], op0=ALU.is_le, op1=ALU.mult,
                                                        accum_out=gsum[:, :]))
                    chain.link(dve.reciprocal(ginv[:, :], gsum[:, :]))
                    chain.link(dve.tensor_scalar(out=gate[:, :], in0=ex[:, :], scalar1=ginv[:, :], scalar2=None,
                                                 op0=ALU.mult))
                    dve.wait_ge(z_made, b + 1)
                    after(dve, zt_ps, b)
                    dve.tensor_tensor(out=zg[:, :].rearrange("p (n r) -> p n r", r=RANK),
                                      in0=z_bank[:, :].rearrange("p (n r) -> p n r", r=RANK),
                                      in1=gate[:, :].unsqueeze(2).to_broadcast([P, NE, RANK]),
                                      op=ALU.mult).then_inc(gated, 1)
                if has(-1):
                    xt_parts(b + 1)
                if has(-2):
                    norm(b + 2)
                if has(1):
                    for half in range(2):
                        c = slice(half * BLK, (half + 1) * BLK)
                        dve.wait_ge(out_ps, (b - 1) * 2 + (half + 1))
                        after(dve, stored, (b - 1) * 16)
                        dve.scalar_tensor_tensor(
                            out=res[:, c], in0=out_bank[half][:, :], scalar=u_ab,
                            in1=h[:, bass.ds(b - 1, 1), c].rearrange("p a e -> p (a e)"),
                            op0=ALU.mult, op1=ALU.add).then_inc(added, 1)
                if has(0):
                    dve.wait_ge(zt_high, b + 1)
                    dve.tensor_tensor(out=zt_lo[:, :, :].rearrange("p k t -> p (k t)"), in0=zt_bank[:, :],
                                      in1=zt_hi[:, :, :].rearrange("p k t -> p (k t)"),
                                      op=ALU.subtract).then_inc(zt_low, 1)
def audio_tower_kernel(nc, x, conv_w, par, pw_w, w_all, wr, keys_t, const, out):
    h0 = nc.dram_tensor("h0", (B, P, E), F32, kind="Internal").ap()
    h1 = nc.dram_tensor("h1", (B, P, E), F32, kind="Internal").ap()
    split_dram = nc.dram_tensor("split_dram", (8, 2, P, PIECE), F16, kind="Internal").ap()
    with ExitStack() as whole:
        def sb(name, shape, dt, stack=whole):
            return stack.enter_context(nc.sbuf_tensor(name, shape, dt))

        cst = sb("cst", [P, 4 * P], F32)
        ident, rot, ones, mask32 = (cst[:, i * P:(i + 1) * P] for i in range(4))
        mask_bf = sb("mask_bf", [P, P], BF16)
        ident_bf = sb("ident_bf", [P, P], BF16)
        scl = sb("scl", [P, 8], F32)
        inv = sb("inv", [P, 8], F32)
        unscale = sb("unscale", [P, 4], F32)
        half_neg = sb("half_neg", [P, 8], F32)
        g_hi = sb("g_hi", [P, KC * NE], F16)
        g_lo = sb("g_lo", [P, KC * NE], F16)
        g_inv = inv[:, 6:7]
        u_exp, u_neg, u_vo, u_ab = (unscale[:, i:i + 1] for i in range(4))

        with ExitStack() as dense:
            wqk_hi = sb("wqk_hi", [P, 8 * PIECE], F16, dense)
            wqk_lo = sb("wqk_lo", [P, 8 * PIECE], F16, dense)
            wv_hi = sb("wv_hi", [P, 4 * PIECE], F16, dense)
            wv_lo = sb("wv_lo", [P, 4 * PIECE], F16, dense)
            with ExitStack() as s:
                phase_a(nc, s, sb, x, conv_w, par, pw_w, w_all, wr, keys_t, const, h0, split_dram,
                        wqk_hi, wqk_lo, wv_hi, wv_lo, cst, ident, ones, mask32, mask_bf, ident_bf,
                        scl, inv, unscale, half_neg, g_hi, g_lo)
            with ExitStack() as s:
                phase_b(nc, s, sb, h0, h1, split_dram, wqk_hi, wqk_lo, wv_hi, wv_lo, ident, rot,
                        mask_bf, ident_bf, u_exp, u_neg, u_vo, half_neg)
        with ExitStack() as s:
            phase_c(nc, s, sb, h1, out, split_dram, ident, u_ab, half_neg, g_hi, g_lo, g_inv)


def constants():
    import numpy as np

    j = np.arange(P) % HD
    inv_freq = (1.0 / 10000.0 ** (np.arange(0, HD, 2, dtype=np.float32) / np.float32(HD))).astype(np.float32)
    t = np.arange(P, dtype=np.float32)
    ang = (inv_freq[j % (HD // 2)][:, None] * t[None, :]).astype(np.float32).astype(np.float64)
    rot = np.cos(ang) + np.where(j < HD // 2, 1.0, -1.0)[:, None] * np.sin(ang)
    mask = np.where(np.arange(P)[None, :] > np.arange(P)[:, None], MASKED, 0.0)
    return np.concatenate([np.eye(P), rot, np.full((P, P), 1.0 / P), mask], 1).astype(np.float32)


def laid_out(inputs):
    import numpy as np

    i = {k: np.asarray(v) for k, v in inputs.items()}
    pieces = [i["L0_attn_" + w].reshape(KC, P, E) for w in ("Wq", "Wk", "Wv", "Wo")]
    pieces = [w.reshape(4, 2, P, E).transpose(0, 2, 1, 3).reshape(4, P, PIECE) for w in pieces]
    a = i["L0_ffn_A_w"].T.reshape(2, 4, P, BOT).transpose(0, 2, 1, 3).reshape(2, P, PIECE)
    b = i["L0_ffn_B_w"].T.reshape(2, 2, P, E).transpose(0, 2, 1, 3).reshape(2, P, PIECE)
    cols = [i["L0_tok_" + k][:, None] for k in ("dw_b", "gn1_w", "gn1_b", "gn2_w", "gn2_b")]
    arrays = {
        "x": i["x"],
        "conv_w": i["L0_tok_conv_in_w"].transpose(1, 2, 0).reshape(CIN, TAPS * H),
        "par": np.concatenate([i["L0_tok_dw_w"].reshape(H, DW)] + cols, 1),
        "pw_w": i["L0_tok_pw_w"].reshape(H, H).T,
        "w_all": np.concatenate(pieces + [a, b], 0),
        "wr": i["L0_ffn_Wq_w"],
        "keys_t": i["L0_ffn_keys"].T,
        "const": constants(),
    }
    return {k: np.ascontiguousarray(v) for k, v in arrays.items()}


def kernel(**inputs):
    import concourse.bacc as bacc
    from concourse.bass_utils import run_bass_kernel_spmd

    nc = bacc.Bacc("TRN2", target_bir_lowering=False, num_devices=1)
    arrays = laid_out(inputs)
    args = {n: nc.dram_tensor(n, a.shape, F32, kind="ExternalInput").ap() for n, a in arrays.items()}
    out = nc.dram_tensor("out", (B, P, E), F32, kind="ExternalOutput").ap()
    audio_tower_kernel(nc, out=out, **args)
    r = run_bass_kernel_spmd(nc, [arrays], core_ids=[0])
    return r.results[0]["out"]
```

```python
from contextlib import ExitStack

import concourse.bass as bass
from concourse import mybir

F32 = mybir.dt.float32
F32R = mybir.dt.float32r
F16 = mybir.dt.float16
BF16 = mybir.dt.bfloat16
I32 = mybir.dt.int32
ALU = mybir.AluOpType
ACT = mybir.ActivationFunctionType
AX_X = mybir.AxisListType.X

P = 128
B, CIN, T = 16, 64, 2048
H, TO = 128, 1024
TAPS, DW = 7, 5
PAD = 3
XW = T + 2 * PAD + 2
GW = T + 4
BLK = 512
NBLK = T // BLK
EPS = 1e-5
E = TO
KC = E // P
HEADS, HD = 16, 64
PAIRS = HEADS // 2
BOT = 512
NE, RANK, RD, TOPK = 64, 8, 16, 16
SCALING = 2.0
PIECE = 2048
NPIECE = 20
TENSOR_OF = [(0, 4), (4, 4), (8, 4), (12, 4), (16, 2), (18, 2)]
Q_, K_, V_, O_, A_, B_ = range(6)
MASKED = -3e38
GB = 2
GT = GB * P
NG = B // GB


def after(eng, sem, n):
    if not isinstance(n, int) or n > 0:
        eng.wait_ge(sem, n)


class Chain:

    def __init__(self, eng, sem):
        self.eng, self.sem, self.n = eng, sem, 0

    def begin(self):
        self.eng.sem_clear(self.sem)
        self.n = 0

    def link(self, ins):
        self.n += 1
        ins.then_inc(self.sem, 1)
        self.eng.wait_ge(self.sem, self.n)


class Step:

    def __init__(self, b, parity, i=0, per=0, items=()):
        self.b, self.parity, self.i, self.per, self.items = b, parity, i, per, items

    def has(self, lag):
        return not isinstance(self.b, int) or 0 <= self.b - lag < B

    def round(self, n):
        return n // 2 + self.i * (self.per // 2)


NORM, PAIRED, PLAIN, KEPT = "norm", "paired", "plain", "kept"
NORMED_IN = [range(0, 4), range(4, 8), range(8, 11), range(11, 14), range(14, 17), range(17, 20)]
RING = 8


def steps_of_phase_a(eng):
    for b in range(6):
        yield Step(b, b % 2, items=[(NORM, m, m, None) for m in NORMED_IN[b]])
    yield None
    with eng.Fori(0, 2) as i:
        for p in range(4):
            n = 2 * p
            kept, tensor = (12 + p, O_) if p < 2 else (16 + p - 2, i + A_)
            yield Step(i * 4 + (6 + p), p % 2, i, 8, [(PAIRED, n, i * 4 + p, i),
                                                      (KEPT, n + 1, i * 2 + kept, tensor)])
    for b in range(14, 20):
        piece = b - 14 + 8
        yield Step(b, b % 2, items=[(PLAIN, 8 + piece, piece, V_)] if b < 18 else [])


def token_moments(dve, chain, h, bn, mv):
    batches = h.shape[1]
    for b in range(batches):
        for half in range(2):
            last = dve.bn_stats(bn[:, b, half, :], h[:, b, half * BLK:(half + 1) * BLK])
    chain.link(last)
    for b in range(batches):
        last = dve.bn_aggr(mv[:, b, :], bn[:, b, :, :].rearrange("p a s -> p (a s)"))
    chain.link(last)
    return dve.tensor_scalar(out=mv[:, 0:batches, 1], in0=mv[:, 0:batches, 1], scalar1=EPS, scalar2=None,
                             op0=ALU.add)


def token_norm(dve, out, h, mv, rstd):
    return dve.tensor_scalar(out=out, in0=h, scalar1=mv[:, 0:1], scalar2=rstd, op0=ALU.subtract,
                             op1=ALU.mult)


def phase_a(nc, st, sb, x, token_w, par, w_all, router, const, h0, split_dram,
            wqk_hi, wqk_lo, wv_hi, wv_lo, cst, ident, ones, mask32, mask_bf, ident_bf,
            scl, inv, unscale, half_neg, g_hi, g_lo, h_ln, xn, tok, h_res, stored):
    def buf(name, shape, dt):
        return sb(name, shape, dt, st)

    def psum(name, shape):
        return st.enter_context(nc.psum_tensor(name, shape, F32))

    def sem(name):
        return st.enter_context(nc.semaphore(name))

    xs = buf("xs", [P, XW], F32)
    pair = [buf(f"pair{i}", [P, XW], F32R) for i in range(2)]
    split = [buf(f"split{i}", [P, XW], F32R) for i in range(2)]
    mid = [buf(f"mid{i}", [P, GW], F32) for i in range(2)]
    dwo = buf("dwo", [P, TO], F32)
    dw_hi = buf("dw_hi", [P, TO], F32R)
    dw_lo = buf("dw_lo", [P, TO], F32R)
    stage = [h_ln[:, :, :].rearrange("p b e -> p (b e)"), h_res[:, :, :].rearrange("p b e -> p (b e)")]
    plus_minus = xn[:, :, :].rearrange("p b e -> p (b e)")
    ring = [w[:, 2 * i * PIECE:2 * (i + 1) * PIECE].bitcast(F32) for w in (wqk_hi, wqk_lo) for i in range(4)]
    squares = plus_minus
    kept_out = [wv_lo[:, 2 * i * PIECE:2 * (i + 1) * PIECE].rearrange("p (t c) -> p t c", t=2) for i in range(2)]
    cw_dup = mid[0][:, 0:TAPS * H]
    cw_pair = mid[0][:, TAPS * H:(TAPS + 4) * H]
    pw32 = mid[0][:, (TAPS + 4) * H:(TAPS + 5) * H]
    wr_sb = mid[1][0:RD, 0:E]
    keys_sb = mid[1][0:RD, E:E + NE]
    cwh_dup = buf("cwh_dup", [P, TAPS * H], F32R)
    cwl_pair = buf("cwl_pair", [P, 4 * H], F32R)
    pw_hi = buf("pw_hi", [P, H], F32R)
    pw_lo = buf("pw_lo", [P, H], F32R)
    prm = buf("prm", [P, DW + 5], F32)
    tap = [prm[:, k:k + 1] for k in range(DW)]
    dw_bias, gn_w, gn_b = prm[:, DW:DW + 1], (prm[:, 6:7], prm[:, 8:9]), (prm[:, 7:8], prm[:, 9:10])
    sq = buf("sq", [P, NPIECE], F32)
    sqt = buf("sqt", [P, 8], F32)
    tmp_i = buf("tmp_i", [P, 8], I32)
    exp_i = buf("exp_i", [P, 8], I32)
    bn1 = buf("bn1", [P, NBLK, 6], F32)
    bn2 = buf("bn2", [P, 2, 6], F32)
    moments = [buf(f"moments{i}", [P, 3], F32) for i in range(2)]
    neg_mean = [buf(f"neg_mean{i}", [P, 1], F32) for i in range(2)]
    var = [buf(f"var{i}", [P, 1], F32) for i in range(2)]
    rstd = [buf(f"rstd{i}", [P, 1], F32) for i in range(2)]
    gscale = [buf(f"gscale{i}", [P, 1], F32) for i in range(2)]
    gbias = [buf(f"gbias{i}", [P, 1], F32) for i in range(2)]
    g32 = buf("g32", [P, KC * NE], F32)
    ln_bn = buf("ln_bn", [P, GB, 2, 6], F32)
    ln_mv = buf("ln_mv", [P, GB, 2], F32)
    ln_rstd = buf("ln_rstd", [P, GB], F32)

    conv_all = psum("conv_ps", [P, NBLK * BLK])
    conv_ps = [conv_all[:, i * BLK:(i + 1) * BLK] for i in range(NBLK)]
    pw_all = psum("pw_ps", [P, TO])

    def pw_ps(b):
        if isinstance(b, int) and b >= B - 2:
            return conv_all[:, (b - (B - 2)) * TO:(b - (B - 3)) * TO]
        return pw_all[:, :]

    stat_ps = psum("stat_ps", [P, 16])
    g_ps = psum("g_ps", [P, KC * NE])

    consts_in = sem("a_consts_in")
    pads_made = sem("a_pads_made")
    pool_done = sem("a_pool_done")
    ready = sem("a_ready")
    g_made = sem("a_g_made")
    g_copied = sem("a_g_copied")
    x_in = sem("a_x_in")
    pair_made = sem("a_pair_made")
    high_made = sem("a_high_made")
    low_made = sem("a_low_made")
    conv_done = sem("a_conv_done")
    evacuated = sem("a_evacuated")
    stat1 = sem("a_stat1")
    stat1_ps = sem("a_stat1_ps")
    var1 = sem("a_var1")
    rstd1 = sem("a_rstd1")
    affine1 = sem("a_affine1")
    gelu1 = sem("a_gelu1")
    tap0_made = sem("a_tap0_made")
    weighed = sem("a_weighed")
    dw_high = sem("a_dw_high")
    dw_split = sem("a_dw_split")
    pw_done = sem("a_pw_done")
    stat2 = sem("a_stat2")
    stat2_ps = sem("a_stat2_ps")
    var2 = sem("a_var2")
    rstd2 = sem("a_rstd2")
    affine2 = sem("a_affine2")
    gelu2 = sem("a_gelu2")
    norm_in = [sem(f"a_norm_in{i}") for i in range(RING)]
    norm_used = sem("a_norm_used")
    w_in = [sem(f"a_w_in{i}") for i in range(2)]
    w_used = [sem(f"a_w_used{i}") for i in range(2)]
    sums_made = sem("a_sums_made")
    paired_hi = sem("a_paired_hi")
    paired_lo = sem("a_paired_lo")
    kept_hi = sem("a_kept_hi")
    kept_lo = sem("a_kept_lo")
    plain_hi = sem("a_plain_hi")
    plain_lo = sem("a_plain_lo")
    kept = sem("a_kept")
    squared = sem("a_squared")
    sums_split = sem("a_sums_split")
    sums_total = sem("a_sums_total")
    scaled = sem("a_scaled")
    chain_v = sem("a_chain_v")
    ln_in = sem("a_ln_in")
    ln_var = sem("a_ln_var")
    ln_root = sem("a_ln_root")
    passed = sem("a_passed")

    N_CONSTS = 4

    def by_dve(b):
        return isinstance(b, int) and b < 2

    def place_parity(n):
        return (n // 2) % 2

    def place(s, n):
        return n // 2 + s.i * (s.per // 2)

    def load_x(eng, b):
        eng.dma_start(xs[0:CIN, PAD:PAD + T], x[b]).then_inc(x_in, 16)
        eng.dma_start(xs[CIN:P, PAD - 1:PAD - 1 + T], x[b]).then_inc(x_in, 16)

    def low_of_x(eng, b, parity):
        eng.wait_ge(pair_made, b + 1)
        eng.tensor_tensor(out=split[parity][CIN:P, 1:XW], in0=xs[CIN:P, 0:XW - 1],
                          in1=pair[parity][CIN:P, 0:XW - 1].bitcast(F32),
                          op=ALU.subtract).then_inc(low_made, 1)
        eng.wait_ge(low_made, b + 1)

    def load_normed(eng, pieces):
        for n in pieces:
            after(eng, norm_used, n - RING + 1)
            eng.dma_start(ring[n % RING], w_all[n]).then_inc(norm_in[n % RING], 16)

    with nc.Block("phase_a") as block:

        @block.sync
        def _(sp):
            sp.dma_start(mid[0][:, 0:12 * H], token_w).then_inc(consts_in, 16)
            sp.dma_start(mid[1][0:RD, 0:E + NE], router).then_inc(consts_in, 16)
            sp.dma_start(cst[:, :], const).then_inc(consts_in, 16)
            sp.dma_start(prm[:, :], par).then_inc(consts_in, 16)

            def copy_high(b, parity):
                after(sp, high_made, b * 16)
                sp.sem_inc(passed, 1)
                sp.wait_ge(pair_made, b + 1)
                sp.dma_start(split[parity][0:CIN, :].bitcast(F32),
                             pair[parity][0:CIN, :].bitcast(F32)).then_inc(high_made, 16)

            for i in range(2):
                sp.sem_inc(w_used[i], 1)
            copy_high(0, 0)
            load_normed(sp, NORMED_IN[0][:1])
            for s in steps_of_phase_a(sp):
                if s is None:
                    continue
                b = s.b

                for kind, n, piece, tensor in s.items:
                    if kind != NORM:
                        sp.wait_ge(w_used[n % 2], s.round(n) + 1)
                        sp.dma_start(stage[n % 2][:, :], w_all[piece]).then_inc(w_in[n % 2], 16)
                if s.has(-1):
                    copy_high(b + 1, 1 - s.parity)
                if isinstance(b, int) and b == 17:
                    sp.wait_ge(w_used[0], 8 + 2 + 1)
                    sp.wait_ge(stored, GB * 16)
                    sp.dma_start(h_ln[:, :, :], h0[0:GB].rearrange("b p e -> p b e")).then_inc(ln_in, 16)
                if s.has(4):
                    sp.wait_ge(gelu2, b - 3)
                    sp.dma_start(h0[b - 4], tok[:, :]).then_inc(stored, 16)
                if isinstance(b, int) and b + 1 < len(NORMED_IN):
                    load_normed(sp, NORMED_IN[b + 1][:1])

        @block.gpsimd
        def _(pool):
            pool.memset(xs[:, 0:PAD], 0.0)
            pool.memset(xs[:, T + PAD - 1:XW], 0.0).then_inc(pads_made, 1)
            pool.wait_ge(pads_made, 1)
            pool.memset(half_neg[:, :], -0.5).then_inc(pool_done, 1)
            pool.wait_ge(pool_done, 1)
            for i in range(2):
                pool.memset(split[i][CIN:P, 0:1].bitcast(F32), 0.0).then_inc(pool_done, 1)
                pool.wait_ge(pool_done, 2 + i)

            for s in steps_of_phase_a(pool):
                if s is None:
                    pool.wait_ge(scaled, 1)
                    continue
                b = s.b

                def sums(half):
                    for kind, n, piece, tensor in s.items:
                        if kind != PAIRED:
                            continue
                        src = stage[n % 2][:, :].rearrange("p (a h c two) -> p a h c two", a=2, h=HEADS, two=2)
                        dst = plus_minus[:, :].rearrange("p (a h s c) -> p a h s c", a=2, h=HEADS, s=2)
                        if half == 0:
                            pool.wait_ge(w_in[n % 2], (s.round(n) + 1) * 16)
                            pool.wait_ge(paired_lo, place(s, n) + 1)
                        for a in range(2):
                            last = pool.tensor_tensor(out=dst[:, a, :, half, :], in0=src[:, a, :, :, 0],
                                                      in1=src[:, a, :, :, 1], op=(ALU.add, ALU.subtract)[half])
                        last.then_inc(sums_made, 1)
                        pool.wait_ge(sums_made, 2 * place(s, n) + 1 + half)
                        if half == 1:
                            pool.sem_inc(w_used[n % 2], 1)

                if s.has(4):
                    pool.wait_ge(var2, b - 3)
                    pool.tensor_tensor(out=rstd[1][:, :], in0=var[1][:, :], in1=half_neg[:, 0:1],
                                       op=ALU.pow).then_inc(rstd2, 1)
                    pool.wait_ge(rstd2, b - 3)
                sums(0)
                if s.has(1):
                    pool.wait_ge(var1, b)
                    pool.tensor_tensor(out=rstd[0][:, :], in0=var[0][:, :], in1=half_neg[:, 0:1],
                                       op=ALU.pow).then_inc(rstd1, 1)
                    pool.wait_ge(rstd1, b)
                sums(1)
                if s.has(-1) and not by_dve(b):
                    low_of_x(pool, b + 1, 1 - s.parity)
                if s.has(2):
                    pool.wait_ge(dw_high, b - 1)
                    pool.tensor_tensor(out=dw_lo[:, :], in0=dwo[:, :], in1=dw_hi[:, :].bitcast(F32),
                                       op=ALU.subtract).then_inc(dw_split, 1)
                    pool.wait_ge(dw_split, b - 1)
            pool.wait_ge(ln_var, 1)
            pool.tensor_tensor(out=ln_rstd[:, :], in0=ln_mv[:, :, 1], in1=half_neg[:, 0:GB],
                               op=ALU.pow).then_inc(ln_root, 1)

        @block.scalar
        def _(act):
            def make_pair(b, parity):
                act.wait_ge(x_in, (b + 1) * 32)
                after(act, conv_done, (b - 1) * NBLK)
                act.activation(pair[parity][:, :], xs[:, :], ACT.Copy).then_inc(pair_made, 1)

            act.sem_inc(kept, 32)
            act.wait_ge(pads_made, 1)
            load_x(act, 0)
            make_pair(0, 0)
            act.wait_ge(low_made, 1)
            load_x(act, 1)
            load_normed(act, NORMED_IN[0][1:])
            act.wait_ge(g_copied, 1)
            act.activation(squares[:, 0:KC * NE], g32[:, :], ACT.Square,
                           accum_out=sqt[:, 6:7]).then_inc(squared, 1)
            for s in steps_of_phase_a(act):
                if s is None:
                    act.wait_ge(scaled, 1)
                    continue
                b = s.b

                def copy_out(blk):
                    act.wait_ge(conv_done, b * NBLK + (blk + 1))
                    if blk == 0:
                        after(act, weighed, b - 1)
                    c = 2 + blk * BLK
                    act.activation(mid[s.parity][:, c:c + BLK], conv_ps[blk],
                                   ACT.Copy).then_inc(evacuated, 1)

                def item(kind, n, piece, tensor):
                    if kind == NORM:
                        act.wait_ge(norm_in[n % RING], (n // RING + 1) * 16)
                        if n == 0:
                            act.wait_ge(squared, 1)
                        else:
                            act.wait_ge(norm_used, n)
                        act.activation(squares, ring[n % RING], ACT.Square,
                                       accum_out=sq[:, n:n + 1]).then_inc(norm_used, 1)
                        return
                    w = stage[n % 2][:, :]
                    scale = scl[:, bass.ds(tensor, 1)]
                    if kind == PAIRED:
                        act.wait_ge(sums_made, 2 * place(s, n) + 2)
                        act.sem_inc(passed, 1)
                        act.activation(wqk_hi[:, bass.ds(piece * PIECE, PIECE)], plus_minus[:, :],
                                       ACT.Copy, scale=scale).then_inc(paired_hi, 1)
                    if kind == PLAIN:
                        act.wait_ge(w_in[n % 2], (s.round(n) + 1) * 16)
                        act.activation(wv_hi[:, (piece - 8) * PIECE:(piece - 7) * PIECE], w,
                                       ACT.Copy, scale=scale).then_inc(plain_hi, 1)
                    if kind == KEPT:
                        act.wait_ge(w_in[n % 2], (s.round(n) + 1) * 16)
                        act.wait_ge(kept, place(s, n) * 16 + 16)
                        act.sem_inc(passed, 1)
                        act.activation(kept_out[place_parity(n)][:, 0, :], w, ACT.Copy,
                                       scale=scale).then_inc(kept_hi, 1)

                if s.has(2):
                    act.wait_ge(gelu1, b - 1)
                    after(act, dw_split, b - 2)
                    act.activation(dwo[:, :], mid[s.parity][:, 0:2 * TO:2], ACT.Identity, bias=dw_bias,
                                   scale=tap[0]).then_inc(tap0_made, 1)
                if s.has(-1):
                    make_pair(b + 1, 1 - s.parity)
                paired = s.items and s.items[0][0] == PAIRED
                first, rest = (s.items[1:], s.items[:1]) if paired else (s.items[:1], s.items[1:])
                if s.has(2) and rest and not paired:
                    item(*first[0])
                    first, rest = rest[:1], rest[1:]
                if s.has(4):
                    act.wait_ge(affine2, b - 3)
                    after(act, stored, (b - 4) * 16)
                    act.activation(tok[:, :], pw_ps(b - 4), ACT.Gelu, bias=gbias[1][:, :],
                                   scale=gscale[1][:, :]).then_inc(gelu2, 1)
                for it in first:
                    item(*it)
                if s.has(2):
                    act.wait_ge(weighed, b - 1)
                    if not isinstance(b, int) or b > 2:
                        act.sem_inc(passed, 1)
                        act.wait_ge(pw_done, b - 2)
                    act.activation(dw_hi[:, :], dwo[:, :], ACT.Copy).then_inc(dw_high, 1)
                if s.has(0):
                    copy_out(0)
                    copy_out(1)
                if paired:
                    item(*rest[0])
                if s.has(1):
                    act.wait_ge(affine1, b)
                    m = mid[1 - s.parity][:, 2:2 + T]
                    act.activation(m, m, ACT.Gelu, bias=gbias[0][:, :],
                                   scale=gscale[0][:, :]).then_inc(gelu1, 1)
                if s.has(-2):
                    act.wait_ge(low_made, b + 2)
                    load_x(act, b + 2)
                if isinstance(b, int) and b + 1 < len(NORMED_IN):
                    load_normed(act, NORMED_IN[b + 1][1:])
                if s.has(0):
                    copy_out(2)
                    copy_out(3)
                for kind, n, piece, tensor in s.items:
                    if kind == KEPT:
                        act.wait_ge(kept_lo, place(s, n) + 1)
                        act.dma_start(split_dram[piece - 12].rearrange("t p c -> p t c"),
                                     kept_out[place_parity(n)]).then_inc(kept, 16)
                if not paired:
                    for it in rest:
                        item(*it)

        @block.tensor
        def _(pe):
            pe.wait_ge(consts_in, 16 * N_CONSTS)
            for k in range(KC):
                last = pe.matmul(g_ps[:, k * NE:(k + 1) * NE], wr_sb[:, k * P:(k + 1) * P], keys_sb,
                                 start=True, stop=True)
            last.then_inc(g_made, 1)
            pe.wait_ge(ready, 1)
            pe.wait_ge(pool_done, 3)
            for s in steps_of_phase_a(pe):
                if s is None:
                    pe.wait_ge(sums_split, 1)
                    pe.matmul(stat_ps[:, 8:15], ones, sqt[:, 0:7], start=True, stop=True).then_inc(sums_total, 1)
                    pe.wait_ge(sums_split, 2)
                    continue
                b = s.b

                def convolve(blk):
                    after(pe, evacuated, (b - 1) * NBLK + (blk + 1))
                    t0 = blk * BLK
                    hi_lo, hi_hi = split[s.parity], pair[s.parity]
                    for k in range(TAPS):
                        pe.matmul(conv_ps[blk], cwh_dup[:, k * H:(k + 1) * H],
                                  hi_lo[:, t0 + k:t0 + k + BLK], start=(k == 0), stop=False)
                    for m in range(4):
                        last = pe.matmul(conv_ps[blk], cwl_pair[:, m * H:(m + 1) * H],
                                         hi_hi[:, t0 + 2 * m:t0 + 2 * m + BLK], start=False, stop=(m == 3))
                    last.then_inc(conv_done, 1)

                if s.has(0):
                    pe.wait_ge(high_made, (b + 1) * 16)
                    pe.wait_ge(low_made, b + 1)
                    convolve(0)
                if s.has(1):
                    pe.wait_ge(stat1, b)
                    pe.matmul(stat_ps[:, 0:3], ones, moments[0][:, :], start=True,
                              stop=True).then_inc(stat1_ps, 1)
                if s.has(0):
                    convolve(1)
                    convolve(2)
                if s.has(3):
                    pe.wait_ge(dw_split, b - 2)
                    if isinstance(b, int) and b - 3 >= B - 2:
                        pe.wait_ge(evacuated, B * NBLK)
                    else:
                        after(pe, gelu2, b - 3)
                    bank = pw_ps(b - 3)
                    for half in range(2):
                        c = slice(half * BLK, (half + 1) * BLK)
                        pe.matmul(bank[:, c], pw_hi[:, :], dw_hi[:, c], start=True, stop=False)
                        pe.matmul(bank[:, c], pw_lo[:, :], dw_hi[:, c], start=False, stop=False)
                        last = pe.matmul(bank[:, c], pw_hi[:, :], dw_lo[:, c], start=False, stop=True)
                    last.then_inc(pw_done, 1)
                if s.has(0):
                    convolve(3)
                if s.has(3):
                    pe.wait_ge(stat2, b - 2)
                    pe.matmul(g_ps[:, 0:3], ones, moments[1][:, :], start=True,
                              stop=True).then_inc(stat2_ps, 1)

        @block.vector
        def _(dve):
            chain = Chain(dve, chain_v)
            chain.begin()

            def rounded(hi, lo, src):
                chain.link(dve.tensor_copy(hi, src))
                return dve.tensor_tensor(out=lo, in0=src, in1=hi.bitcast(F32), op=ALU.subtract)

            for m in mid:
                dve.memset(m[:, GW - 2:GW], 0.0)
            dve.wait_ge(consts_in, 16 * N_CONSTS)
            dve.tensor_copy(mask_bf[:, :], mask32)
            dve.tensor_copy(ident_bf[:, :], ident)
            dve.tensor_copy(cwh_dup[:, :], cw_dup)
            dve.tensor_copy(dw_hi[:, 0:4 * H], cw_pair)
            rounded(pw_hi[:, :], pw_lo[:, :], pw32)
            dve.tensor_tensor(out=cwl_pair[:, :], in0=cw_pair, in1=dw_hi[:, 0:4 * H].bitcast(F32),
                              op=ALU.subtract).then_inc(ready, 1)
            low_of_x(dve, 0, 0)
            dve.wait_ge(g_made, 1)
            dve.tensor_copy(g32[:, :], g_ps[:, :]).then_inc(g_copied, 1)
            dve.wait_ge(g_copied, 1)
            for m in mid:
                dve.memset(m[:, 0:2], 0.0)

            def average(which, bn):
                m = moments[which]
                chain.link(dve.bn_aggr(m[:, 0:2], bn.rearrange("p a s -> p (a s)")))
                return dve.scalar_tensor_tensor(out=m[:, 2:3], in0=m[:, 0:1], scalar=m[:, 0:1],
                                                in1=m[:, 1:2], op0=ALU.mult, op1=ALU.add)

            def variance(which):
                ps = (stat_ps, g_ps)[which]
                mean, msq = ps[:, 0:1], ps[:, 2:3]
                chain.link(dve.tensor_scalar(out=neg_mean[which][:, :], in0=mean, scalar1=-1.0, scalar2=None,
                                             op0=ALU.mult))
                chain.link(dve.tensor_tensor(out=var[which][:, :], in0=mean, in1=neg_mean[which][:, :],
                                             op=ALU.mult))
                return dve.tensor_scalar(out=var[which][:, :], in0=var[which][:, :], scalar1=msq, scalar2=EPS,
                                         op0=ALU.add, op1=ALU.add)

            def affine(which):
                chain.link(dve.tensor_tensor(out=gscale[which][:, :], in0=rstd[which][:, :], in1=gn_w[which],
                                             op=ALU.mult))
                return dve.scalar_tensor_tensor(out=gbias[which][:, :], in0=neg_mean[which][:, :],
                                                scalar=gscale[which][:, :], in1=gn_b[which],
                                                op0=ALU.mult, op1=ALU.add)

            for s in steps_of_phase_a(dve):
                if s is None:
                    dve.wait_ge(norm_used, NPIECE)
                    dve.wait_ge(squared, 1)
                    dve.tensor_reduce(out=sqt[:, 0:4], in_=sq[:, 0:16].rearrange("p (t n) -> p t n", n=4),
                                      axis=AX_X, op=ALU.add)
                    dve.tensor_reduce(out=sqt[:, 4:6], in_=sq[:, 16:20].rearrange("p (t n) -> p t n", n=2),
                                      axis=AX_X, op=ALU.add).then_inc(sums_split, 1)
                    dve.wait_ge(sums_total, 1)
                    steps = iter(range(2, 40))

                    def link(ins):
                        ins.then_inc(sums_split, 1)
                        dve.wait_ge(sums_split, next(steps))

                    link(dve.tensor_scalar(out=sqt[:, 0:7], in0=stat_ps[:, 8:15], scalar1=float(P), scalar2=1e-18,
                                           op0=ALU.mult, op1=ALU.max))
                    link(dve.tensor_scalar(out=tmp_i[:, 0:7], in0=sqt[:, 0:7].bitcast(I32), scalar1=24,
                                           scalar2=None, op0=ALU.logical_shift_right))
                    link(dve.tensor_scalar(out=exp_i[:, 0:7], in0=tmp_i[:, 0:7], scalar1=-1.0, scalar2=199.0,
                                           op0=ALU.mult, op1=ALU.add))
                    link(dve.tensor_scalar(out=scl[:, 0:7].bitcast(I32), in0=exp_i[:, 0:7], scalar1=23,
                                           scalar2=None, op0=ALU.logical_shift_left))
                    link(dve.tensor_scalar(out=exp_i[:, 0:7], in0=tmp_i[:, 0:7], scalar1=1.0, scalar2=55.0,
                                           op0=ALU.mult, op1=ALU.add))
                    link(dve.tensor_scalar(out=inv[:, 0:7].bitcast(I32), in0=exp_i[:, 0:7], scalar1=23,
                                           scalar2=None, op0=ALU.logical_shift_left))
                    for c, (t, u, f) in enumerate(((Q_, K_, 0.5 / HD ** 0.5), (Q_, K_, -0.5 / HD ** 0.5),
                                                   (V_, O_, 1.0), (A_, B_, SCALING))):
                        dve.tensor_scalar(out=unscale[:, c:c + 1], in0=inv[:, t:t + 1], scalar1=inv[:, u:u + 1],
                                          scalar2=f, op0=ALU.mult, op1=ALU.mult)
                    link(dve.tensor_scalar(out=g_hi[:, :], in0=g32[:, :], scalar1=scl[:, 6:7], scalar2=None,
                                           op0=ALU.mult))
                    dve.scalar_tensor_tensor(out=g_lo[:, :], in0=g32[:, :], scalar=scl[:, 6:7], in1=g_hi[:, :],
                                             op0=ALU.mult, op1=ALU.subtract).then_inc(scaled, 1)
                    dve.sem_inc(paired_lo, 1)
                    continue
                b = s.b
                chain.begin()


                def taps(*ks):
                    for k in ks:
                        last = dve.scalar_tensor_tensor(out=dwo[:, :], in0=mid[s.parity][:, k:k + 2 * TO - 1:2],
                                                        scalar=tap[k], in1=dwo[:, :], op0=ALU.mult, op1=ALU.add)
                        chain.link(last)

                def stats(blk):
                    dve.wait_ge(evacuated, b * NBLK + (blk + 1))
                    c = 2 + blk * BLK
                    return dve.bn_stats(bn1[:, blk, :], mid[s.parity][:, c:c + BLK])

                def low_part(kind, n, piece, tensor):
                    if kind == NORM:
                        return
                    w = stage[n % 2][:, :]
                    if kind == PAIRED:
                        dve.wait_ge(paired_hi, place(s, n) + 1)
                        src, hi = plus_minus[:, :], wqk_hi[:, bass.ds(piece * PIECE, PIECE)]
                        lo, made = wqk_lo[:, bass.ds(piece * PIECE, PIECE)], paired_lo
                    if kind == KEPT:
                        dve.wait_ge(kept_hi, place(s, n) + 1)
                        src, hi, lo, made = w, kept_out[place_parity(n)][:, 0, :], kept_out[place_parity(n)][:, 1, :], kept_lo
                    if kind == PLAIN:
                        dve.wait_ge(plain_hi, piece - 7)
                        dve.wait_ge(kept, 32 + 16 * 8)
                        c = slice((piece - 8) * PIECE, (piece - 7) * PIECE)
                        src, hi, lo, made = w, wv_hi[:, c], wv_lo[:, c], plain_lo
                    dve.scalar_tensor_tensor(out=lo, in0=src, scalar=scl[:, bass.ds(tensor, 1)], in1=hi,
                                             op0=ALU.mult, op1=ALU.subtract).then_inc(made, 1)
                    if kind == KEPT:
                        dve.wait_ge(kept_lo, place(s, n) + 1)
                    if kind == PLAIN:
                        dve.wait_ge(plain_lo, piece - 7)
                    if kind != PAIRED:
                        dve.sem_inc(w_used[n % 2], 1)

                if by_dve(b):
                    low_of_x(dve, b + 1, 1 - s.parity)
                if s.has(4):
                    dve.wait_ge(stat2_ps, b - 3)
                    variance(1).then_inc(var2, 1)
                if s.has(2):
                    dve.wait_ge(tap0_made, b - 1)
                    taps(1, 2)
                if s.has(1):
                    dve.wait_ge(stat1_ps, b)
                    variance(0).then_inc(var1, 1)
                if s.has(4):
                    if isinstance(b, int) and b - 4 >= B - 2:
                        dve.wait_ge(gelu2, b - 4)
                    dve.wait_ge(rstd2, b - 3)
                    affine(1).then_inc(affine2, 1)
                if s.has(2):
                    taps(3)
                if s.has(1):
                    dve.wait_ge(rstd1, b)
                    affine(0).then_inc(affine1, 1)
                if s.has(2):
                    taps(4)
                    dve.sem_inc(weighed, 1)
                for it in s.items:
                    if it[0] == KEPT:
                        low_part(*it)
                if s.has(3):
                    dve.wait_ge(pw_done, b - 2)
                    bank = pw_ps(b - 3)
                    dve.bn_stats(bn2[:, 0, :], bank[:, 0:BLK])
                    chain.link(dve.bn_stats(bn2[:, 1, :], bank[:, BLK:TO]))
                    average(1, bn2[:, :, :]).then_inc(stat2, 1)
                if s.has(0):
                    for blk in range(2):
                        stats(blk)
                for it in s.items:
                    if it[0] != KEPT:
                        low_part(*it)
                if s.has(0):
                    for blk in range(2, NBLK):
                        last = stats(blk)
                    chain.link(last)
                    average(0, bn1[:, :, :]).then_inc(stat1, 1)
                if isinstance(b, int) and b == 18:
                    dve.wait_ge(ln_in, 16)
                    token_moments(dve, chain, h_ln, ln_bn, ln_mv).then_inc(ln_var, 1)
            dve.wait_ge(ln_root, 1)
            for b in range(GB):
                token_norm(dve, xn[:, b, :], h_ln[:, b, :], ln_mv[:, b, :], ln_rstd[:, b:b + 1])


def phase_b(nc, st, sb, h0, h1, split_dram, wqk_hi, wqk_lo, wv_hi, wv_lo, ident, rot,
            mask_bf, ident_bf, u_exp, u_neg, u_vo, half_neg, h_ln, xn, h_all, ab, h_res, h0_stored, stored):
    def buf(name, shape, dt):
        return sb(name, shape, dt, st)

    def psum(name, shape):
        return st.enter_context(nc.psum_tensor(name, shape, F32))

    def sem(name):
        return st.enter_context(nc.semaphore(name))

    NH = GB * 2
    wo_hi = buf("wo_hi", [P, 4 * PIECE], F16)
    wo_lo = buf("wo_lo", [P, 4 * PIECE], F16)
    xt_hi = buf("xt_hi", [P, KC, GT], F16)
    xt_lo = buf("xt_lo", [P, KC, GT], F16)
    v_hi = buf("v_hi", [P, GB, E], F16)
    v_lo = buf("v_lo", [P, GB, E], F16)
    qk32 = buf("qk32", [P, 2 * GT], F32)
    qk_hi = [buf(f"qk_hi{i}", [P, 2 * GT], F16) for i in range(2)]
    qk_lo = [buf(f"qk_lo{i}", [P, 2 * GT], F16) for i in range(2)]
    prob = buf("prob", [P, NH, P], F32)
    pn = buf("pn", [P, NH, P], F32)
    pt_hi = [buf(f"pt_hi{i}", [P, NH, P], F16) for i in range(2)]
    pt_lo = [buf(f"pt_lo{i}", [P, NH, P], F16) for i in range(2)]
    o_hi = buf("o_hi", [P, PAIRS, GT], F16)
    o_lo = buf("o_lo", [P, PAIRS, GT], F16)
    mx = buf("mx", [P, NH], F32)
    nb = buf("nb", [P, NH], F32)
    rsum = buf("rsum", [P, NH], F32)
    rinv = buf("rinv", [P, NH], F32)
    bn = buf("bnb", [P, GB, 2, 6], F32)
    mvb = buf("mvb", [P, GB, 2], F32)
    rstd = buf("rstdb", [P, GB], F32)

    qk_ps = [psum(f"qk_ps{i}", [P, 2 * GT]) for i in range(2)]
    out_ps = [psum(f"out_ps{i}", [P, BLK]) for i in range(2)]
    s_ps = psum("s_ps", [P, 2, BLK])
    t_ps = psum("t_ps", [P, BLK])
    o_ps = psum("o_ps", [P, BLK])

    wo_in = sem("b_wo_in")
    ln_in = sem("b_ln_in")
    ab_in = sem("b_ab_in")
    all_in = sem("b_all_in")
    res_in = sem("b_res_in")
    var_made = sem("b_var_made")
    rstd_made = sem("b_rstd_made")
    normed = sem("b_normed")
    xt_ps = sem("b_xt_ps")
    xt_high = sem("b_xt_high")
    xt_low = sem("b_xt_low")
    v_ps = sem("b_v_ps")
    v_high = sem("b_v_high")
    v_low = sem("b_v_low")
    wo_ps = sem("b_wo_ps")
    added = sem("b_added")
    qk_made = sem("b_qk_made")
    rotated = sem("b_rotated")
    qk_high = sem("b_qk_high")
    qk_low = sem("b_qk_low")
    scores = sem("b_scores")
    bias_made = sem("b_bias_made")
    exp_made = sem("b_exp_made")
    inverted = sem("b_inverted")
    divided = sem("b_divided")
    pt_ps = sem("b_pt_ps")
    pt_high = sem("b_pt_high")
    pt_low = sem("b_pt_low")
    o_made = sem("b_o_made")
    o_high = sem("b_o_high")
    o_low = sem("b_o_low")
    chain_v = sem("b_chain_v")

    def groups(eng):
        yield 0, True
        with eng.Fori(1, NG - 1) as g:
            yield g, True
        yield NG - 1, False

    WIDE = GB * 2

    with nc.Block("phase_b") as block:

        @block.sync
        def _(sp):
            def load(dst, g, signal):
                sp.dma_start(dst[:, :, :], h0[bass.ds(g * GB, GB)].rearrange("b p e -> p b e")).then_inc(signal, 16)

            for g, more in groups(sp):
                after(sp, stored, g * 16 * GB)
                load(h_res, g, res_in)
                if more:
                    sp.wait_ge(normed, (g + 1) * GB)
                    load(h_ln, g + 1, ln_in)
                if isinstance(g, int) and g == 0:
                    for n in range(4):
                        for part, dst in enumerate((wo_hi, wo_lo)):
                            sp.dma_start(dst[:, n * PIECE:(n + 1) * PIECE], split_dram[n, part]).then_inc(wo_in, 16)
                    sp.wait_ge(h0_stored, 16 * B)
                if not more:
                    sp.wait_ge(normed, NG * GB)
                    sp.dma_start(h_ln[:, 0, :], h1[0]).then_inc(ln_in, 16)
                    sp.wait_ge(v_ps, NG * WIDE)
                    for i, dst in enumerate(ab):
                        for n in range(2):
                            sp.dma_start(dst[:, n * PIECE:(n + 1) * PIECE],
                                         split_dram[4 + 2 * (i // 2) + n, i % 2]).then_inc(ab_in, 16)
                    sp.wait_ge(qk_made, NG * PAIRS)
                    for n in range(0, B - GB, GB):
                        sp.dma_start(h_all[:, n:n + GB, :],
                                     h1[n:n + GB].rearrange("b p e -> p b e")).then_inc(all_in, 16)
                for b in range(GB):
                    sp.wait_ge(added, g * WIDE + (b + 1) * 2)
                    sp.dma_start(h1[g * GB + b], h_res[:, b, :]).then_inc(stored, 16)
            sp.wait_ge(ab_in, 16 * 8)
            sp.wait_ge(all_in, 16 * (NG - 1))

        @block.gpsimd
        def _(pool):
            def root(g):
                pool.wait_ge(var_made, g)
                pool.tensor_tensor(out=rstd[:, :], in0=mvb[:, :, 1], in1=half_neg[:, 0:GB],
                                   op=ALU.pow).then_inc(rstd_made, 1)
                pool.wait_ge(rstd_made, g)

            for g, more in groups(pool):
                for j in range(PAIRS):
                    n = g * PAIRS + j
                    pool.wait_ge(inverted, n + 1)
                    after(pool, pt_ps, n)
                    pool.tensor_tensor(out=pn[:, :, :], in0=prob[:, :, :],
                                       in1=rinv[:, :].unsqueeze(2).to_broadcast([P, NH, P]),
                                       op=ALU.mult).then_inc(divided, 1)
                    pool.wait_ge(divided, n + 1)
                    if j == 2:
                        root(g + 1)

        @block.scalar
        def _(act):
            def high(dst, src):
                return act.activation(dst, src, ACT.Copy)

            def xt_part(g, f):
                act.wait_ge(xt_ps, g * WIDE + (f + 1))
                b, half = f // 2, f % 2
                high(xt_hi[:, half * 4:half * 4 + 4, b * P:(b + 1) * P],
                     qk_ps[f % 2][:, :].rearrange("p (k t) -> p k t", k=4)).then_inc(xt_high, 1)

            def v_parts(g):
                for f in range(WIDE):
                    act.wait_ge(v_ps, g * WIDE + (f + 1))
                    b, half = f // 2, f % 2
                    high(v_hi[:, b, half * BLK:(half + 1) * BLK], qk_ps[f % 2][:, :]).then_inc(v_high, 1)

            def qk_part(g, j):
                act.wait_ge(rotated, g * PAIRS + (j + 1))
                after(act, scores, g * PAIRS + (j - 1))
                high(qk_hi[j % 2][:, :], qk32[:, :]).then_inc(qk_high, 1)

            def exps(g, j):
                act.wait_ge(bias_made, g * PAIRS + (j + 1))
                after(act, divided, g * PAIRS + j)
                for hh in range(2):
                    for b in range(GB):
                        c = hh * GB + b
                        act.activation(prob[:, c, :], s_ps[:, hh, b * P:(b + 1) * P], ACT.Exp,
                                       bias=nb[:, c:c + 1], scale=u_exp,
                                       accum_out=rsum[:, c:c + 1]).then_inc(exp_made, 1)

            def pt_part(g, j):
                act.wait_ge(pt_ps, g * PAIRS + (j + 1))
                after(act, o_made, g * PAIRS + (j - 1))
                high(pt_hi[j % 2][:, :, :].rearrange("p a t -> p (a t)"), t_ps[:, :]).then_inc(pt_high, 1)

            def o_part(g, j):
                act.wait_ge(o_made, g * PAIRS + (j + 1))
                high(o_hi[:, j, :], o_ps[:, 0:GT]).then_inc(o_high, 1)

            for f in range(WIDE):
                xt_part(0, f)
            v_parts(0)
            for g, more in groups(act):
                qk_part(g, 0)
                for j in range(PAIRS):
                    if j + 1 < PAIRS:
                        qk_part(g, j + 1)
                    elif more:
                        xt_part(g + 1, 0)
                    exps(g, j)
                    if j >= 1:
                        pt_part(g, j - 1)
                    if j >= 2:
                        o_part(g, j - 2)
                pt_part(g, PAIRS - 1)
                o_part(g, PAIRS - 2)
                if more:
                    xt_part(g + 1, 1)
                o_part(g, PAIRS - 1)
                if more:
                    xt_part(g + 1, 2)
                    xt_part(g + 1, 3)
                    v_parts(g + 1)

        @block.tensor
        def _(pe):
            def steps_of(out, pairs, start, stop):
                steps = []
                for l, r in pairs:
                    steps += [(l[0], r[0]), (l[0], r[1]), (l[1], r[0])]
                n = len(steps)
                return [(out, l, r, start and i == 0, stop and i == n - 1) for i, (l, r) in enumerate(steps)]

            def products(out, pairs, start=True, stop=True):
                for o, l, r, first, end in steps_of(out, pairs, start, stop):
                    last = pe.matmul(o, l, r, start=first, stop=end)
                return last

            def both_heads(sums):
                for pair in zip(*(steps_of(*s) for s in sums)):
                    for o, l, r, first, end in pair:
                        last = pe.matmul(o, l, r, start=first, stop=end)
                return last

            def parts(hi, lo, *index):
                return hi[index], lo[index]

            ALL = slice(None)

            def transpose_xn(g, f):
                b, half = f // 2, f % 2
                pe.wait_ge(normed, g * GB + (b + 1))
                if f < 2:
                    after(pe, rotated, g * PAIRS - (1 - f))
                else:
                    pe.wait_ge(xt_low, g * WIDE + (f - 1))
                for k in range(4):
                    c = half * 4 + k
                    last = pe.transpose(qk_ps[f % 2][:, k * P:(k + 1) * P], xn[:, b, c * P:(c + 1) * P], ident)
                last.then_inc(xt_ps, 1)

            def project_v(g):
                pe.wait_ge(xt_low, (g + 1) * WIDE)
                for f in range(WIDE):
                    b, half = f // 2, f % 2
                    if f >= 2:
                        pe.wait_ge(v_low, g * WIDE + (f - 1))
                    products(qk_ps[f % 2][:, :], [
                        (parts(xt_hi, xt_lo, ALL, k, slice(b * P, (b + 1) * P)),
                         parts(wv_hi, wv_lo, ALL, slice(k * E + half * BLK, k * E + (half + 1) * BLK)))
                        for k in range(KC)]).then_inc(v_ps, 1)

            def project_qk(g, j):
                if j < 2:
                    pe.wait_ge(v_low, (g + 1) * WIDE - (1 - j))
                else:
                    pe.wait_ge(rotated, g * PAIRS + (j - 1))
                for which in range(2):
                    last = products(qk_ps[j % 2][:, which * GT:(which + 1) * GT], [
                        (parts(wqk_hi, wqk_lo, ALL, slice((which * KC + k) * E + j * P, (which * KC + k) * E + (j + 1) * P)),
                         parts(xt_hi, xt_lo, ALL, k, ALL))
                        for k in range(KC)])
                last.then_inc(qk_made, 1)

            def score(g, j):
                pe.wait_ge(qk_low, g * PAIRS + (j + 1))
                after(pe, exp_made, (g * PAIRS + j) * NH)
                for hh in range(2):
                    pe.matmul(s_ps[:, hh, 0:GT], ident_bf[:, :],
                              mask_bf[:, :].unsqueeze(1).to_broadcast([P, GB, P]), start=True, stop=False)
                for b in range(GB):
                    sums = []
                    for hh in range(2):
                        rows = slice(hh * HD, (hh + 1) * HD)
                        q = parts(qk_hi[j % 2], qk_lo[j % 2], rows, slice(b * P, (b + 1) * P))
                        k = parts(qk_hi[j % 2], qk_lo[j % 2], rows, slice(GT + b * P, GT + (b + 1) * P))
                        sums.append((s_ps[:, hh, b * P:(b + 1) * P], [(q, k)], False, b == GB - 1))
                    last = both_heads(sums)
                last.then_inc(scores, 1)

            def transpose_p(g, j):
                pe.wait_ge(divided, g * PAIRS + (j + 1))
                after(pe, pt_low, g * PAIRS + j)
                for c in range(NH):
                    last = pe.transpose(t_ps[:, c * P:(c + 1) * P], pn[:, c, :], ident)
                last.then_inc(pt_ps, 1)

            def weigh_v(g, j):
                pe.wait_ge(pt_low, g * PAIRS + (j + 1))
                if j == 0:
                    pe.wait_ge(v_low, (g + 1) * WIDE)
                after(pe, o_low, g * PAIRS + j)
                for b in range(GB):
                    sums = []
                    for hh in range(2):
                        head = (2 * j + hh) * HD
                        v = parts(v_hi, v_lo, ALL, b, slice(head, head + HD))
                        p = parts(pt_hi[j % 2], pt_lo[j % 2], ALL, hh * GB + b, ALL)
                        sums.append((o_ps[hh * HD:(hh + 1) * HD, b * P:(b + 1) * P], [(v, p)], True, True))
                    last = both_heads(sums)
                last.then_inc(o_made, 1)

            def project_out(g, f, first, last):
                b, half = f // 2, f % 2
                if first == 0:
                    after(pe, added, g * WIDE + (f - 1))
                pe.wait_ge(o_low, g * PAIRS + last)
                done = products(out_ps[f % 2][:, :], [
                    (parts(o_hi, o_lo, ALL, j, slice(b * P, (b + 1) * P)),
                     parts(wo_hi, wo_lo, ALL, slice(j * E + half * BLK, j * E + (half + 1) * BLK)))
                    for j in range(first, last)], start=first == 0, stop=last == PAIRS)
                if last == PAIRS:
                    done.then_inc(wo_ps, 1)

            for f in range(WIDE):
                transpose_xn(0, f)
            project_v(0)
            pe.wait_ge(wo_in, 16 * 8)
            for g, more in groups(pe):
                project_qk(g, 0)
                for j in range(PAIRS):
                    if j + 1 < PAIRS:
                        project_qk(g, j + 1)
                    else:
                        if more:
                            transpose_xn(g + 1, 0)
                        project_out(g, 0, 0, 4)
                    score(g, j)
                    if j >= 1:
                        transpose_p(g, j - 1)
                    if j >= 2:
                        weigh_v(g, j - 2)
                project_out(g, 1, 0, 5)
                project_out(g, 0, 4, 5)
                transpose_p(g, PAIRS - 1)
                weigh_v(g, PAIRS - 2)
                project_out(g, 0, 5, 6)
                if more:
                    transpose_xn(g + 1, 1)
                weigh_v(g, PAIRS - 1)
                project_out(g, 0, 6, 7)
                project_out(g, 1, 5, 7)
                if more:
                    transpose_xn(g + 1, 2)
                project_out(g, 0, 7, 8)
                project_out(g, 1, 7, 8)
                if more:
                    transpose_xn(g + 1, 3)
                project_out(g, 2, 0, PAIRS)
                project_out(g, 3, 0, PAIRS)
                if more:
                    project_v(g + 1)

        @block.vector
        def _(dve):
            chain = Chain(dve, chain_v)

            def statistics(g, batches):
                dve.wait_ge(ln_in, g * 16)
                token_moments(dve, chain, h_ln[:, 0:batches, :], bn, mvb).then_inc(var_made, 1)

            def norm(g, batches):
                dve.wait_ge(rstd_made, g)
                after(dve, xt_ps, g * WIDE)
                for b in range(batches):
                    token_norm(dve, xn[:, b, :], h_ln[:, b, :], mvb[:, b, :],
                               rstd[:, b:b + 1]).then_inc(normed, 1)

            def low(dst, src, hi):
                return dve.tensor_tensor(out=dst, in0=src, in1=hi, op=ALU.subtract)

            def xt_part(g, f):
                dve.wait_ge(xt_high, g * WIDE + (f + 1))
                b, half = f // 2, f % 2
                at = (slice(None), slice(half * 4, half * 4 + 4), slice(b * P, (b + 1) * P))
                low(xt_lo[at], qk_ps[f % 2][:, :].rearrange("p (k t) -> p k t", k=4),
                    xt_hi[at]).then_inc(xt_low, 1)

            def v_parts(g):
                for f in range(WIDE):
                    dve.wait_ge(v_high, g * WIDE + (f + 1))
                    b, half = f // 2, f % 2
                    at = (slice(None), b, slice(half * BLK, (half + 1) * BLK))
                    low(v_lo[at], qk_ps[f % 2][:, :], v_hi[at]).then_inc(v_low, 1)

            def rotate(g, j):
                dve.wait_ge(qk_made, g * PAIRS + (j + 1))
                after(dve, qk_low, g * PAIRS + j)
                dve.tensor_tensor(out=qk32[:, :].rearrange("p (a t) -> p a t", t=P),
                                  in0=qk_ps[j % 2][:, :].rearrange("p (a t) -> p a t", t=P),
                                  in1=rot.unsqueeze(1).to_broadcast([P, 2 * GB, P]),
                                  op=ALU.mult).then_inc(rotated, 1)

            def qk_part(g, j):
                dve.wait_ge(qk_high, g * PAIRS + (j + 1))
                low(qk_lo[j % 2][:, :], qk32[:, :], qk_hi[j % 2][:, :]).then_inc(qk_low, 1)

            def maxima(g, j):
                dve.wait_ge(scores, g * PAIRS + (j + 1))
                chain.link(dve.tensor_reduce(out=mx[:, :].rearrange("p (h b) -> p h b", h=2),
                                             in_=s_ps[:, :, 0:GT].rearrange("p h (b t) -> p h b t", b=GB),
                                             axis=AX_X, op=ALU.max))
                dve.tensor_scalar(out=nb[:, :], in0=mx[:, :], scalar1=u_neg, scalar2=None,
                                  op0=ALU.mult).then_inc(bias_made, 1)

            def invert(g, j):
                dve.wait_ge(exp_made, (g * PAIRS + (j + 1)) * NH)
                after(dve, divided, g * PAIRS + j)
                dve.reciprocal(rinv[:, :], rsum[:, :]).then_inc(inverted, 1)

            def pt_part(g, j):
                dve.wait_ge(pt_high, g * PAIRS + (j + 1))
                low(pt_lo[j % 2][:, :, :].rearrange("p a t -> p (a t)"), t_ps[:, :],
                    pt_hi[j % 2][:, :, :].rearrange("p a t -> p (a t)")).then_inc(pt_low, 1)

            def o_part(g, j):
                dve.wait_ge(o_high, g * PAIRS + (j + 1))
                low(o_lo[:, j, :], o_ps[:, 0:GT], o_hi[:, j, :]).then_inc(o_low, 1)

            def residual(g, outputs):
                dve.wait_ge(res_in, (g + 1) * 16)
                for f in outputs:
                    dve.wait_ge(wo_ps, g * WIDE + (f + 1))
                    b, half = f // 2, f % 2
                    at = h_res[:, b, half * BLK:(half + 1) * BLK]
                    dve.scalar_tensor_tensor(out=at, in0=out_ps[f % 2][:, :], scalar=u_vo, in1=at,
                                             op0=ALU.mult, op1=ALU.add).then_inc(added, 1)

            chain.begin()
            dve.sem_inc(normed, GB)
            for f in range(WIDE):
                xt_part(0, f)
            v_parts(0)
            for g, more in groups(dve):
                chain.begin()
                rotate(g, 0)
                qk_part(g, 0)
                for j in range(PAIRS):
                    if j + 1 < PAIRS:
                        rotate(g, j + 1)
                    elif more:
                        xt_part(g + 1, 0)
                    maxima(g, j)
                    if j + 1 < PAIRS:
                        qk_part(g, j + 1)
                    if j == 1:
                        statistics(g + 1, GB if more else 1)
                    invert(g, j)
                    if j >= 1:
                        pt_part(g, j - 1)
                    if j >= 2:
                        o_part(g, j - 2)
                    if j == 4:
                        norm(g + 1, GB if more else 1)
                pt_part(g, PAIRS - 1)
                o_part(g, PAIRS - 2)
                if more:
                    xt_part(g + 1, 1)
                o_part(g, PAIRS - 1)
                if more:
                    xt_part(g + 1, 2)
                residual(g, (0, 1))
                if more:
                    xt_part(g + 1, 3)
                residual(g, (2, 3))
                if more:
                    v_parts(g + 1)


def phase_c(nc, st, sb, h1, out, ident, u_ab, half_neg, g_hi, g_lo, g_inv, xn_first, h, ab, h1_stored):
    def buf(name, shape, dt):
        return sb(name, shape, dt, st)

    def psum(name, shape):
        return st.enter_context(nc.psum_tensor(name, shape, F32))

    def sem(name):
        return st.enter_context(nc.semaphore(name))

    ZC = BOT // P
    a_hi, a_lo, b_hi, b_lo = ab
    xn = xn_first[:, 0, :]
    xt_hi = buf("xtc_hi", [P, KC, P], F16)
    xt_lo = buf("xtc_lo", [P, KC, P], F16)
    sc = buf("sc", [P, NE], F32)
    left8 = buf("left8", [P, NE], F32)
    left16 = buf("left16", [P, NE], F32)
    top = buf("top", [P, 2, 8], F32)
    neg_top = buf("neg_top", [P, 1], F32)
    ex = buf("ex", [P, NE], F32)
    gate = buf("gate", [P, NE], F32)
    gsum = buf("gsum", [P, 1], F32)
    ginv = buf("ginv", [P, 1], F32)
    zg = buf("zg", [P, BOT], F32)
    zt_hi = buf("zt_hi", [P, ZC, P], F16)
    zt_lo = buf("zt_lo", [P, ZC, P], F16)
    res = buf("res", [P, E], F32)
    bn = buf("bnc", [P, 2, 6], F32)
    mvc = buf("mvc", [P, 2], F32)
    rstd = buf("rstdc", [P, 1], F32)

    xt_bank = [psum(f"xt_bank{i}", [P, BLK]) for i in range(2)]
    out_bank = [psum(f"out_bank{i}", [P, BLK]) for i in range(2)]
    z_bank = psum("z_bank", [P, BOT])
    zt_bank = psum("zt_bank", [P, BOT])
    sc_bank = psum("sc_bank", [P, NE])

    h_in = sem("c_h_in")
    var_made = sem("c_var_made")
    rstd_made = sem("c_rstd_made")
    normed = sem("c_normed")
    xt_ps = sem("c_xt_ps")
    xt_high = sem("c_xt_high")
    xt_low = sem("c_xt_low")
    scored = sem("c_scored")
    z_made = sem("c_z_made")
    top_made = sem("c_top_made")
    exp_made = sem("c_exp_made")
    gated = sem("c_gated")
    zt_ps = sem("c_zt_ps")
    zt_high = sem("c_zt_high")
    zt_low = sem("c_zt_low")
    out_ps = sem("c_out_ps")
    added = sem("c_added")
    stored = sem("c_stored")
    chain_v = sem("c_chain_v")

    def steps(eng):
        def has(b):
            return lambda lag: not isinstance(b, int) or 0 <= b - lag < B

        for b in (0, 1):
            yield b, has(b)
        with eng.Fori(2, B - 2) as b:
            yield b, has(b)
        for b in (B - 2, B - 1, B):
            yield b, has(b)

    def products(pe, bank, pairs):
        for c, ((l_hi, l_lo), (r_hi, r_lo)) in enumerate(pairs):
            pe.matmul(bank, l_hi, r_hi, start=(c == 0), stop=False)
            pe.matmul(bank, l_hi, r_lo, start=False, stop=False)
            last = pe.matmul(bank, l_lo, r_hi, start=False, stop=(c == len(pairs) - 1))
        return last

    with nc.Block("phase_c") as block:

        @block.sync
        def _(sp):
            sp.wait_ge(h1_stored, 16 * B)
            sp.dma_start(h[:, B - GB:B, :], h1[B - GB:B].rearrange("b p e -> p b e")).then_inc(h_in, 16)
            for b, has in steps(sp):
                if has(1):
                    sp.wait_ge(added, b * 2)
                    sp.dma_start(out[b - 1], res[:, :]).then_inc(stored, 16)
            sp.wait_ge(stored, 16 * B)

        @block.gpsimd
        def _(pool):
            with pool.Fori(1, B) as b:
                pool.wait_ge(var_made, b)
                pool.tensor_tensor(out=rstd[:, :], in0=mvc[:, 1:2], in1=half_neg[:, 0:1],
                                   op=ALU.pow).then_inc(rstd_made, 1)

        @block.scalar
        def _(act):
            def xt_parts(b):
                for f in range(2):
                    act.wait_ge(xt_ps, b * 2 + (f + 1))
                    act.activation(xt_hi[:, f * 4:f * 4 + 4, :],
                                   xt_bank[f][:, :].rearrange("p (k t) -> p k t", k=4),
                                   ACT.Copy).then_inc(xt_high, 1)

            xt_parts(0)
            for b, has in steps(act):
                if has(0):
                    act.wait_ge(top_made, b + 1)
                    act.activation(ex[:, :], sc[:, :], ACT.Exp, bias=neg_top[:, :]).then_inc(exp_made, 1)
                if has(-1):
                    xt_parts(b + 1)
                if has(0):
                    act.wait_ge(zt_ps, b + 1)
                    act.activation(zt_hi[:, :, :].rearrange("p k t -> p (k t)"), zt_bank[:, :],
                                   ACT.Copy).then_inc(zt_high, 1)

        @block.tensor
        def _(pe):
            def transpose_xn(b):
                pe.wait_ge(normed, b + 1)
                for f in range(2):
                    after(pe, xt_low, (b - 1) * 2 + (f + 1))
                    for k in range(4):
                        c = f * 4 + k
                        last = pe.transpose(xt_bank[f][:, k * P:(k + 1) * P], xn[:, c * P:(c + 1) * P], ident)
                    last.then_inc(xt_ps, 1)

            transpose_xn(0)
            for b, has in steps(pe):
                x_parts = [(xt_hi[:, k, :], xt_lo[:, k, :]) for k in range(KC)]
                if has(0):
                    pe.wait_ge(xt_low, (b + 1) * 2)
                    after(pe, top_made, b)
                    products(pe, sc_bank[:, :], [
                        (x_parts[k], (g_hi[:, k * NE:(k + 1) * NE], g_lo[:, k * NE:(k + 1) * NE]))
                        for k in range(KC)]).then_inc(scored, 1)
                    after(pe, gated, b)
                    products(pe, z_bank[:, :], [
                        (x_parts[k], (a_hi[:, k * BOT:(k + 1) * BOT], a_lo[:, k * BOT:(k + 1) * BOT]))
                        for k in range(KC)]).then_inc(z_made, 1)
                if has(-1):
                    transpose_xn(b + 1)
                if has(1):
                    pe.wait_ge(zt_low, b)
                    for half in range(2):
                        after(pe, added, (b - 2) * 2 + (half + 1))
                        products(pe, out_bank[half][:, :], [
                            ((zt_hi[:, k, :], zt_lo[:, k, :]),
                             tuple(w[:, k * E + half * BLK:k * E + (half + 1) * BLK] for w in (b_hi, b_lo)))
                            for k in range(ZC)]).then_inc(out_ps, 1)
                if has(0):
                    pe.wait_ge(gated, b + 1)
                    for k in range(ZC):
                        last = pe.transpose(zt_bank[:, k * P:(k + 1) * P], zg[:, k * P:(k + 1) * P], ident)
                    last.then_inc(zt_ps, 1)

        @block.vector
        def _(dve):
            chain = Chain(dve, chain_v)

            def norm(b):
                at = [h[:, bass.ds(b, 1), half * BLK:(half + 1) * BLK].rearrange("p a e -> p (a e)")
                      for half in range(2)]
                dve.bn_stats(bn[:, 0, :], at[0])
                chain.link(dve.bn_stats(bn[:, 1, :], at[1]))
                chain.link(dve.bn_aggr(mvc[:, :], bn[:, :, :].rearrange("p a s -> p (a s)")))
                chain.link(dve.tensor_scalar(out=mvc[:, 1:2], in0=mvc[:, 1:2], scalar1=EPS, scalar2=None,
                                             op0=ALU.add))
                dve.sem_inc(var_made, 1)
                dve.wait_ge(rstd_made, b)
                after(dve, xt_ps, b * 2)
                dve.tensor_scalar(out=xn, in0=h[:, bass.ds(b, 1), :].rearrange("p a e -> p (a e)"),
                                  scalar1=mvc[:, 0:1], scalar2=rstd[:, :], op0=ALU.subtract,
                                  op1=ALU.mult).then_inc(normed, 1)

            def xt_parts(b):
                for f in range(2):
                    dve.wait_ge(xt_high, b * 2 + (f + 1))
                    dve.tensor_tensor(out=xt_lo[:, f * 4:f * 4 + 4, :],
                                      in0=xt_bank[f][:, :].rearrange("p (k t) -> p k t", k=4),
                                      in1=xt_hi[:, f * 4:f * 4 + 4, :], op=ALU.subtract).then_inc(xt_low, 1)

            chain.begin()
            dve.sem_inc(normed, 1)
            xt_parts(0)
            chain.begin()
            norm(1)
            dve.wait_ge(h_in, 16)
            for b, has in steps(dve):
                chain.begin()
                if has(0):
                    dve.wait_ge(scored, b + 1)
                    chain.link(dve.tensor_scalar(out=sc[:, :], in0=sc_bank[:, :], scalar1=g_inv, scalar2=None,
                                                 op0=ALU.mult))
                    chain.link(dve.max(out=top[:, 0, :], in_=sc[:, :]))
                    dve.tensor_scalar(out=neg_top[:, :], in0=top[:, 0, 0:1], scalar1=-1.0, scalar2=None,
                                      op0=ALU.mult).then_inc(top_made, 1)
                    chain.link(dve.match_replace(out=left8[:, :], in_to_replace=top[:, 0, :],
                                                 in_values=sc[:, :], imm_value=MASKED))
                    chain.link(dve.max(out=top[:, 1, :], in_=left8[:, :]))
                    chain.link(dve.match_replace(out=left16[:, :], in_to_replace=top[:, 1, :],
                                                 in_values=left8[:, :], imm_value=MASKED))
                    dve.wait_ge(exp_made, b + 1)
                    chain.link(dve.scalar_tensor_tensor(out=ex[:, :], in0=left16[:, :], scalar=MASKED / 2,
                                                        in1=ex[:, :], op0=ALU.is_le, op1=ALU.mult,
                                                        accum_out=gsum[:, :]))
                    chain.link(dve.reciprocal(ginv[:, :], gsum[:, :]))
                    chain.link(dve.tensor_scalar(out=gate[:, :], in0=ex[:, :], scalar1=ginv[:, :], scalar2=None,
                                                 op0=ALU.mult))
                    dve.wait_ge(z_made, b + 1)
                    after(dve, zt_ps, b)
                    dve.tensor_tensor(out=zg[:, :].rearrange("p (n r) -> p n r", r=RANK),
                                      in0=z_bank[:, :].rearrange("p (n r) -> p n r", r=RANK),
                                      in1=gate[:, :].unsqueeze(2).to_broadcast([P, NE, RANK]),
                                      op=ALU.mult).then_inc(gated, 1)
                if has(-1):
                    xt_parts(b + 1)
                if has(-2):
                    norm(b + 2)
                if has(1):
                    for half in range(2):
                        c = slice(half * BLK, (half + 1) * BLK)
                        dve.wait_ge(out_ps, (b - 1) * 2 + (half + 1))
                        after(dve, stored, (b - 1) * 16)
                        dve.scalar_tensor_tensor(
                            out=res[:, c], in0=out_bank[half][:, :], scalar=u_ab,
                            in1=h[:, bass.ds(b - 1, 1), c].rearrange("p a e -> p (a e)"),
                            op0=ALU.mult, op1=ALU.add).then_inc(added, 1)
                if has(0):
                    dve.wait_ge(zt_high, b + 1)
                    dve.tensor_tensor(out=zt_lo[:, :, :].rearrange("p k t -> p (k t)"), in0=zt_bank[:, :],
                                      in1=zt_hi[:, :, :].rearrange("p k t -> p (k t)"),
                                      op=ALU.subtract).then_inc(zt_low, 1)
def audio_tower_kernel(nc, x, token_w, par, w_all, router, const, out):
    h0 = nc.dram_tensor("h0", (B, P, E), F32, kind="Internal").ap()
    h1 = nc.dram_tensor("h1", (B, P, E), F32, kind="Internal").ap()
    split_dram = nc.dram_tensor("split_dram", (8, 2, P, PIECE), F16, kind="Internal").ap()
    with ExitStack() as whole:
        def sb(name, shape, dt, stack=whole):
            return stack.enter_context(nc.sbuf_tensor(name, shape, dt))

        cst = sb("cst", [P, 4 * P], F32)
        ident, rot, ones, mask32 = (cst[:, i * P:(i + 1) * P] for i in range(4))
        mask_bf = sb("mask_bf", [P, P], BF16)
        ident_bf = sb("ident_bf", [P, P], BF16)
        scl = sb("scl", [P, 8], F32)
        inv = sb("inv", [P, 8], F32)
        unscale = sb("unscale", [P, 4], F32)
        half_neg = sb("half_neg", [P, 8], F32)
        g_hi = sb("g_hi", [P, KC * NE], F16)
        g_lo = sb("g_lo", [P, KC * NE], F16)
        g_inv = inv[:, 6:7]
        u_exp, u_neg, u_vo, u_ab = (unscale[:, i:i + 1] for i in range(4))

        wqk = sb("wqk", [P, 16 * PIECE], F16)
        wqk_hi, wqk_lo = wqk[:, 0:8 * PIECE], wqk[:, 8 * PIECE:16 * PIECE]
        wv_hi = sb("wv_hi", [P, 4 * PIECE], F16)
        wv_lo = sb("wv_lo", [P, 4 * PIECE], F16)
        h_all = wqk[:, :].bitcast(F32).rearrange("p (b e) -> p b e", b=B)
        ab = [w[:, i * 2 * PIECE:(i + 1) * 2 * PIECE] for i in range(2) for w in (wv_hi, wv_lo)]
        h_ln = sb("h_ln", [P, GB, E], F32)
        xn = sb("xn", [P, GB, E], F32)
        tok = sb("tok", [P, TO], F32)
        h_res = sb("h_res", [P, GB, E], F32)
        h0_stored = whole.enter_context(nc.semaphore("h0_stored"))
        h1_stored = whole.enter_context(nc.semaphore("h1_stored"))
        with ExitStack() as s:
            phase_a(nc, s, sb, x, token_w, par, w_all, router, const, h0, split_dram,
                    wqk_hi, wqk_lo, wv_hi, wv_lo, cst, ident, ones, mask32, mask_bf, ident_bf,
                    scl, inv, unscale, half_neg, g_hi, g_lo, h_ln, xn, tok, h_res, h0_stored)
        with ExitStack() as s:
            phase_b(nc, s, sb, h0, h1, split_dram, wqk_hi, wqk_lo, wv_hi, wv_lo, ident, rot,
                    mask_bf, ident_bf, u_exp, u_neg, u_vo, half_neg, h_ln, xn, h_all, ab, h_res, h0_stored, h1_stored)
        with ExitStack() as s:
            phase_c(nc, s, sb, h1, out, ident, u_ab, half_neg, g_hi, g_lo, g_inv, xn, h_all, ab, h1_stored)


def constants():
    import numpy as np

    j = np.arange(P) % HD
    inv_freq = (1.0 / 10000.0 ** (np.arange(0, HD, 2, dtype=np.float32) / np.float32(HD))).astype(np.float32)
    t = np.arange(P, dtype=np.float32)
    ang = (inv_freq[j % (HD // 2)][:, None] * t[None, :]).astype(np.float32).astype(np.float64)
    rot = np.cos(ang) + np.where(j < HD // 2, 1.0, -1.0)[:, None] * np.sin(ang)
    mask = np.where(np.arange(P)[None, :] > np.arange(P)[:, None], MASKED, 0.0)
    return np.concatenate([np.eye(P), rot, np.full((P, P), 1.0 / P), mask], 1).astype(np.float32)


def laid_out(inputs):
    import numpy as np

    i = {k: np.asarray(v) for k, v in inputs.items()}
    pieces = [i["L0_attn_" + w].reshape(KC, P, E) for w in ("Wq", "Wk", "Wv", "Wo")]
    pieces = [w.reshape(4, 2, P, E).transpose(0, 2, 1, 3).reshape(4, P, PIECE) for w in pieces]
    a = i["L0_ffn_A_w"].T.reshape(2, 4, P, BOT).transpose(0, 2, 1, 3).reshape(2, P, PIECE)
    b = i["L0_ffn_B_w"].T.reshape(2, 2, P, E).transpose(0, 2, 1, 3).reshape(2, P, PIECE)
    conv = i["L0_tok_conv_in_w"].transpose(1, 2, 0)
    none = np.zeros_like(conv[:, 0:1])
    pairs = np.concatenate([conv, none], 1).reshape(CIN, 4, 2, H).transpose(2, 0, 1, 3).reshape(P, 4 * H)
    conv = conv.reshape(CIN, TAPS * H)
    cols = [i["L0_tok_" + k][:, None] for k in ("dw_b", "gn1_w", "gn1_b", "gn2_w", "gn2_b")]
    arrays = {
        "x": i["x"],
        "token_w": np.concatenate([np.concatenate([conv, conv], 0), pairs, i["L0_tok_pw_w"].reshape(H, H).T], 1),
        "par": np.concatenate([i["L0_tok_dw_w"].reshape(H, DW)] + cols, 1),
        "w_all": np.concatenate(pieces + [a, b], 0),
        "router": np.concatenate([i["L0_ffn_Wq_w"], i["L0_ffn_keys"].T], 1),
        "const": constants(),
    }
    return {k: np.ascontiguousarray(v) for k, v in arrays.items()}


def kernel(**inputs):
    import concourse.bacc as bacc
    from concourse.bass_utils import run_bass_kernel_spmd

    nc = bacc.Bacc("TRN2", target_bir_lowering=False, num_devices=1)
    arrays = laid_out(inputs)
    args = {n: nc.dram_tensor(n, a.shape, F32, kind="ExternalInput").ap() for n, a in arrays.items()}
    out = nc.dram_tensor("out", (B, P, E), F32, kind="ExternalOutput").ap()
    audio_tower_kernel(nc, out=out, **args)
    r = run_bass_kernel_spmd(nc, [arrays], core_ids=[0])
    return r.results[0]["out"]
```
